# Optimizing a Trainium2 kernel written in Bass

```python
import numpy as np
import jax
import jax.numpy as jnp

def _softmax(x, axis=-1):
    return jax.nn.softmax(x, axis=axis)

def _gelu(x):
    return jax.nn.gelu(x, approximate=True)

def _silu(x):
    return jax.nn.silu(x)

def _sigmoid(x):
    return jax.nn.sigmoid(x)

def _layernorm(x, axis=-1, eps=1e-05):
    m = jnp.mean(x, axis=axis, keepdims=True)
    v = jnp.var(x, axis=axis, keepdims=True)
    return (x - m) / jnp.sqrt(v + eps)

def _scatter_add(tgt, idx, src, axis=0):
    return tgt.at[idx].add(src)

def _segment_sum(src, seg, n):
    return jax.ops.segment_sum(src, seg, n)
kernel_name = 'mk_xattn_seq_d2_seqx_r4_7123b8'

def setup_inputs(seed: int=0):
    np.random.seed(seed)
    _w = jnp.asarray

    def _rec_inputs():
        import jax
        import jax.numpy as jnp
        _rk = jax.random.key(seed)
        x = 7.22e-05 + 1 * jax.random.normal(jax.random.fold_in(_rk, 1), (8, 112, 512), jnp.float32)
        _lenS = 112 - jax.random.randint(jax.random.fold_in(_rk, 7), (8,), 0, max(1, 112 // 4) + 1, jnp.int32)
        _lenS2 = 375 - jax.random.randint(jax.random.fold_in(_rk, 8), (8,), 0, max(1, 375 // 4) + 1, jnp.int32)
        _ctx_2048P = jax.random.normal(jax.random.fold_in(_rk, 11), (8, 16, 512), jnp.float32)
        _ctx_2048c = jax.random.dirichlet(jax.random.fold_in(_rk, 511), 0.3 * jnp.ones((16,), jnp.float32), (8, 375))
        _ctx_2048t = jnp.einsum('bsk,bkd->bsd', _ctx_2048c, _ctx_2048P)
        _ctx_2048t = _ctx_2048t * jax.lax.rsqrt(jnp.mean(jnp.square(_ctx_2048t)) + 1e-12) * 0.953939
        ctx_2048 = 4.13588e-05 + 0.999923 * (_ctx_2048t + 0.3 * jax.random.normal(jax.random.fold_in(_rk, 611), (8, 375, 512), jnp.float32))
        _validS = jnp.arange(112)[None, :] < _lenS[:, None]
        _validS2 = jnp.arange(375)[None, :] < _lenS2[:, None]
        _causal = jnp.tril(jnp.ones((112, 112), dtype=bool))
        mask_Bx1xSxS2_ff0 = jnp.where(jnp.ones((8, 1, 112, 375), dtype=bool), 0.0, -1000000000.0).astype(jnp.float32)
        return (x, ctx_2048, mask_Bx1xSxS2_ff0)
    x, ctx_2048, mask_Bx1xSxS2_ff0 = _rec_inputs()

    def _L0_xattn_setup():
        import jax, jax.numpy as jnp
        import numpy as np
        H = 512
        NH = 32
        KVH = 8
        HD = H // NH
        GROUPS = NH // KVH
        EPS = 1e-06
        B, L, S = (4, 256, 256)

        def _gqa_forward(hidden_state, encoder_hidden_state, encoder_attention_mask, Wq, bq, Wk, bk, Wv, bv, Wo, bo, gamma, beta):
            b, l, _ = hidden_state.shape
            s = encoder_hidden_state.shape[1]
            q = hidden_state @ Wq + bq
            k = encoder_hidden_state @ Wk + bk
            v = encoder_hidden_state @ Wv + bv
            q = q.reshape(b, l, KVH, GROUPS, HD).transpose(0, 2, 3, 1, 4)
            k = k.reshape(b, s, KVH, HD).transpose(0, 2, 1, 3)
            v = v.reshape(b, s, KVH, HD).transpose(0, 2, 1, 3)
            scale = 1.0 / jnp.sqrt(jnp.asarray(HD, q.dtype))
            scores = jnp.einsum('bkgld,bksd->bkgls', q, k) * scale
            scores = scores + encoder_attention_mask[:, :, None, :, :]
            attn = jax.nn.softmax(scores, axis=-1)
            out = jnp.einsum('bkgls,bksd->bkgld', attn, v)
            out = out.transpose(0, 3, 1, 2, 4).reshape(b, l, H)
            out = out @ Wo + bo
            x = out + hidden_state
            mu = jnp.mean(x, axis=-1, keepdims=True)
            var = jnp.var(x, axis=-1, keepdims=True)
            return (x - mu) * jax.lax.rsqrt(var + EPS) * gamma + beta
        key = jax.random.key(seed)
        ks = jax.random.split(key, 12)
        sd = 0.02
        return {'hidden_state': jax.random.normal(ks[0], (B, L, H), jnp.float32), 'encoder_hidden_state': jax.random.normal(ks[1], (B, S, H), jnp.float32), 'encoder_attention_mask': jnp.zeros((B, 1, L, S), jnp.float32), 'Wq': jax.random.normal(ks[2], (H, H), jnp.float32) * sd, 'bq': jnp.zeros((H,), jnp.float32), 'Wk': jax.random.normal(ks[3], (H, KVH * HD), jnp.float32) * sd, 'bk': jnp.zeros((KVH * HD,), jnp.float32), 'Wv': jax.random.normal(ks[4], (H, KVH * HD), jnp.float32) * sd, 'bv': jnp.zeros((KVH * HD,), jnp.float32), 'Wo': jax.random.normal(ks[5], (H, H), jnp.float32) * sd, 'bo': jnp.zeros((H,), jnp.float32), 'gamma': jnp.ones((H,), jnp.float32), 'beta': jnp.zeros((H,), jnp.float32)}
    _L0_xattn_all = _L0_xattn_setup()
    _L0_xattn_in = {k: v for k, v in _L0_xattn_all.items() if k in ('Wq', 'bq', 'Wk', 'bk', 'Wv', 'bv', 'Wo', 'bo', 'gamma', 'beta')}
    del _L0_xattn_all

    def _L1_xattn_setup():
        import jax, jax.numpy as jnp
        import numpy as np
        B, Q, S1, S2 = (4, 64, 512, 512)
        D, H, K, F = (512, 16, 128, 2048)
        LN_EPS = 1e-05

        def _layer_norm(x, scale, offset):
            mu = jnp.mean(x, axis=-1, keepdims=True)
            var = jnp.var(x, axis=-1, keepdims=True)
            return (x - mu) * jax.lax.rsqrt(var + LN_EPS) * scale + offset

        def _cross_attention(q_in, kv_in, wq, bq, wk, bk, wv, bv, wo, bo, bias_k, bias_v):
            b, q_len, _ = q_in.shape
            t = kv_in.shape[1]
            qh = (q_in @ wq + bq).reshape(b, q_len, H, K)
            kh = (kv_in @ wk + bk).reshape(b, t, H, K)
            vh = (kv_in @ wv + bv).reshape(b, t, H, K)
            kh = jnp.concatenate([kh, jnp.broadcast_to(bias_k, (b, 1, H, K))], axis=1)
            vh = jnp.concatenate([vh, jnp.broadcast_to(bias_v, (b, 1, H, K))], axis=1)
            scale = jnp.sqrt(jnp.asarray(K, q_in.dtype))
            logits = jnp.einsum('bqhk,bthk->bhqt', qh, kh) / scale
            weights = jax.nn.softmax(logits, axis=-1)
            ctx = jnp.einsum('bhqt,bthk->bqhk', weights, vh).reshape(b, q_len, H * K)
            return ctx @ wo + bo

        def _forward(x, xf_1, xf_2, ln1_scale, ln1_offset, wq1, bq1, wk1, bk1, wv1, bv1, wo1, bo1, bias_k1, bias_v1, ln2_scale, ln2_offset, wq2, bq2, wk2, bk2, wv2, bv2, wo2, bo2, bias_k2, bias_v2, ln_mlp_scale, ln_mlp_offset, w_fc1, b_fc1, w_fc2, b_fc2):
            res = x
            h = _layer_norm(x, ln1_scale, ln1_offset)
            x = res + _cross_attention(h, xf_1, wq1, bq1, wk1, bk1, wv1, bv1, wo1, bo1, bias_k1, bias_v1)
            res = x
            h = _layer_norm(x, ln2_scale, ln2_offset)
            x = res + _cross_attention(h, xf_2, wq2, bq2, wk2, bk2, wv2, bv2, wo2, bo2, bias_k2, bias_v2)
            h = _layer_norm(x, ln_mlp_scale, ln_mlp_offset)
            h = jax.nn.gelu(h @ w_fc1 + b_fc1, approximate=False) @ w_fc2 + b_fc2
            return x + h
        key = jax.random.key(seed)
        ks = iter(jax.random.split(key, 64))

        def rn(shape, s=0.02):
            return jax.random.normal(next(ks), shape, jnp.float32) * s
        inp = {'x': rn((B, Q, D), 1.0), 'xf_1': rn((B, S1, D), 1.0), 'xf_2': rn((B, S2, D), 1.0)}
        for i in (1, 2):
            inp[f'ln{i}_scale'] = jnp.ones((D,), jnp.float32)
            inp[f'ln{i}_offset'] = jnp.zeros((D,), jnp.float32)
            inp[f'wq{i}'] = rn((D, H * K))
            inp[f'bq{i}'] = jnp.zeros((H * K,), jnp.float32)
            inp[f'wk{i}'] = rn((D, H * K))
            inp[f'bk{i}'] = jnp.zeros((H * K,), jnp.float32)
            inp[f'wv{i}'] = rn((D, H * K))
            inp[f'bv{i}'] = jnp.zeros((H * K,), jnp.float32)
            inp[f'wo{i}'] = rn((H * K, D))
            inp[f'bo{i}'] = jnp.zeros((D,), jnp.float32)
            inp[f'bias_k{i}'] = rn((1, 1, H, K))
            inp[f'bias_v{i}'] = rn((1, 1, H, K))
        inp['ln_mlp_scale'] = jnp.ones((D,), jnp.float32)
        inp['ln_mlp_offset'] = jnp.zeros((D,), jnp.float32)
        inp['w_fc1'] = rn((D, F))
        inp['b_fc1'] = jnp.zeros((F,), jnp.float32)
        inp['w_fc2'] = rn((F, D))
        inp['b_fc2'] = jnp.zeros((D,), jnp.float32)
        return inp
    _L1_xattn_all = _L1_xattn_setup()
    _L1_xattn_in = {k: v for k, v in _L1_xattn_all.items() if k in ('ln1_scale', 'ln1_offset', 'wq1', 'bq1', 'wk1', 'bk1', 'wv1', 'bv1', 'wo1', 'bo1', 'bias_k1', 'bias_v1', 'ln2_scale', 'ln2_offset', 'wq2', 'bq2', 'wk2', 'bk2', 'wv2', 'bv2', 'wo2', 'bo2', 'bias_k2', 'bias_v2', 'ln_mlp_scale', 'ln_mlp_offset', 'w_fc1', 'b_fc1', 'w_fc2', 'b_fc2')}
    del _L1_xattn_all
    return {'x': x, 'ctx_2048': ctx_2048, 'mask_Bx1xSxS2_ff0': mask_Bx1xSxS2_ff0, 'L0_xattn_Wq': _L0_xattn_in['Wq'], 'L0_xattn_bq': _L0_xattn_in['bq'], 'L0_xattn_Wk': _L0_xattn_in['Wk'], 'L0_xattn_bk': _L0_xattn_in['bk'], 'L0_xattn_Wv': _L0_xattn_in['Wv'], 'L0_xattn_bv': _L0_xattn_in['bv'], 'L0_xattn_Wo': _L0_xattn_in['Wo'], 'L0_xattn_bo': _L0_xattn_in['bo'], 'L0_xattn_gamma': _L0_xattn_in['gamma'], 'L0_xattn_beta': _L0_xattn_in['beta'], 'L1_xattn_ln1_scale': _L1_xattn_in['ln1_scale'], 'L1_xattn_ln1_offset': _L1_xattn_in['ln1_offset'], 'L1_xattn_wq1': _L1_xattn_in['wq1'], 'L1_xattn_bq1': _L1_xattn_in['bq1'], 'L1_xattn_wk1': _L1_xattn_in['wk1'], 'L1_xattn_bk1': _L1_xattn_in['bk1'], 'L1_xattn_wv1': _L1_xattn_in['wv1'], 'L1_xattn_bv1': _L1_xattn_in['bv1'], 'L1_xattn_wo1': _L1_xattn_in['wo1'], 'L1_xattn_bo1': _L1_xattn_in['bo1'], 'L1_xattn_bias_k1': _L1_xattn_in['bias_k1'], 'L1_xattn_bias_v1': _L1_xattn_in['bias_v1'], 'L1_xattn_ln2_scale': _L1_xattn_in['ln2_scale'], 'L1_xattn_ln2_offset': _L1_xattn_in['ln2_offset'], 'L1_xattn_wq2': _L1_xattn_in['wq2'], 'L1_xattn_bq2': _L1_xattn_in['bq2'], 'L1_xattn_wk2': _L1_xattn_in['wk2'], 'L1_xattn_bk2': _L1_xattn_in['bk2'], 'L1_xattn_wv2': _L1_xattn_in['wv2'], 'L1_xattn_bv2': _L1_xattn_in['bv2'], 'L1_xattn_wo2': _L1_xattn_in['wo2'], 'L1_xattn_bo2': _L1_xattn_in['bo2'], 'L1_xattn_bias_k2': _L1_xattn_in['bias_k2'], 'L1_xattn_bias_v2': _L1_xattn_in['bias_v2'], 'L1_xattn_ln_mlp_scale': _L1_xattn_in['ln_mlp_scale'], 'L1_xattn_ln_mlp_offset': _L1_xattn_in['ln_mlp_offset'], 'L1_xattn_w_fc1': _L1_xattn_in['w_fc1'], 'L1_xattn_b_fc1': _L1_xattn_in['b_fc1'], 'L1_xattn_w_fc2': _L1_xattn_in['w_fc2'], 'L1_xattn_b_fc2': _L1_xattn_in['b_fc2']}

def reference(x, ctx_2048, mask_Bx1xSxS2_ff0, L0_xattn_Wq, L0_xattn_bq, L0_xattn_Wk, L0_xattn_bk, L0_xattn_Wv, L0_xattn_bv, L0_xattn_Wo, L0_xattn_bo, L0_xattn_gamma, L0_xattn_beta, L1_xattn_ln1_scale, L1_xattn_ln1_offset, L1_xattn_wq1, L1_xattn_bq1, L1_xattn_wk1, L1_xattn_bk1, L1_xattn_wv1, L1_xattn_bv1, L1_xattn_wo1, L1_xattn_bo1, L1_xattn_bias_k1, L1_xattn_bias_v1, L1_xattn_ln2_scale, L1_xattn_ln2_offset, L1_xattn_wq2, L1_xattn_bq2, L1_xattn_wk2, L1_xattn_bk2, L1_xattn_wv2, L1_xattn_bv2, L1_xattn_wo2, L1_xattn_bo2, L1_xattn_bias_k2, L1_xattn_bias_v2, L1_xattn_ln_mlp_scale, L1_xattn_ln_mlp_offset, L1_xattn_w_fc1, L1_xattn_b_fc1, L1_xattn_w_fc2, L1_xattn_b_fc2):
    import jax
    import jax.numpy as jnp

    def _L0_xattn_ref(hidden_state, encoder_hidden_state, encoder_attention_mask, Wq, bq, Wk, bk, Wv, bv, Wo, bo, gamma, beta):
        import jax, jax.numpy as jnp
        import numpy as np
        H = 512
        NH = 32
        KVH = 8
        HD = H // NH
        GROUPS = NH // KVH
        EPS = 1e-06
        B, L, S = (4, 256, 256)

        def _gqa_forward(hidden_state, encoder_hidden_state, encoder_attention_mask, Wq, bq, Wk, bk, Wv, bv, Wo, bo, gamma, beta):
            b, l, _ = hidden_state.shape
            s = encoder_hidden_state.shape[1]
            q = hidden_state @ Wq + bq
            k = encoder_hidden_state @ Wk + bk
            v = encoder_hidden_state @ Wv + bv
            q = q.reshape(b, l, KVH, GROUPS, HD).transpose(0, 2, 3, 1, 4)
            k = k.reshape(b, s, KVH, HD).transpose(0, 2, 1, 3)
            v = v.reshape(b, s, KVH, HD).transpose(0, 2, 1, 3)
            scale = 1.0 / jnp.sqrt(jnp.asarray(HD, q.dtype))
            scores = jnp.einsum('bkgld,bksd->bkgls', q, k) * scale
            scores = scores + encoder_attention_mask[:, :, None, :, :]
            attn = jax.nn.softmax(scores, axis=-1)
            out = jnp.einsum('bkgls,bksd->bkgld', attn, v)
            out = out.transpose(0, 3, 1, 2, 4).reshape(b, l, H)
            out = out @ Wo + bo
            x = out + hidden_state
            mu = jnp.mean(x, axis=-1, keepdims=True)
            var = jnp.var(x, axis=-1, keepdims=True)
            return (x - mu) * jax.lax.rsqrt(var + EPS) * gamma + beta
        return _gqa_forward(hidden_state, encoder_hidden_state, encoder_attention_mask, Wq, bq, Wk, bk, Wv, bv, Wo, bo, gamma, beta)

    def _L1_xattn_ref(x, xf_1, xf_2, ln1_scale, ln1_offset, wq1, bq1, wk1, bk1, wv1, bv1, wo1, bo1, bias_k1, bias_v1, ln2_scale, ln2_offset, wq2, bq2, wk2, bk2, wv2, bv2, wo2, bo2, bias_k2, bias_v2, ln_mlp_scale, ln_mlp_offset, w_fc1, b_fc1, w_fc2, b_fc2):
        import jax, jax.numpy as jnp
        import numpy as np
        B, Q, S1, S2 = (4, 64, 512, 512)
        D, H, K, F = (512, 16, 128, 2048)
        LN_EPS = 1e-05

        def _layer_norm(x, scale, offset):
            mu = jnp.mean(x, axis=-1, keepdims=True)
            var = jnp.var(x, axis=-1, keepdims=True)
            return (x - mu) * jax.lax.rsqrt(var + LN_EPS) * scale + offset

        def _cross_attention(q_in, kv_in, wq, bq, wk, bk, wv, bv, wo, bo, bias_k, bias_v):
            b, q_len, _ = q_in.shape
            t = kv_in.shape[1]
            qh = (q_in @ wq + bq).reshape(b, q_len, H, K)
            kh = (kv_in @ wk + bk).reshape(b, t, H, K)
            vh = (kv_in @ wv + bv).reshape(b, t, H, K)
            kh = jnp.concatenate([kh, jnp.broadcast_to(bias_k, (b, 1, H, K))], axis=1)
            vh = jnp.concatenate([vh, jnp.broadcast_to(bias_v, (b, 1, H, K))], axis=1)
            scale = jnp.sqrt(jnp.asarray(K, q_in.dtype))
            logits = jnp.einsum('bqhk,bthk->bhqt', qh, kh) / scale
            weights = jax.nn.softmax(logits, axis=-1)
            ctx = jnp.einsum('bhqt,bthk->bqhk', weights, vh).reshape(b, q_len, H * K)
            return ctx @ wo + bo

        def _forward(x, xf_1, xf_2, ln1_scale, ln1_offset, wq1, bq1, wk1, bk1, wv1, bv1, wo1, bo1, bias_k1, bias_v1, ln2_scale, ln2_offset, wq2, bq2, wk2, bk2, wv2, bv2, wo2, bo2, bias_k2, bias_v2, ln_mlp_scale, ln_mlp_offset, w_fc1, b_fc1, w_fc2, b_fc2):
            res = x
            h = _layer_norm(x, ln1_scale, ln1_offset)
            x = res + _cross_attention(h, xf_1, wq1, bq1, wk1, bk1, wv1, bv1, wo1, bo1, bias_k1, bias_v1)
            res = x
            h = _layer_norm(x, ln2_scale, ln2_offset)
            x = res + _cross_attention(h, xf_2, wq2, bq2, wk2, bk2, wv2, bv2, wo2, bo2, bias_k2, bias_v2)
            h = _layer_norm(x, ln_mlp_scale, ln_mlp_offset)
            h = jax.nn.gelu(h @ w_fc1 + b_fc1, approximate=False) @ w_fc2 + b_fc2
            return x + h
        return _forward(x, xf_1, xf_2, ln1_scale, ln1_offset, wq1, bq1, wk1, bk1, wv1, bv1, wo1, bo1, bias_k1, bias_v1, ln2_scale, ln2_offset, wq2, bq2, wk2, bk2, wv2, bv2, wo2, bo2, bias_k2, bias_v2, ln_mlp_scale, ln_mlp_offset, w_fc1, b_fc1, w_fc2, b_fc2)
    x = _L0_xattn_ref(x, ctx_2048, mask_Bx1xSxS2_ff0, L0_xattn_Wq, L0_xattn_bq, L0_xattn_Wk, L0_xattn_bk, L0_xattn_Wv, L0_xattn_bv, L0_xattn_Wo, L0_xattn_bo, L0_xattn_gamma, L0_xattn_beta)
    x = _L1_xattn_ref(x, ctx_2048, ctx_2048, L1_xattn_ln1_scale, L1_xattn_ln1_offset, L1_xattn_wq1, L1_xattn_bq1, L1_xattn_wk1, L1_xattn_bk1, L1_xattn_wv1, L1_xattn_bv1, L1_xattn_wo1, L1_xattn_bo1, L1_xattn_bias_k1, L1_xattn_bias_v1, L1_xattn_ln2_scale, L1_xattn_ln2_offset, L1_xattn_wq2, L1_xattn_bq2, L1_xattn_wk2, L1_xattn_bk2, L1_xattn_wv2, L1_xattn_bv2, L1_xattn_wo2, L1_xattn_bo2, L1_xattn_bias_k2, L1_xattn_bias_v2, L1_xattn_ln_mlp_scale, L1_xattn_ln_mlp_offset, L1_xattn_w_fc1, L1_xattn_b_fc1, L1_xattn_w_fc2, L1_xattn_b_fc2)
    return x

_drawn_inputs = setup_inputs


def setup_inputs(seed=0):
    import zlib

    import numpy as np

    out = dict(_drawn_inputs(seed))
    spreads = {'L0_xattn_bq': (0.0, 0.8),
     'L0_xattn_bk': (0.0, 2.0),
     'L0_xattn_bv': (0.0, 0.1),
     'L0_xattn_bo': (0.0, 0.1),
     'L0_xattn_gamma': (1.0, 0.2),
     'L0_xattn_beta': (0.0, 0.1),
     'L1_xattn_ln1_scale': (1.0, 0.6),
     'L1_xattn_ln1_offset': (0.0, 0.8),
     'L1_xattn_bq1': (0.0, 0.8),
     'L1_xattn_bk1': (0.0, 2.0),
     'L1_xattn_bv1': (0.0, 0.1),
     'L1_xattn_bo1': (0.0, 0.1),
     'L1_xattn_ln2_scale': (1.0, 0.6),
     'L1_xattn_ln2_offset': (0.0, 0.8),
     'L1_xattn_bq2': (0.0, 0.8),
     'L1_xattn_bk2': (0.0, 2.0),
     'L1_xattn_bv2': (0.0, 0.1),
     'L1_xattn_bo2': (0.0, 0.1),
     'L1_xattn_ln_mlp_scale': (1.0, 0.2),
     'L1_xattn_ln_mlp_offset': (0.0, 0.361),
     'L1_xattn_b_fc1': (0.0, 0.1),
     'L1_xattn_b_fc2': (0.0, 0.1)}
    factors = {'L0_xattn_Wq': 8.0,
     'L0_xattn_Wk': 7.818,
     'L1_xattn_wq1': 4.013,
     'L1_xattn_wk1': 3.913,
     'L1_xattn_bias_k1': 64.0,
     'L1_xattn_bias_v1': 64.0,
     'L1_xattn_wq2': 4.045,
     'L1_xattn_wk2': 3.962,
     'L1_xattn_bias_k2': 64.0,
     'L1_xattn_bias_v2': 64.0}
    for name, (base, spread) in spreads.items():
        noise = np.random.default_rng([zlib.crc32(name.encode()), seed]).standard_normal(out[name].shape)
        drawn = base * np.exp(spread * noise) if base else spread * noise
        out[name] = jnp.asarray(drawn.astype(out[name].dtype))
    for name, factor in factors.items():
        out[name] = (out[name] * factor).astype(out[name].dtype)
    return out
```

```python
from contextlib import ExitStack

import concourse.bass as bass
from concourse import mybir

F32 = mybir.dt.float32
F32R = mybir.dt.float32r
ALU = mybir.AluOpType
ACT = mybir.ActivationFunctionType
AX_X = mybir.AxisListType.X

P = 128
B, L, S, D = 8, 112, 375, 512
HALVES = 2
HB = B // HALVES
T = HB * L
DC = D // P
SC = 3
KC = S // SC
SK = S + 1
NH0, HD0 = 32, 16
C0 = 4
HPC = NH0 // C0
KV2 = 2
ATT = 2
NH1, HD1 = 16, 128
G1 = 4
HPG = NH1 // G1
GW = HPG * HD1
MLPG = 4
SCALE0 = 0.25
SCALE1 = float(HD1) ** -0.5
EPS0, EPS1 = 1e-6, 1e-5

PJ, SCR, TP = 3, 2, 2

PJ_C = HB * SC
PJ_CU = 15
PJ_W0 = PJ_C + C0 * PJ_CU
PJ_A = PJ_W0 + 6
PJ_GU = HPG + HB * (HPG + SC) + HB
PJ_AU = 6 + G1 * PJ_GU
PJ_M = PJ_A + ATT * PJ_AU
PJ_MU = 9
PJ_H = PJ_M + 6 + MLPG * PJ_MU

MID_C = HB * SC
MID_CU = HB
MID_A = MID_C + C0 * MID_CU
MID_GU = HPG + HB * (HPG + SC)
MID_AU = HB + G1 * MID_GU
MID_M = MID_A + ATT * MID_AU
MID_H = MID_M + HB + MLPG * HPG

K_UNIT = (1, 10, 11, 12)
PLACED = 2
SC_CU, SC_GU = HB * HPC, HB * HPG
SC_A = C0 * SC_CU
SC_H = SC_A + ATT * G1 * SC_GU
TP_CU = HB * HPC + HB
TP_A = C0 * TP_CU
TP_H = TP_A + ATT * G1 * SC_GU
O_A = C0 * HB
O_H = O_A + ATT * G1 * HB

WQ_H = C0 + ATT * G1 + MLPG
WK_H = C0 + ATT * G1
WV_H = 1 + ATT * G1
WO_H = 1 + ATT * G1 + MLPG
RAW_X = 2 + HB * DC
RAW_C = RAW_X + DC
RAW_W0 = RAW_C + 2 * C0
RAW_A = RAW_W0 + DC
RAW_GU = 4 * DC
RAW_M = RAW_A + ATT * G1 * RAW_GU
RAW_H = RAW_M + MLPG * 2 * DC
assert PJ_H % PJ == 0 and PJ_A % PJ == 0 and PJ_GU % PJ == 0 and PJ_MU % PJ == 0
assert RAW_C % 2 == 0 and RAW_W0 % 2 == 0

PRM_LN = ATT * G1 * 16
PRM_B1 = PRM_LN + 3 * 8
PRM_C = PRM_B1 + 16
PRM_N = PRM_C + C0 * 3
NL = ATT + 1


def tp_unit(u, h):
    return 4 * u + h + max(0, (u - 1) // 2)


def tp_out_unit(b):
    return 4 * (2 * b + 3) + b if b < HB - 1 else TP_CU - 1


def xattn_program(nc, x, x_t, ctx_t, mask, wq0, wk0, wv0, wo0, wq, wk, wv, wo, w1, w2,
                  bias_v, bv, prm_in, rows_in, out):
    bv_hi_dram = nc.dram_tensor("bv_hi_scratch", (ATT * G1, GW), F32, kind="Internal").ap()
    bv_lo_dram = nc.dram_tensor("bv_lo_scratch", (ATT * G1, GW), F32, kind="Internal").ap()

    with ExitStack() as ctx:
        def sb(name, shape, dt=F32):
            return ctx.enter_context(nc.sbuf_tensor(name, shape, dt))

        def sem(name):
            return ctx.enter_context(nc.semaphore(name))

        ctx_hi = sb("ctx_hi", [P, DC, HB, SK], F32R)
        ctx_lo = sb("ctx_lo", [P, DC, HB, SK], F32R)
        h_hi = sb("h_hi", [P, DC, T], F32R)
        h_lo = sb("h_lo", [P, DC, T], F32R)
        qo_hi = sb("qo_hi", [P, 2 * HPG, T], F32R)
        qo_lo = sb("qo_lo", [P, 2 * HPG, T], F32R)
        k_hi = sb("k_hi", [P, HPG, SK], F32R)
        k_lo = sb("k_lo", [P, HPG, SK], F32R)
        v_hi = sb("v_hi", [P, SC * GW], F32R)
        v_lo = sb("v_lo", [P, SC * GW], F32R)
        probs = sb("probs", [P, HPG, 384])
        pt_hi = sb("pt_hi", [P, HPG, SC * L], F32R)
        pt_lo = sb("pt_lo", [P, HPG, SC * L], F32R)
        w_hi = {n: sb(f"w{n}_hi", [P, DC, GW], F32R) for n in "qkvo"}
        w_lo = {n: sb(f"w{n}_lo", [P, DC, GW], F32R) for n in "qkvo"}
        raw = sb("raw", [P, 2, GW])
        xacc = sb("xacc", [P, HB * D])
        ident = sb("ident", [P, P])
        o_nat = sb("o_nat", [P, HPC, HD0])
        prm = sb("prm", [P, PRM_N])
        cur = sb("cur", [P, 16])
        ln_cur = sb("ln_cur", [P, 8])
        neg_max = sb("neg_max", [P, HPC])
        row_sum = sb("row_sum", [P, 2, HPC])
        inv_sum = sb("inv_sum", [P, HPC])
        stats = sb("stats", [P, HB, 6])
        mean_var = sb("mean_var", [P, HB, 2])
        std = sb("std", [P, HB])
        rstd = sb("rstd", [P, HB])
        eps = sb("eps", [P, 2])

        probs_flat = probs[:].rearrange("p h n -> p (h n)")
        tmp = [probs_flat[:, 512 * i:512 * i + 512] for i in range(3)]
        xa = xacc[:].rearrange("p (b n) -> p b n", b=HB)
        mask_v = xacc[0:L, 0:HB * S].rearrange("p (b n) -> p b n", b=HB)
        q0_f32 = xacc[:, 1536:1536 + T]
        q0_split = [qo_lo[:, e, :] for e in range(2)]
        place_sel = qo_lo[:].rearrange("p h n -> p (h n)")[:, 2 * T:2 * T + 2 * HPC * P].rearrange(
            "p (e j m) -> p e j m", e=2, j=HPC)
        v0 = [v[:].rearrange("p (n d) -> p n d", d=P) for v in (v_hi, v_lo)]
        v1 = [v[:].rearrange("p (c n) -> p c n", c=SC) for v in (v_hi, v_lo)]
        v0c = k_hi[:].rearrange("p h n -> p (h n)")[:, SK:SK + 768].rearrange(
            "p (n k e) -> p n k e", k=KV2, e=2 * HD0)
        wv_flat = [w["v"][:].rearrange("p c n -> p (c n)") for w in (w_hi, w_lo)]
        ot0 = [w[:, 0:C0 * T].rearrange("p (c t) -> p c t", c=C0) for w in wv_flat]
        flat = {n: [w[n][:].rearrange("p c n -> p (c n)") for w in (w_hi, w_lo)] for n in "qkvo"}

        pj = [ctx.enter_context(nc.psum_tensor(f"pj{i}", [P, 512], F32)) for i in range(PJ)]
        scores = [ctx.enter_context(nc.psum_tensor(f"scores{i}", [P, 512], F32)) for i in range(SCR)]
        tp = [ctx.enter_context(nc.psum_tensor(f"tp{i}", [P, 512], F32)) for i in range(TP)]
        o_ps = ctx.enter_context(nc.psum_tensor("o_ps", [P, 512], F32))

        pj_ready, pj_mid, pj_free = sem("pj_ready"), sem("pj_mid"), sem("pj_free")
        sc_ready = sem("sc_ready")
        tp_ready, tp_mid, tp_free = sem("tp_ready"), sem("tp_mid"), sem("tp_free")
        o_ready, o_mid, o_free = sem("o_ready"), sem("o_mid"), sem("o_free")
        max_ready, exp_ready = sem("max_ready"), sem("exp_ready")
        inv_ready, norm_ready = sem("inv_ready"), sem("norm_ready")
        raw_ready = [sem("raw_ready0"), sem("raw_ready1")]
        raw_free = [sem("raw_free0"), sem("raw_free1")]
        split_hi = sem("split_hi")
        w_ready = {n: sem(f"w{n}_ready") for n in "qkvo"}
        w_free = {n: sem(f"w{n}_free") for n in "qkvo"}
        tok_ready, ctx_ready = sem("tok_ready"), sem("ctx_ready")
        cur_ready, q0_hi, sel_zero = sem("cur_ready"), sem("q0_hi"), sem("sel_zero")
        q0_ready, v0c_ready, kbias_hi = sem("q0_ready"), sem("v0c_ready"), sem("kbias_hi")
        o_sum, o_inv, o_nat_ready = sem("o_sum"), sem("o_inv"), sem("o_nat_ready")
        qh_done = sem("qh_done")
        ln_chain, std_ready, xn_ready, ln_t, ln_par = (
            sem("ln_chain"), sem("std_ready"), sem("xn_ready"), sem("ln_t"), sem("ln_par"))
        post_ln, bias_added = sem("post_ln"), sem("bias_added")
        mask_in, x_in, rows_ready, bvrow_in, out_done = (
            sem("mask_in"), sem("x_in"), sem("rows_ready"), sem("bvrow_in"), sem("out_done"))
        setup_dma, setup_dve, setup_pool, setup_bv = (
            sem("setup_dma"), sem("setup_dve"), sem("setup_pool"), sem("setup_bv"))

        pool_passed, dve_passed, pe_passed = sem("pool_passed"), sem("dve_passed"), sem("pe_passed")

        block = ctx.enter_context(nc.Block())

        @block.sync
        def _(sp):
            sp.dma_start(prm[:], prm_in).then_inc(setup_dma, 16)
            sp.dma_start(xa[0:ATT * G1, 0, :], bias_v).then_inc(setup_dma, 16)
            sp.dma_start(xa[0:ATT * G1, 1, :], bv).then_inc(setup_dma, 16)

            def load(half_use, n, src, shape):
                slot = n % 2
                dst = raw[:, slot, 0:shape[0] * shape[1]]
                if shape[0] > 1:
                    dst = dst.rearrange("p (c n) -> p c n", c=shape[0])
                sp.wait_ge(raw_free[slot], half_use + n // 2 + 1)
                sp.dma_start(dst, src).then_inc(raw_ready[slot], 16)

            with sp.Fori(0, HALVES) as hf:
                base = hf * (RAW_H // 2)
                for i in range(2):
                    load(base, i, wv0[2 * i * P:(2 * i + 2) * P, :].rearrange(
                        "(c p) n -> p c n", p=P), (2, P))
                for b in range(HB):
                    for c in range(DC):
                        load(base, 2 + b * DC + c,
                             ctx_t[c * P:(c + 1) * P, bass.ds(hf * HB + b, 1), :].rearrange(
                                 "p b n -> p (b n)"), (1, S))
                for c in range(DC):
                    load(base, RAW_X + c, x_t[c * P:(c + 1) * P, bass.ds(hf * T, T)], (1, T))
                with sp.Fori(0, C0) as c:
                    cb = base + RAW_C // 2 + c
                    load(cb, 0, wq0[:, bass.ds(c * P, P)].rearrange("(c p) n -> p c n", p=P), (DC, P))
                    load(cb, 1, wk0[:, bass.ds(c * P, P)].rearrange("(c p) n -> p c n", p=P), (DC, P))
                for c in range(DC):
                    load(base, RAW_W0 + c, wo0[c * P:(c + 1) * P, :], (1, GW))
                with sp.Fori(0, ATT) as a:
                    with sp.Fori(0, G1) as g:
                        gb = base + RAW_A // 2 + (a * G1 + g) * (RAW_GU // 2)
                        for i, w in enumerate((wq, wk, wv)):
                            for c in range(DC):
                                load(gb, DC * i + c,
                                     w[bass.ds(a * D + c * P, P), bass.ds(g * GW, GW)], (1, GW))
                        for c in range(DC):
                            load(gb, 3 * DC + c,
                                 wo[bass.ds((a * G1 + g) * GW + c * P, P), :], (1, GW))
                with sp.Fori(0, MLPG) as m:
                    mb = base + RAW_M // 2 + m * DC
                    for c in range(DC):
                        load(mb, c, w1[c * P:(c + 1) * P, bass.ds(m * GW, GW)], (1, GW))
                    for c in range(DC):
                        load(mb, DC + c, w2[bass.ds(m * GW + c * P, P), :], (1, GW))
            sp.wait_ge(out_done, 16 * (HALVES + 1))

        @block.gpsimd
        def _(pool):
            nc.gpsimd.memset(ident[:], 0.0).then_inc(setup_pool, 1)
            nc.gpsimd.memset(eps[:, 0:1], EPS0)
            nc.gpsimd.memset(eps[:, 1:2], EPS1)
            nc.gpsimd.memset(ctx_hi[:, :, :, S:SK].bitcast(F32), 0.0)
            nc.gpsimd.memset(ctx_lo[:, :, :, S:SK].bitcast(F32), 0.0)
            pool.wait_ge(setup_pool, 1)
            nc.gpsimd.affine_select(out=ident[:], in_=ident[:], compare_op=ALU.not_equal, fill=1.0,
                                    base=0, pattern=[[-1, P]], channel_multiplier=1).then_inc(setup_pool, 1)
            for s in raw_free:
                pool.sem_inc(s, 1)

            def split(half_base, n, shape, hi, lo, signal, k):
                slot = n % 2
                src = raw[:, slot, 0:shape[0] * shape[1]]
                if shape[0] > 1:
                    src = src.rearrange("p (c n) -> p c n", c=shape[0])
                pool.wait_ge(raw_ready[slot], (half_base + (n // 2 + 1)) * 16)
                pool.sem_inc(pool_passed, 1)
                nc.gpsimd.tensor_scalar(hi, src, 1.0, 0.0, ALU.mult, ALU.add).then_inc(split_hi, 1)
                pool.wait_ge(split_hi, half_base * 2 + n + 1)
                nc.gpsimd.tensor_tensor(lo, src, hi.bitcast(F32), ALU.subtract).then_inc(signal, k)
                return slot

            def split_free(half_base, n, shape, hi, lo, signal, k, done):
                slot = split(half_base, n, shape, hi, lo, signal, k)
                pool.wait_ge(signal, done)
                pool.sem_inc(raw_free[slot], 1)

            def weights(half_base, n0, name, use, pieces=DC):
                pool.wait_ge(w_free[name], use + 1)
                for c in range(pieces):
                    if pieces == DC:
                        hi, lo, shape = w_hi[name][:, c, :], w_lo[name][:, c, :], (1, GW)
                    else:
                        wd = DC // pieces * P
                        hi, lo = (f[:, wd * c:wd * c + wd].rearrange("p (c n) -> p c n", n=P)
                                  for f in flat[name])
                        shape = (DC // pieces, P)
                    k = DC // pieces
                    split_free(half_base, n0 + c, shape, hi, lo, w_ready[name], k,
                               use * DC + k * (c + 1))

            with pool.Fori(0, HALVES) as hf:
                base = hf * (RAW_H // 2)
                pool.wait_ge(pj_free, hf * PJ_H + PJ)
                weights(base, 0, "v", hf * WV_H, pieces=2)
                for b in range(HB):
                    for c in range(DC):
                        split_free(base, 2 + b * DC + c, (1, S), ctx_hi[:, c, b, 0:S],
                                   ctx_lo[:, c, b, 0:S], ctx_ready, 1,
                                   hf * (HB * DC) + b * DC + c + 1)
                for c in range(DC):
                    split_free(base, RAW_X + c, (1, T), h_hi[:, c, :], h_lo[:, c, :], tok_ready, 1,
                               hf * DC + c + 1)
                with pool.Fori(0, C0) as c:
                    weights(base + RAW_C // 2 + c, 0, "q", hf * WQ_H + c, pieces=1)
                    weights(base + RAW_C // 2 + c, 1, "k", hf * WK_H + c, pieces=1)
                weights(base, RAW_W0, "o", hf * WO_H)
                with pool.Fori(0, ATT) as a:
                    with pool.Fori(0, G1) as g:
                        gb = base + RAW_A // 2 + (a * G1 + g) * (RAW_GU // 2)
                        weights(gb, 0, "q", hf * WQ_H + C0 + a * G1 + g)
                        weights(gb, DC, "k", hf * WK_H + C0 + a * G1 + g)
                        weights(gb, 2 * DC, "v", hf * WV_H + 1 + a * G1 + g)
                        weights(gb, 3 * DC, "o", hf * WO_H + 1 + a * G1 + g)
                with pool.Fori(0, MLPG) as m:
                    mb = base + RAW_M // 2 + m * DC
                    weights(mb, 0, "q", hf * WQ_H + C0 + ATT * G1 + m)
                    weights(mb, DC, "o", hf * WO_H + 1 + ATT * G1 + m)

        @block.tensor
        def _(pe):
            def three(dst, lhs, rhs, first, last):
                (l_hi, l_lo), (r_hi, r_lo) = lhs, rhs
                nc.tensor.matmul(dst, l_hi, r_hi, start=first, stop=False)
                nc.tensor.matmul(dst, l_hi, r_lo, start=False, stop=False)
                return nc.tensor.matmul(dst, l_lo, r_hi, start=False, stop=last)

            def transpose(dst, src, parts):
                return nc.tensor.transpose(dst, src, ident[0:parts, 0:parts])

            def q_stage(base, use, unit, width=GW):
                for h in range(width // P):
                    pe.wait_ge(pj_free, base + unit + h + 1)
                    for c in range(DC):
                        if h == 0:
                            pe.wait_ge(w_ready["q"], use * DC + (c + 1 if width == GW else DC))
                        lhs = ([w["q"][:, c, h * P:(h + 1) * P] for w in (w_hi, w_lo)] if width == GW
                               else [f[:, c * P:(c + 1) * P] for f in flat["q"]])
                        last = three(pj[(unit + h) % PJ][:, 0:T], lhs,
                                     (h_hi[:, c, :], h_lo[:, c, :]), c == 0, c == DC - 1)
                    last.then_inc(pj_ready, 1)

            def out_stage(base, use, unit, src, ready, pad=1):
                for b in range(HB):
                    ready(b)
                    pe.wait_ge(pj_free, base + unit + b + 1)
                    for h in range(HPG):
                        if b == 0:
                            pe.wait_ge(w_ready["o"], use * DC + h + 1)
                        last = three(pj[(unit + b) % PJ][0:L, :],
                                     [s[:, h, b * L:(b + 1) * L] for s in src],
                                     (w_hi["o"][:, h, :], w_lo["o"][:, h, :]), h == 0, h == HPG - 1)
                    last.then_inc(pj_ready, pad if b == HB - 1 else 1)

            def ln_stage(base, unit, nl):
                for b in range(HB):
                    pe.wait_ge(xn_ready, nl * HB + b + 1)
                    pe.wait_ge(pj_free, base + unit + b + 1)
                    for c in range(DC):
                        last = transpose(pj[(unit + b) % PJ][:, c * L:(c + 1) * L],
                                         tmp[0][0:L, c * P:(c + 1) * P], L)
                    last.then_inc(pj_ready, 3 if b == HB - 1 else 1)

            pe.wait_ge(setup_dve, 1)
            with pe.Fori(0, HALVES) as hf:
                pjb = hf * PJ_H
                for b in range(HB):
                    pe.wait_ge(ctx_ready, hf * (HB * DC) + (b + 1) * DC)
                    for s in range(SC):
                        unit = b * SC + s
                        pe.wait_ge(pj_free, pjb + unit + 1)
                        if unit == 0:
                            pe.wait_ge(w_ready["v"], hf * WV_H * DC + DC)
                        for c in range(DC):
                            last = three(pj[unit % PJ][0:KC, 0:P],
                                         [t[:, c, b, s * KC:(s + 1) * KC] for t in (ctx_hi, ctx_lo)],
                                         [f[:, c * P:(c + 1) * P] for f in flat["v"]],
                                         c == 0, c == DC - 1)
                        last.then_inc(pj_ready, 1)
                pe.wait_ge(tok_ready, hf * DC + DC)
                pe.sem_inc(pe_passed, 1)
                with pe.Fori(0, C0) as c8:
                    cpj = pjb + c8 * PJ_CU + PJ_C
                    csc = hf * SC_H + c8 * SC_CU
                    ctp = hf * TP_H + c8 * TP_CU
                    co = hf * O_H + c8 * HB
                    q_stage(cpj, hf * WQ_H + c8, 0, width=P)

                    def keys0(b):
                        pe.wait_ge(pj_free, cpj + K_UNIT[b] + 1)
                        if b == 0:
                            pe.wait_ge(w_ready["k"], (hf * WK_H + c8) * DC + DC)
                        for c in range(DC):
                            last = three(pj[K_UNIT[b] % PJ][:, 0:SK],
                                         [f[:, c * P:(c + 1) * P] for f in flat["k"]],
                                         (ctx_hi[:, c, b, :], ctx_lo[:, c, b, :]), c == 0, c == DC - 1)
                        last.then_inc(pj_ready, 3 if b == HB - 1 else 1)

                    def place(js):
                        for j in js:
                            unit = PLACED + j
                            if j == 0:
                                pe.wait_ge(pj_free, cpj + 1 + PJ)
                            pe.wait_ge(pj_free, cpj + unit + 1)
                            for e in range(2):
                                last = nc.tensor.matmul(pj[unit % PJ][:, 0:T], place_sel[:, e, j, :],
                                                        q0_split[e], start=(e == 0), stop=(e == 1))
                            last.then_inc(pj_ready, 1)

                    def scores0(u, h):
                        b, j = u // 2, (u % 2) * 4 + h
                        if u % 2 == 0 and h == 0:
                            pe.wait_ge(pj_free, cpj + K_UNIT[b] + 1 + PJ)
                        if b == 0:
                            pe.wait_ge(pj_free, cpj + PLACED + j + 1 + PJ)
                        pe.wait_ge(max_ready, csc + 4 * u + h + 1)
                        nc.tensor.matmul(scores[h % SCR][0:L, 0:SK], qo_hi[:, j, b * L:(b + 1) * L],
                                         k_hi[:, 0, :], start=True, stop=True).then_inc(sc_ready, 1)

                    def out_transpose0(b):
                        n = tp_out_unit(b)
                        pe.wait_ge(o_nat_ready, (hf * C0 + c8) * HB + b + 1)
                        pe.wait_ge(tp_free, ctp + n + 1)
                        transpose(tp[n % TP][:, 0:L],
                                  o_nat[0:L, :, :].rearrange("p h d -> p (h d)"), L).then_inc(tp_ready, 1)

                    keys0(0)
                    place(range(4))
                    for h in range(4):
                        scores0(0, h)
                    place(range(4, 8))
                    for u in range(2 * HB):
                        b, hh = u // 2, u % 2
                        for h in range(4):
                            n = tp_unit(u, h)
                            pe.wait_ge(exp_ready, csc + 4 * u + h + 1 + SCR)
                            pe.wait_ge(tp_free, ctp + n + 1)
                            for s in range(SC):
                                last = transpose(tp[n % TP][0:KC, s * L:(s + 1) * L],
                                                 probs[0:L, h, s * KC:(s + 1) * KC], L)
                            last.then_inc(tp_ready, 1)
                            if u + 1 < 2 * HB:
                                scores0(u + 1, h)
                        if u % 2 == 0 and u + 2 < 2 * HB:
                            keys0((u + 2) // 2)
                        if u % 2 == 0 and u >= 2:
                            out_transpose0(u // 2 - 1)
                        if u == 0:
                            pe.wait_ge(v0c_ready, (hf * C0 + c8) * 2 + 2)
                        if hh == 0:
                            pe.wait_ge(o_free, co + b + 1)
                        for h in range(4):
                            j = hh * 4 + h
                            pe.wait_ge(tp_free, ctp + tp_unit(u, h) + 1 + TP)
                            for s in range(SC):
                                keys = slice(s * L, (s + 1) * L)
                                nc.tensor.matmul(o_ps[0:L, 32 * j:32 * j + 32], pt_hi[0:KC, h, keys],
                                                 v0c[0:KC, b * SC + s, hh, :], start=(s == 0), stop=False)
                                last = nc.tensor.matmul(o_ps[0:L, 32 * j:32 * j + HD0], pt_lo[0:KC, h, keys],
                                                        v0c[0:KC, b * SC + s, hh, 0:HD0], start=False,
                                                        stop=(s == SC - 1))
                        if hh == 1:
                            last.then_inc(o_ready, 1)
                    out_transpose0(HB - 1)

                def ready0(b):
                    if b == 0:
                        pe.wait_ge(tp_free, hf * TP_H + TP_A + TP)
                out_stage(pjb + PJ_W0, hf * WO_H, 0, ot0, ready0, pad=3)

                with pe.Fori(0, ATT) as a:
                    apj = pjb + a * PJ_AU + PJ_A
                    ln_stage(apj, 0, hf * NL + a)
                    pe.wait_ge(pj_free, apj + 6 + PJ)
                    pe.sem_inc(pe_passed, 1)
                    with pe.Fori(0, G1) as g:
                        ag = a * G1 + g
                        gpj = apj + g * PJ_GU + 6
                        gsc = hf * SC_H + ag * SC_GU + SC_A
                        gtp = hf * TP_H + ag * SC_GU + TP_A
                        go = hf * O_H + ag * HB + O_A
                        use_k, use_v = hf * WK_H + ag + C0, hf * WV_H + ag + 1

                        def keys1(b, h):
                            unit = HPG + b * (HPG + SC) + h
                            pe.wait_ge(pj_free, gpj + unit + 1)
                            for c in range(DC):
                                if b == 0 and h == 0:
                                    pe.wait_ge(w_ready["k"], use_k * DC + c + 1)
                                last = three(pj[unit % PJ][:, 0:SK],
                                             [w["k"][:, c, h * P:(h + 1) * P] for w in (w_hi, w_lo)],
                                             (ctx_hi[:, c, b, :], ctx_lo[:, c, b, :]),
                                             c == 0, c == DC - 1)
                            last.then_inc(pj_ready, 1)

                        def values1(b, s):
                            unit = HPG + b * (HPG + SC) + HPG + s
                            pe.wait_ge(pj_free, gpj + unit + 1)
                            for c in range(DC):
                                if b == 0 and s == 0:
                                    pe.wait_ge(w_ready["v"], use_v * DC + c + 1)
                                last = three(pj[unit % PJ][0:KC, :],
                                             [t[:, c, b, s * KC:(s + 1) * KC] for t in (ctx_hi, ctx_lo)],
                                             (w_hi["v"][:, c, :], w_lo["v"][:, c, :]),
                                             c == 0, c == DC - 1)
                            last.then_inc(pj_ready, 1)

                        def scores1(b, h):
                            n = b * HPG + h
                            if h == 0:
                                pe.wait_ge(pj_free, gpj + HPG + b * (HPG + SC) + HPG + PJ)
                            pe.wait_ge(exp_ready, gsc + n + 1)
                            three(scores[n % SCR][0:L, 0:SK],
                                  [q[:, h, b * L:(b + 1) * L] for q in (qo_hi, qo_lo)],
                                  (k_hi[:, h, :], k_lo[:, h, :]), True, True).then_inc(sc_ready, 1)

                        def transpose1(b, h):
                            n = b * HPG + h
                            pe.wait_ge(norm_ready, (hf * ATT * G1 + ag) * SC_GU + n + 1)
                            pe.wait_ge(tp_free, gtp + n + 1)
                            for s in range(SC):
                                last = transpose(tp[n % TP][0:KC + 1, s * L:(s + 1) * L],
                                                 probs[0:L, h, s * KC:(s + 1) * KC + 1], L)
                            last.then_inc(tp_ready, 1)

                        def weigh1(b):
                            if b == 0:
                                pe.wait_ge(bvrow_in, (hf * ATT * G1 + ag) * 32 + 32)
                            pe.wait_ge(pj_free, gpj + HPG + (b + 1) * (HPG + SC) + PJ)
                            pe.wait_ge(o_free, go + b + 1)
                            for h in range(HPG):
                                pe.wait_ge(tp_free, gtp + b * HPG + h + 1 + TP)
                                for s in range(SC):
                                    n = KC + 1 if s == SC - 1 else KC
                                    last = three(o_ps[:, h * L:(h + 1) * L],
                                                 [v[0:n, s, h * P:(h + 1) * P] for v in v1],
                                                 [q[0:n, h, s * L:(s + 1) * L] for q in (pt_hi, pt_lo)],
                                                 s == 0, s == SC - 1)
                            last.then_inc(o_ready, 1)

                        q_stage(gpj, hf * WQ_H + ag + C0, 0)
                        for b in range(HB):
                            if b > 0:
                                transpose1(b - 1, 0)
                                transpose1(b - 1, 1)
                            keys1(b, 0)
                            if b > 0:
                                transpose1(b - 1, 2)
                                transpose1(b - 1, 3)
                            for h in range(1, HPG):
                                keys1(b, h)
                            if b > 0:
                                weigh1(b - 1)
                            values1(b, 0)
                            scores1(b, 0)
                            scores1(b, 1)
                            values1(b, 1)
                            scores1(b, 2)
                            scores1(b, 3)
                            values1(b, 2)
                        for h in range(HPG):
                            transpose1(HB - 1, h)
                        weigh1(HB - 1)

                        def ready1(b):
                            pe.wait_ge(o_free, go + b + 1 + 1)
                        out_stage(gpj, hf * WO_H + ag + 1, PJ_GU - HB,
                                  [q[:, HPG:2 * HPG, :] for q in (qo_hi, qo_lo)], ready1)

                ln_stage(pjb + PJ_M, 0, hf * NL + ATT)
                pe.wait_ge(pj_free, pjb + PJ_M + 6 + PJ)
                pe.sem_inc(pe_passed, 1)
                with pe.Fori(0, MLPG) as m:
                    mpj = pjb + m * PJ_MU + (PJ_M + 6)
                    q_stage(mpj, hf * WQ_H + m + (C0 + ATT * G1), 0)

                    def ready2(b):
                        if b == 0:
                            pe.wait_ge(pj_free, mpj + HPG + PJ)
                    out_stage(mpj, hf * WO_H + m + (1 + ATT * G1), HPG,
                              [q[:, 0:HPG, :] for q in (qo_hi, qo_lo)], ready2, pad=2)

        @block.scalar
        def _(act):
            def move(dst, src, ready, n, bias=None, mid=None):
                act.wait_ge(ready, n)
                if bias is None:
                    i = nc.scalar.activation(dst, src, ACT.Copy)
                else:
                    i = nc.scalar.activation(dst, src, ACT.Identity, bias=bias)
                if mid is not None:
                    i.then_inc(mid, 1)

            def ln_std(nn, which):
                act.wait_ge(ln_chain, nn * 9 + 8)
                nc.scalar.activation(std[0:L, :], mean_var[0:L, :, 1], ACT.Sqrt,
                                     bias=eps[0:L, which:which + 1]).then_inc(std_ready, 1)

            def ln_stage(nl):
                for b in range(HB):
                    act.wait_ge(ln_t, (nl * HB + b + 1) * 4)
                    nc.scalar.activation(h_hi[:, :, b * L:(b + 1) * L],
                                         tmp[1][:, 0:T].rearrange("p (c l) -> p c l", c=DC),
                                         ACT.Copy).then_inc(pj_mid, 1)

            act.wait_ge(setup_bv, 3)
            act.dma_start(bv_hi_dram, pt_hi[:].rearrange("p h n -> p (h n)")[0:8, 0:GW].bitcast(F32)).then_inc(setup_dma, 16)
            act.dma_start(bv_lo_dram, pt_lo[:].rearrange("p h n -> p (h n)")[0:8, 0:GW].bitcast(F32)).then_inc(setup_dma, 16)
            act.wait_ge(setup_dma, 80)
            act.sem_inc(out_done, 16)
            act.wait_ge(setup_pool, 2)
            for s in w_free.values():
                act.sem_inc(s, 1)

            with act.Fori(0, HALVES) as hf:
                pjb = hf * PJ_H
                act.wait_ge(out_done, hf * 16 + 16)
                act.dma_start(mask_v, mask[bass.ds(hf * HB, HB), :, :].rearrange("b p n -> p b n")).then_inc(mask_in, 16)
                for b in range(HB):
                    for s in range(SC):
                        unit = b * SC + s
                        move(v0[0][0:KC, unit, :], pj[unit % PJ][0:KC, 0:P], pj_ready, pjb + unit + 1,
                             mid=pj_mid)
                with act.Fori(0, C0) as c8:
                    cpj = pjb + c8 * PJ_CU + PJ_C
                    csc = hf * SC_H + c8 * SC_CU
                    ctp = hf * TP_H + c8 * TP_CU
                    co = hf * O_H + c8 * HB
                    cc = hf * C0 + c8

                    def keys0(b):
                        move(k_hi[:, 0, :], pj[K_UNIT[b] % PJ][:, 0:SK], pj_ready, cpj + K_UNIT[b] + 1,
                             bias=cur[:, 1:2], mid=pj_mid)
                        if b == HB - 1:
                            act.sem_inc(w_free["k"], 1)

                    def exps0(n):
                        b, j, h = n // HPC, n % HPC, n % 4
                        act.wait_ge(max_ready, csc + n + 1 + SCR)
                        nc.scalar.activation(probs[0:L, h, 0:S], probs[0:L, h, 0:S], ACT.Exp,
                                             bias=neg_max[0:L, j:j + 1], scale=-1.0,
                                             accum_out=row_sum[0:L, b % 2, j:j + 1]).then_inc(exp_ready, 1)

                    def out0(b):
                        n = tp_out_unit(b)
                        for k, dst in ((0, ot0[0]),):
                            act.wait_ge(tp_ready, ctp + n + 1)
                            nc.scalar.activation(dst[:, bass.ds(c8, 1), b * L:(b + 1) * L].rearrange("p c l -> p (c l)"),
                                                 tp[n % TP][:, 0:L], ACT.Identity,
                                                 bias=cur[:, 2:3]).then_inc(tp_mid, 1)

                    act.wait_ge(cur_ready, hf * WQ_H + c8 + 1)
                    act.wait_ge(pj_ready, cpj + 1)
                    act.sem_inc(w_free["q"], 1)
                    nc.scalar.activation(q0_f32, pj[0][:, 0:T], ACT.Identity, bias=cur[:, 0:1],
                                         scale=SCALE0).then_inc(q0_ready, 1)
                    keys0(0)
                    for n in range(3):
                        exps0(n)
                    for u in range(2 * HB):
                        for h in range(4):
                            n = tp_unit(u, h)
                            move(pt_hi[0:KC, h, :], tp[n % TP][0:KC, 0:SC * L], tp_ready, ctp + n + 1,
                                 mid=tp_mid)
                            if 4 * u + h + 3 < SC_CU:
                                exps0(4 * u + h + 3)
                        if u % 2 == 0 and u + 2 < 2 * HB:
                            keys0((u + 2) // 2)
                        if u % 2 == 0 and u >= 2:
                            out0(u // 2 - 1)
                        if u % 2 == 1:
                            b = u // 2
                            act.wait_ge(o_ready, co + b + 1)
                            nc.scalar.activation(o_nat[0:L, :, :],
                                                 o_ps[0:L, 0:256].rearrange("p (h e) -> p h e", e=32)[:, :, HD0:32],
                                                 ACT.Copy).then_inc(o_mid, 1)
                    out0(HB - 1)
                act.wait_ge(max_ready, hf * SC_H + SC_A + SCR)
                act.dma_start(xa[0:L, :, :], x[bass.ds(hf * T, T), :].rearrange("(b p) n -> p b n", p=L)).then_inc(x_in, 16)
                act.dma_start(probs_flat[0:L, :], rows_in[0:1, 0:3 * D].partition_broadcast(L)).then_inc(rows_ready, 16)
                ln_std(hf * 4, 0)

                with act.Fori(0, ATT) as a:
                    apj = pjb + a * PJ_AU + PJ_A
                    act.wait_ge(post_ln, hf * 12 + 12)
                    act.dma_start(tmp[2][0:L, :], rows_in[0:1, bass.ds((a + 3) * D, D)].partition_broadcast(L)).then_inc(rows_ready, 16)
                    ln_std(hf * 4 + a + 1, 1)
                    ln_stage(hf * NL + a)
                    with act.Fori(0, G1) as g:
                        ag = a * G1 + g
                        gpj = apj + g * PJ_GU + 6
                        gsc = hf * SC_H + ag * SC_GU + SC_A
                        gtp = hf * TP_H + ag * SC_GU + TP_A
                        go = hf * O_H + ag * HB + O_A
                        gg = hf * ATT * G1 + ag

                        def values1(b, s):
                            unit = HPG + b * (HPG + SC) + HPG + s
                            move(v1[0][0:KC, s, :], pj[unit % PJ][0:KC, :], pj_ready, gpj + unit + 1,
                                 mid=pj_mid)
                            if b == HB - 1 and s == SC - 1:
                                act.sem_inc(w_free["v"], 1)

                        def keys1(b, h):
                            unit = HPG + b * (HPG + SC) + h
                            move(k_hi[:, h, 0:S], pj[unit % PJ][:, 0:S], pj_ready, gpj + unit + 1,
                                 bias=cur[:, 4 + h:5 + h], mid=pj_mid)
                            if b == HB - 1 and h == HPG - 1:
                                act.sem_inc(w_free["k"], 1)

                        def exps1(b, h):
                            n = b * HPG + h
                            act.wait_ge(max_ready, gsc + n + 1 + SCR)
                            nc.scalar.activation(probs[0:L, h, 0:SK], scores[n % SCR][0:L, 0:SK], ACT.Exp,
                                                 bias=neg_max[0:L, h:h + 1],
                                                 accum_out=row_sum[0:L, 0, h:h + 1]).then_inc(exp_ready, 1)

                        def split_p(b, h):
                            n = b * HPG + h
                            move(pt_hi[0:KC + 1, h, :], tp[n % TP][0:KC + 1, 0:SC * L], tp_ready,
                                 gtp + n + 1, mid=tp_mid)

                        def out1(b):
                            act.wait_ge(o_ready, go + b + 1)
                            for h in range(HPG):
                                i = nc.scalar.activation(qo_hi[:, HPG + h, b * L:(b + 1) * L],
                                                         o_ps[:, h * L:(h + 1) * L], ACT.Identity,
                                                         bias=cur[:, 12 + h:13 + h])
                            i.then_inc(o_mid, 1)

                        act.wait_ge(cur_ready, hf * WQ_H + ag + C0 + 1)
                        act.wait_ge(o_ready, go)
                        act.dma_start(v1[0][KC:KC + 1, SC - 1, :].bitcast(F32), bv_hi_dram[bass.ds(ag, 1), :]).then_inc(bvrow_in, 16)
                        act.dma_start(v1[1][KC:KC + 1, SC - 1, :].bitcast(F32), bv_lo_dram[bass.ds(ag, 1), :]).then_inc(bvrow_in, 16)
                        for h in range(HPG):
                            if h == 3:
                                act.wait_ge(pj_free, gpj + 1 + PJ)
                            act.wait_ge(pj_ready, gpj + h + 1)
                            nc.scalar.activation(tmp[h % 3][:, 0:T], pj[h % PJ][:, 0:T], ACT.Identity,
                                                 bias=cur[:, h:h + 1], scale=SCALE1).then_inc(pj_mid, 1)
                        act.sem_inc(w_free["q"], 1)
                        for b in range(HB):
                            if b > 0:
                                split_p(b - 1, 0)
                                split_p(b - 1, 1)
                            keys1(b, 0)
                            if b > 0:
                                split_p(b - 1, 2)
                                split_p(b - 1, 3)
                            for h in range(1, HPG):
                                keys1(b, h)
                            if b > 0:
                                out1(b - 1)
                            values1(b, 0)
                            exps1(b, 0)
                            exps1(b, 1)
                            values1(b, 1)
                            exps1(b, 2)
                            exps1(b, 3)
                            values1(b, 2)
                        for h in range(HPG):
                            split_p(HB - 1, h)
                        out1(HB - 1)

                act.dma_start(tmp[2][0:L, :], rows_in[0:1, 5 * D:6 * D].partition_broadcast(L)).then_inc(rows_ready, 16)
                ln_std(hf * 4 + 3, 1)
                ln_stage(hf * NL + ATT)
                with act.Fori(0, MLPG) as m:
                    mpj = pjb + m * PJ_MU + (PJ_M + 6)
                    act.wait_ge(cur_ready, hf * WQ_H + m + (C0 + ATT * G1) + 1)
                    for h in range(HPG):
                        act.wait_ge(pj_free, mpj + h + 1)
                        act.wait_ge(pj_ready, mpj + h + 1)
                        nc.scalar.activation(tmp[h % 3][:, 0:T], pj[h % PJ][:, 0:T], ACT.Gelu,
                                             bias=cur[:, h:h + 1]).then_inc(pj_mid, 1)
                    act.sem_inc(w_free["q"], 1)
                act.wait_ge(pj_free, pjb + PJ_H + PJ)
                act.dma_start(out[bass.ds(hf * T, T), :].rearrange("(b p) n -> p b n", p=L), xa[0:L, :, :]).then_inc(out_done, 16)

        @block.vector
        def _(dve):
            def lo_of(dst, src, hi, mid, n, signal, k=1, bias=None):
                dve.wait_ge(mid, n)
                if bias is None:
                    i = nc.vector.tensor_tensor(dst, src, hi.bitcast(F32), ALU.subtract)
                else:
                    i = nc.vector.scalar_tensor_tensor(dst, src, bias, hi.bitcast(F32), ALU.add, ALU.subtract)
                i.then_inc(signal, k)

            def ln_stats(nn):
                for b in range(HB):
                    nc.vector.bn_stats(stats[0:L, b, :], xa[0:L, b, :]).then_inc(ln_chain, 1)
                for b in range(HB):
                    dve.wait_ge(ln_chain, nn * 9 + b + 1)
                    dve.sem_inc(dve_passed, 1)
                    nc.vector.bn_aggr(mean_var[0:L, b, :], stats[0:L, b, :]).then_inc(ln_chain, 1)
                dve.wait_ge(std_ready, nn + 1)
                nc.vector.reciprocal(rstd[0:L, :], std[0:L, :]).then_inc(ln_chain, 1)
                dve.wait_ge(ln_chain, nn * 9 + 9)

            def ln_stage(base, unit, nn, nl, mid0, par):
                nc.vector.tensor_copy(ln_cur[:], par).then_inc(ln_par, 1)
                ln_stats(nn)
                dve.wait_ge(ln_par, nl + 1)
                dve.wait_ge(rows_ready, nn * 16 + 16)

                def normed(b):
                    nc.vector.tensor_scalar(tmp[0][0:L, :], xa[0:L, b, :], mean_var[0:L, b, 0:1],
                                            rstd[0:L, b:b + 1], ALU.subtract, ALU.mult).then_inc(xn_ready, 1)
                    dve.wait_ge(xn_ready, nl * HB + b + 1)
                    nc.vector.tensor_tensor(xa[0:L, b, :], xa[0:L, b, :], tmp[2][0:L, :], ALU.add).then_inc(bias_added, 1)

                normed(0)
                for b in range(HB):
                    bank = pj[(unit + b) % PJ]
                    dve.wait_ge(pj_ready, base + unit + b + 1)
                    dve.wait_ge(pj_free, base + unit + b + PJ)
                    for c in range(DC):
                        nc.vector.tensor_scalar(tmp[1][:, c * L:(c + 1) * L], bank[:, c * L:(c + 1) * L],
                                                ln_cur[:, c:c + 1], ln_cur[:, 4 + c:5 + c],
                                                ALU.mult, ALU.add).then_inc(ln_t, 1)
                    if b + 1 < HB:
                        normed(b + 1)
                    lo_of(h_lo[:, :, b * L:(b + 1) * L], tmp[1][:, 0:T].rearrange("p (c l) -> p c l", c=DC),
                          h_hi[:, :, b * L:(b + 1) * L], pj_mid, mid0 + b + 1, pj_free,
                          3 if b == HB - 1 else 1)

            def out_stage(base, unit, pad=1):
                for b in range(HB):
                    dve.wait_ge(pj_ready, base + unit + b + 1)
                    if b == HB - 1:
                        dve.sem_inc(w_free["o"], 1)
                    nc.vector.tensor_tensor(xa[0:L, b, :], pj[(unit + b) % PJ][0:L, :], xa[0:L, b, :],
                                            ALU.add).then_inc(pj_free, pad if b == HB - 1 else 1)

            def q_stage(base, mid0, done0):
                for h in range(HPG):
                    dve.wait_ge(pj_mid, mid0 + h + 1)
                    nc.vector.tensor_copy(qo_hi[:, h, :], tmp[h % 3][:, 0:T]).then_inc(qh_done, 1)
                    lo_of(qo_lo[:, h, :], tmp[h % 3][:, 0:T], qo_hi[:, h, :], qh_done, done0 + h + 1, pj_free)

            dve.wait_ge(setup_pool, 2)
            dve.sem_inc(pj_free, PJ)
            dve.sem_inc(max_ready, SCR)
            dve.sem_inc(exp_ready, SCR)
            dve.sem_inc(tp_free, TP)
            dve.sem_inc(o_free, 1)
            dve.wait_ge(setup_dma, 48)
            q1 = prm[:, 0:PRM_LN].rearrange("p (j e) -> p j e", e=16)[:, :, 0:HPG]
            nc.vector.tensor_scalar(q1, q1, SCALE1, None, ALU.mult).then_inc(setup_dve, 1)
            q0 = prm[:, PRM_C:PRM_N].rearrange("p (c e) -> p c e", e=3)[:, :, 0]
            nc.vector.tensor_scalar(q0, q0, SCALE0, None, ALU.mult).then_inc(setup_dve, 1)
            rows8 = xa[0:ATT * G1, :, :]
            nc.vector.tensor_tensor(rows8[:, 2, :], rows8[:, 0, :], rows8[:, 1, :], ALU.subtract).then_inc(setup_bv, 1)
            dve.wait_ge(setup_bv, 1)
            row_hi = pt_hi[:].rearrange("p h n -> p (h n)")[0:8, 0:GW]
            row_lo = pt_lo[:].rearrange("p h n -> p (h n)")[0:8, 0:GW]
            nc.vector.tensor_copy(row_hi, rows8[:, 2, :]).then_inc(setup_bv, 1)
            dve.wait_ge(setup_bv, 2)
            nc.vector.tensor_tensor(row_lo, rows8[:, 2, :], row_hi.bitcast(F32), ALU.subtract).then_inc(setup_bv, 1)
            dve.wait_ge(setup_dve, 2)

            with dve.Fori(0, HALVES) as hf:
                pjb = hf * PJ_H
                midb = hf * MID_H
                dve.wait_ge(pj_free, pjb + PJ)
                nc.vector.memset(place_sel.bitcast(F32), 0.0).then_inc(sel_zero, 1)
                dve.wait_ge(sel_zero, hf + 1)
                for kv in range(KV2):
                    heads = ident[:, kv * 64:kv * 64 + 64].rearrange("p (j d) -> p j d", d=HD0)
                    for e in range(2):
                        for r in range(2):
                            at = 64 * kv + 32 * r + 16 * e
                            nc.vector.tensor_copy(place_sel[:, e, 4 * kv:4 * kv + 4, at:at + HD0], heads)
                for b in range(HB):
                    for s in range(SC):
                        unit = b * SC + s
                        lo_of(v0[1][0:KC, unit, :], pj[unit % PJ][0:KC, 0:P], v0[0][0:KC, unit, :],
                              pj_mid, midb + unit + 1, pj_free)
                with dve.Fori(0, C0) as c8:
                    cpj = pjb + c8 * PJ_CU + PJ_C
                    cmid = midb + c8 * MID_CU + MID_C
                    csc = hf * SC_H + c8 * SC_CU
                    ctp = hf * TP_H + c8 * TP_CU
                    co = hf * O_H + c8 * HB
                    cc = hf * C0 + c8
                    ob = hf * (C0 * HB) + c8 * HB

                    def keys0(b):
                        dve.wait_ge(pj_mid, cmid + b + 1)
                        for r in (32, 96):
                            rows = slice(r, r + 32)
                            i = nc.vector.scalar_tensor_tensor(
                                k_hi[rows, 0, :], pj[K_UNIT[b] % PJ][rows, 0:SK], cur[rows, 1:2],
                                k_hi[rows, 0, :].bitcast(F32), ALU.add, ALU.subtract)
                        i.then_inc(pj_free, 3 if b == HB - 1 else 1)

                    def placed(js):
                        for j in js:
                            unit = PLACED + j
                            dve.wait_ge(pj_ready, cpj + unit + 1)
                            nc.vector.tensor_copy(qo_hi[:, j, :], pj[unit % PJ][:, 0:T]).then_inc(pj_free, 1)

                    def max0(u, h):
                        b, j = u // 2, (u % 2) * 4 + h
                        dve.wait_ge(sc_ready, csc + 4 * u + h + 1)
                        dve.sem_inc(dve_passed, 1)
                        nc.vector.tensor_tensor_reduce(
                            probs[0:L, h, 0:S], scores[h % SCR][0:L, 0:S], mask_v[:, b, :], -1.0, 3.0e38,
                            ALU.add, ALU.min, neg_max[0:L, j:j + 1]).then_inc(max_ready, 1)

                    def out0(b):
                        n = tp_out_unit(b)
                        dst = [o[:, bass.ds(c8, 1), b * L:(b + 1) * L].rearrange("p c l -> p (c l)") for o in ot0]
                        lo_of(dst[1], tp[n % TP][:, 0:L], dst[0], tp_mid, ctp + n + 1, tp_free,
                              bias=cur[:, 2:3])

                    dve.wait_ge(pj_ready, cpj + 1)
                    dve.wait_ge(pj_free, cpj + PJ)
                    dve.wait_ge(tp_free, ctp + TP)
                    nc.vector.tensor_copy(cur[:, 0:3], prm[:, bass.ds(c8 * 3 + PRM_C, 3)]).then_inc(cur_ready, 1)
                    dve.wait_ge(q0_ready, cc + 1)
                    nc.vector.tensor_copy(q0_split[0], q0_f32).then_inc(q0_hi, 1)
                    lo_of(q0_split[1], q0_f32, q0_split[0], q0_hi, cc + 1, pj_free)
                    dve.wait_ge(cur_ready, hf * WQ_H + c8 + 1)
                    keys0(0)
                    placed(range(4))
                    dve.wait_ge(mask_in, hf * 16 + 16)
                    for h in range(4):
                        max0(0, h)
                    placed(range(4, 8))
                    for e, v in enumerate(v0):
                        nc.vector.tensor_copy(
                            v0c[0:KC, :, :, e * HD0:(e + 1) * HD0],
                            v[0:KC, :, bass.ds(c8 * (KV2 * HD0), KV2 * HD0)].bitcast(F32).rearrange(
                                "p n (k d) -> p n k d", d=HD0)).then_inc(v0c_ready, 1)
                    for u in range(2 * HB):
                        b = u // 2
                        for h in range(4):
                            n = tp_unit(u, h)
                            if u + 1 < 2 * HB:
                                max0(u + 1, h)
                            lo_of(pt_lo[0:KC, h, :], tp[n % TP][0:KC, 0:SC * L], pt_hi[0:KC, h, :],
                                  tp_mid, ctp + n + 1, tp_free)
                        if u % 2 == 0 and u + 2 < 2 * HB:
                            keys0((u + 2) // 2)
                        if u % 2 == 0 and u >= 2:
                            out0(u // 2 - 1)
                        if u % 2 == 1:
                            dve.wait_ge(exp_ready, csc + 4 * u + 4 + SCR)
                            nc.vector.reciprocal(inv_sum[0:L, :], row_sum[0:L, b % 2, :]).then_inc(o_inv, 1)
                            dve.wait_ge(o_mid, co + b + 1)
                            o_hi = o_ps[0:L, 0:256].rearrange("p (h e) -> p h e", e=32)[:, :, 0:HD0]
                            nc.vector.tensor_tensor(o_nat[0:L], o_hi, o_nat[0:L], ALU.add).then_inc(o_free, 1)
                            dve.wait_ge(o_inv, ob + b + 1)
                            dve.wait_ge(o_free, co + b + 2)
                            nc.vector.tensor_tensor(o_nat[0:L], o_nat[0:L],
                                                    inv_sum[0:L, :].unsqueeze(2).broadcast_to([L, HPC, HD0]),
                                                    ALU.mult).then_inc(o_nat_ready, 1)
                    out0(HB - 1)

                dve.wait_ge(x_in, hf * 16 + 16)
                dve.wait_ge(rows_ready, hf * 64 + 16)
                for b in range(HB):
                    nc.vector.tensor_tensor(xa[0:L, b, :], xa[0:L, b, :], tmp[0][0:L, :], ALU.add).then_inc(bias_added, 1)
                dve.wait_ge(bias_added, hf * 16 + 4)
                out_stage(pjb + PJ_W0, 0, pad=3)
                dve.sem_inc(w_free["v"], 1)
                dve.wait_ge(pj_free, pjb + PJ_A + PJ)
                ln_stats(hf * 4)
                for b in range(HB):
                    nc.vector.tensor_scalar(xa[0:L, b, :], xa[0:L, b, :], mean_var[0:L, b, 0:1],
                                            rstd[0:L, b:b + 1], ALU.subtract, ALU.mult).then_inc(post_ln, 1)
                for k, op in ((1, ALU.mult), (2, ALU.add)):
                    for b in range(HB):
                        dve.wait_ge(post_ln, hf * 12 + 4 * (k - 1) + b + 1)
                        nc.vector.tensor_tensor(xa[0:L, b, :], xa[0:L, b, :], tmp[k][0:L, :], op).then_inc(post_ln, 1)
                dve.wait_ge(post_ln, hf * 12 + 12)
                dve.sem_inc(dve_passed, 1)

                with dve.Fori(0, ATT) as a:
                    apj = pjb + a * PJ_AU + PJ_A
                    amid = midb + a * MID_AU + MID_A
                    dve.wait_ge(pj_free, apj + PJ)
                    ln_stage(apj, 0, hf * 4 + a + 1, hf * NL + a, amid,
                             prm[:, bass.ds(a * 8 + PRM_LN, 8)])
                    with dve.Fori(0, G1) as g:
                        ag = a * G1 + g
                        gpj = apj + g * PJ_GU + 6
                        gmid = amid + g * MID_GU + HB
                        gsc = hf * SC_H + ag * SC_GU + SC_A
                        gtp = hf * TP_H + ag * SC_GU + TP_A
                        go = hf * O_H + ag * HB + O_A
                        gg = (hf * ATT * G1 + ag) * SC_GU

                        def keys1(b, h):
                            unit = HPG + b * (HPG + SC) + h
                            lo_of(k_lo[:, h, 0:S], pj[unit % PJ][:, 0:S], k_hi[:, h, 0:S], pj_mid,
                                  gmid + unit + 1, pj_free, bias=cur[:, 4 + h:5 + h])

                        def values1(b, s):
                            unit = HPG + b * (HPG + SC) + HPG + s
                            lo_of(v1[1][0:KC, s, :], pj[unit % PJ][0:KC, :], v1[0][0:KC, s, :], pj_mid,
                                  gmid + unit + 1, pj_free)

                        def max1(b, h):
                            n = b * HPG + h
                            dve.wait_ge(sc_ready, gsc + n + 1)
                            nc.vector.tensor_reduce(neg_max[0:L, h:h + 1], scores[n % SCR][0:L, 0:SK], AX_X,
                                                    ALU.max, negate=True).then_inc(max_ready, 1)

                        def norm1(b, h):
                            n = b * HPG + h
                            dve.wait_ge(exp_ready, gsc + n + 1 + SCR)
                            nc.vector.reciprocal(inv_sum[0:L, h:h + 1], row_sum[0:L, 0, h:h + 1]).then_inc(inv_ready, 1)
                            dve.wait_ge(inv_ready, gg + n + 1)
                            nc.vector.tensor_scalar(probs[0:L, h, 0:SK], probs[0:L, h, 0:SK],
                                                    inv_sum[0:L, h:h + 1], None, ALU.mult).then_inc(norm_ready, 1)

                        def split_p(b, h):
                            n = b * HPG + h
                            lo_of(pt_lo[0:KC + 1, h, :], tp[n % TP][0:KC + 1, 0:SC * L],
                                  pt_hi[0:KC + 1, h, :], tp_mid, gtp + n + 1, tp_free)

                        def out1(b):
                            dve.wait_ge(o_mid, go + b + 1)
                            for h in range(HPG):
                                cols = slice(b * L, (b + 1) * L)
                                i = nc.vector.scalar_tensor_tensor(
                                    qo_lo[:, HPG + h, cols], o_ps[:, h * L:(h + 1) * L], cur[:, 12 + h:13 + h],
                                    qo_hi[:, HPG + h, cols].bitcast(F32), ALU.add, ALU.subtract)
                            i.then_inc(o_free, 1)

                        dve.wait_ge(pj_ready, gpj + 1)
                        dve.wait_ge(o_free, go + 1)
                        nc.vector.tensor_copy(cur[:], prm[:, bass.ds(ag * 16, 16)]).then_inc(cur_ready, 1)
                        dve.wait_ge(cur_ready, hf * WQ_H + ag + C0 + 1)
                        kb = cur[:, 8:12].unsqueeze(2)
                        nc.vector.tensor_copy(k_hi[:, :, S:SK], kb).then_inc(kbias_hi, 1)
                        dve.wait_ge(kbias_hi, hf * ATT * G1 + ag + 1)
                        nc.vector.tensor_tensor(k_lo[:, :, S:SK], kb, k_hi[:, :, S:SK].bitcast(F32), ALU.subtract)
                        q_stage(gpj, gmid, (hf * (ATT * G1 + MLPG) + ag) * HPG)
                        for b in range(HB):
                            if b > 0:
                                split_p(b - 1, 0)
                                split_p(b - 1, 1)
                            keys1(b, 0)
                            if b > 0:
                                split_p(b - 1, 2)
                                split_p(b - 1, 3)
                            for h in range(1, HPG):
                                keys1(b, h)
                            if b > 0:
                                out1(b - 1)
                            values1(b, 0)
                            max1(b, 0)
                            max1(b, 1)
                            norm1(b, 0)
                            norm1(b, 1)
                            values1(b, 1)
                            max1(b, 2)
                            max1(b, 3)
                            norm1(b, 2)
                            norm1(b, 3)
                            values1(b, 2)
                        for h in range(HPG):
                            split_p(HB - 1, h)
                        out1(HB - 1)
                        out_stage(gpj, PJ_GU - HB)

                mlp = pjb + PJ_M
                dve.wait_ge(pj_free, mlp + PJ)
                ln_stage(mlp, 0, hf * 4 + 3, hf * NL + ATT, midb + MID_M, prm[:, PRM_LN + 16:PRM_LN + 24])
                with dve.Fori(0, MLPG) as m:
                    mpj = pjb + m * PJ_MU + (PJ_M + 6)
                    dve.wait_ge(pj_ready, mpj + 1)
                    dve.wait_ge(o_free, hf * O_H + O_H + 1)
                    nc.vector.tensor_copy(cur[:, 0:HPG], prm[:, bass.ds(m * HPG + PRM_B1, HPG)]).then_inc(cur_ready, 1)
                    q_stage(mpj, midb + m * HPG + (MID_M + HB), (hf * (ATT * G1 + MLPG) + m + ATT * G1) * HPG)
                    out_stage(mpj, HPG, pad=2)


def kernel(**inputs):
    import numpy as np
    import concourse.bacc as bacc
    from concourse.bass_utils import run_bass_kernel_spmd

    i = {k: np.asarray(v) for k, v in inputs.items()}
    L0, L1 = "L0_xattn_", "L1_xattn_"
    tokens = i["x"].reshape(B * L, D)

    def columns(v, n):
        return v.reshape(n, P).T

    def both(name):
        return np.stack([i[f"{L1}{name}1"], i[f"{L1}{name}2"]])

    def rep_kv(a):
        s = a.shape[:-1]
        return np.repeat(a.reshape(*s, 8, 1, HD0), 4, axis=-2).reshape(*s, D)

    heads = [both(n).reshape(ATT * G1, HPG, P) for n in ("bq", "bk", "bias_k", "bv")]
    per_group = np.stack(heads, axis=1).reshape(ATT * G1 * 16, P).T
    norms = [columns(i[L1 + n], DC) for n in
             ("ln1_scale", "ln1_offset", "ln2_scale", "ln2_offset", "ln_mlp_scale", "ln_mlp_offset")]
    per_chunk = np.stack([i[L0 + "bq"].reshape(C0, P), rep_kv(i[L0 + "bk"]).reshape(C0, P),
                          rep_kv(i[L0 + "bv"]).reshape(C0, P)], axis=1).reshape(C0 * 3, P).T
    prm = np.concatenate([per_group, *norms, columns(i[L1 + "b_fc1"], 16), per_chunk], axis=1)
    rows = np.concatenate([i[L0 + "bo"], i[L0 + "gamma"], i[L0 + "beta"], i[L1 + "bo1"], i[L1 + "bo2"],
                           i[L1 + "b_fc2"]]).reshape(1, 6 * D)
    arrays = {
        "x": tokens, "x_t": tokens.T, "ctx_t": i["ctx_2048"].transpose(2, 0, 1),
        "mask": i["mask_Bx1xSxS2_ff0"].reshape(B, L, S),
        "wq0": i[L0 + "Wq"], "wk0": rep_kv(i[L0 + "Wk"]), "wv0": i[L0 + "Wv"], "wo0": i[L0 + "Wo"],
        "wq": both("wq").reshape(ATT * D, NH1 * HD1), "wk": both("wk").reshape(ATT * D, NH1 * HD1),
        "wv": both("wv").reshape(ATT * D, NH1 * HD1), "wo": both("wo").reshape(ATT * NH1 * HD1, D),
        "w1": i[L1 + "w_fc1"], "w2": i[L1 + "w_fc2"],
        "bias_v": both("bias_v").reshape(ATT * G1, GW), "bv": both("bv").reshape(ATT * G1, GW),
        "prm": prm, "rows": rows,
    }
    nc = bacc.Bacc("TRN2", target_bir_lowering=False, num_devices=1)
    sent, args = {}, []
    for name, a in arrays.items():
        sent[f"in_{name}"] = np.ascontiguousarray(a)
        args.append(nc.dram_tensor(f"in_{name}", a.shape, mybir.dt.float32, kind="ExternalInput").ap())
    args.append(nc.dram_tensor("out", (B * L, D), mybir.dt.float32, kind="ExternalOutput").ap())
    xattn_program(nc, *args)
    r = run_bass_kernel_spmd(nc, [sent], core_ids=[0])
    return r.results[0]["out"].reshape(B, L, D)
```

```python
from contextlib import ExitStack

import concourse.bass as bass
from concourse import mybir

F32 = mybir.dt.float32
F32R = mybir.dt.float32r
ALU = mybir.AluOpType
ACT = mybir.ActivationFunctionType
AX_X = mybir.AxisListType.X

P = 128
B, L, S, D = 8, 112, 375, 512
HALVES = 2
HB = B // HALVES
T = HB * L
DC = D // P
SC = 3
KC = S // SC
SK = S + 1
NH0, HD0 = 32, 16
C0 = 4
HPC = NH0 // C0
KV2 = 2
ATT = 2
NH1, HD1 = 16, 128
G1 = 4
HPG = NH1 // G1
GW = HPG * HD1
MLPG = 4
SCALE0 = 0.25
SCALE1 = float(HD1) ** -0.5
EPS0, EPS1 = 1e-6, 1e-5

PJ, SCR, TP = 3, 2, 2

PJ_C = HB * SC
PJ_CU = 15
PJ_W0 = PJ_C + C0 * PJ_CU
PJ_A = PJ_W0 + 6
PJ_GU = HPG + HB * (HPG + SC) + HB
PJ_AU = 6 + G1 * PJ_GU
PJ_M = PJ_A + ATT * PJ_AU
PJ_MU = 9
PJ_H = PJ_M + 6 + MLPG * PJ_MU

MID_C = HB * SC
MID_CU = HB + HPC // 2
MID_A = MID_C + C0 * MID_CU
MID_GU = HPG + HB * (HPG + SC)
MID_AU = HB + G1 * MID_GU
MID_M = MID_A + ATT * MID_AU
MID_H = MID_M + HB + MLPG * HPG

K_UNIT = (1, 10, 11, 12)
PLACED = 2
SC_CU, SC_GU = HB * HPC, HB * HPG
SC_A = C0 * SC_CU
SC_H = SC_A + ATT * G1 * SC_GU
TP_CU = HB * HPC + 2 * HB + HB
TP_A = C0 * TP_CU
TP_H = TP_A + ATT * G1 * SC_GU
TM_CU = TP_CU - 2 * HB
TM_A = C0 * TM_CU
TM_H = TM_A + ATT * G1 * SC_GU
O_CU = 2 * HB
O_A = C0 * O_CU
O_H = O_A + ATT * G1 * HB

WQ_H = C0 + ATT * G1 + MLPG
WK_H = C0 + ATT * G1
WV_H = 1 + ATT * G1
WO_H = 1 + ATT * G1 + MLPG
RAW_X = 2 + HB * DC
RAW_C = RAW_X + DC
RAW_W0 = RAW_C + 2 * C0
RAW_A = RAW_W0 + DC
RAW_GU = 4 * DC
RAW_M = RAW_A + ATT * G1 * RAW_GU
RAW_H = RAW_M + MLPG * 2 * DC
assert PJ_H % PJ == 0 and PJ_A % PJ == 0 and PJ_GU % PJ == 0 and PJ_MU % PJ == 0
assert RAW_C % 2 == 0 and RAW_W0 % 2 == 0

PRM_LN = ATT * G1 * 16
PRM_B1 = PRM_LN + 3 * 8
PRM_C = PRM_B1 + 16
PRM_N = PRM_C + C0 * 3
NL = ATT + 1


TP_ORDER = []
for n in range(HB * HPC):
    TP_ORDER.append(("probs", n))
    if n >= 9 and n % 4 == 1:
        TP_ORDER.append(("four", (n - 9) // 4))
    if n >= 15 and n % HPC == 7:
        TP_ORDER.append(("batch", (n - 15) // HPC))
TP_ORDER += [("four", 2 * HB - 2), ("four", 2 * HB - 1), ("batch", HB - 1)]
assert len(TP_ORDER) == TP_CU


def tp_unit(what, i):
    return TP_ORDER.index((what, i))


def tp_mid_unit(what, i):
    unit = tp_unit(what, i)
    return unit - sum(w == "four" for w, _ in TP_ORDER[:unit])


def mid_keys(b):
    return 0 if b == 0 else HPC // 2 + b


def xattn_program(nc, x, x_t, ctx_t, mask, wq0, wk0, wv0, wo0, wq, wk, wv, wo, w1, w2,
                  bias_v, bv, prm_in, rows_in, out):
    bv_hi_dram = nc.dram_tensor("bv_hi_scratch", (ATT * G1, GW), F32, kind="Internal").ap()
    bv_lo_dram = nc.dram_tensor("bv_lo_scratch", (ATT * G1, GW), F32, kind="Internal").ap()

    with ExitStack() as ctx:
        def sb(name, shape, dt=F32):
            return ctx.enter_context(nc.sbuf_tensor(name, shape, dt))

        def sem(name):
            return ctx.enter_context(nc.semaphore(name))

        ctx_hi = sb("ctx_hi", [P, DC, HB, SK], F32R)
        ctx_lo = sb("ctx_lo", [P, DC, HB, SK], F32R)
        h_hi = sb("h_hi", [P, DC, T], F32R)
        h_lo = sb("h_lo", [P, DC, T], F32R)
        qo_hi = sb("qo_hi", [P, 2 * HPG, T], F32R)
        qo_lo = sb("qo_lo", [P, 2 * HPG, T], F32R)
        k_hi = sb("k_hi", [P, HPG, SK], F32R)
        k_lo = sb("k_lo", [P, HPG, SK], F32R)
        v_hi = sb("v_hi", [P, SC * GW], F32R)
        v_lo = sb("v_lo", [P, SC * GW], F32R)
        probs = sb("probs", [P, HPG, 384])
        pt_hi = sb("pt_hi", [P, HPG, SC * L], F32R)
        pt_lo = sb("pt_lo", [P, HPG, SC * L], F32R)
        w_hi = {n: sb(f"w{n}_hi", [P, DC, GW], F32R) for n in "qkvo"}
        w_lo = {n: sb(f"w{n}_lo", [P, DC, GW], F32R) for n in "qkvo"}
        raw = sb("raw", [P, 2, GW])
        xacc = sb("xacc", [P, HB * D])
        ident = sb("ident", [P, P])
        o_nat = sb("o_nat", [P, HPC, HD0])
        prm = sb("prm", [P, PRM_N])
        cur = sb("cur", [P, 16])
        ln_cur = sb("ln_cur", [P, 8])
        neg_max = sb("neg_max", [P, HPC])
        row_sum = sb("row_sum", [P, 2, HPC])
        inv_sum = sb("inv_sum", [P, HPC])
        stats = sb("stats", [P, HB, 6])
        mean_var = sb("mean_var", [P, HB, 2])
        std = sb("std", [P, HB])
        rstd = sb("rstd", [P, HB])
        eps = sb("eps", [P, 2])

        probs_flat = probs[:].rearrange("p h n -> p (h n)")
        tmp = [probs_flat[:, 512 * i:512 * i + 512] for i in range(3)]
        xa = xacc[:].rearrange("p (b n) -> p b n", b=HB)
        mask_v = xacc[0:L, 0:HB * S].rearrange("p (b n) -> p b n", b=HB)
        q0_f32 = xacc[:, 1536:1536 + T]
        q0_split = [qo_lo[:, e, :] for e in range(2)]
        place_sel = qo_lo[:].rearrange("p h n -> p (h n)")[:, 2 * T:2 * T + 2 * HPC * P].rearrange(
            "p (e j m) -> p e j m", e=2, j=HPC)
        o_t = q0_f32[0:32, :]
        pt0 = [[pt_hi[:], pt_lo[:]],
               [w["k"][:].rearrange("p c n -> p (c n)")[:, 512:512 + 4 * SC * L].rearrange(
                   "p (h n) -> p h n", h=4) for w in (w_hi, w_lo)]]
        k0 = [k_hi[:, 0, :], k_lo[:, 0, :]]
        v0 = [v[:].rearrange("p (n d) -> p n d", d=P) for v in (v_hi, v_lo)]
        v1 = [v[:].rearrange("p (c n) -> p c n", c=SC) for v in (v_hi, v_lo)]
        v0c = k_hi[:].rearrange("p h n -> p (h n)")[:, SK:SK + 768].rearrange(
            "p (n k e) -> p n k e", k=KV2, e=2 * HD0)
        wv_flat = [w["v"][:].rearrange("p c n -> p (c n)") for w in (w_hi, w_lo)]
        ot0 = [w[:, 0:C0 * T].rearrange("p (c t) -> p c t", c=C0) for w in wv_flat]
        flat = {n: [w[n][:].rearrange("p c n -> p (c n)") for w in (w_hi, w_lo)] for n in "qkvo"}

        pj = [ctx.enter_context(nc.psum_tensor(f"pj{i}", [P, 512], F32)) for i in range(PJ)]
        scores = [ctx.enter_context(nc.psum_tensor(f"scores{i}", [P, 512], F32)) for i in range(SCR)]
        tp = [ctx.enter_context(nc.psum_tensor(f"tp{i}", [P, 512], F32)) for i in range(TP)]
        o_ps = ctx.enter_context(nc.psum_tensor("o_ps", [P, 512], F32))

        pj_ready, pj_mid, pj_free = sem("pj_ready"), sem("pj_mid"), sem("pj_free")
        sc_ready = sem("sc_ready")
        tp_ready, tp_mid, tp_free = sem("tp_ready"), sem("tp_mid"), sem("tp_free")
        o_ready, o_mid, o_free = sem("o_ready"), sem("o_mid"), sem("o_free")
        max_ready, exp_ready = sem("max_ready"), sem("exp_ready")
        inv_ready, norm_ready = sem("inv_ready"), sem("norm_ready")
        raw_ready = [sem("raw_ready0"), sem("raw_ready1")]
        raw_free = [sem("raw_free0"), sem("raw_free1")]
        split_hi = sem("split_hi")
        w_ready = {n: sem(f"w{n}_ready") for n in "qkvo"}
        w_free = {n: sem(f"w{n}_free") for n in "qkvo"}
        tok_ready, ctx_ready = sem("tok_ready"), sem("ctx_ready")
        cur_ready, q0_hi, sel_zero = sem("cur_ready"), sem("q0_hi"), sem("sel_zero")
        q0_ready, v0c_ready, kbias_hi = sem("q0_ready"), sem("v0c_ready"), sem("kbias_hi")
        o_inv, o_nat_ready = sem("o_inv"), sem("o_nat_ready")
        qh_done = sem("qh_done")
        ln_chain, std_ready, xn_ready, ln_t, ln_par = (
            sem("ln_chain"), sem("std_ready"), sem("xn_ready"), sem("ln_t"), sem("ln_par"))
        post_ln, bias_added = sem("post_ln"), sem("bias_added")
        mask_in, x_in, rows_ready, bvrow_in, out_done = (
            sem("mask_in"), sem("x_in"), sem("rows_ready"), sem("bvrow_in"), sem("out_done"))
        setup_dma, setup_dve, setup_pool, setup_bv = (
            sem("setup_dma"), sem("setup_dve"), sem("setup_pool"), sem("setup_bv"))

        pool_passed, dve_passed, pe_passed = sem("pool_passed"), sem("dve_passed"), sem("pe_passed")

        block = ctx.enter_context(nc.Block())

        @block.sync
        def _(sp):
            sp.dma_start(prm[:], prm_in).then_inc(setup_dma, 16)
            sp.dma_start(xa[0:ATT * G1, 0, :], bias_v).then_inc(setup_dma, 16)
            sp.dma_start(xa[0:ATT * G1, 1, :], bv).then_inc(setup_dma, 16)

            def load(half_use, n, src, shape):
                slot = n % 2
                dst = raw[:, slot, 0:shape[0] * shape[1]]
                if shape[0] > 1:
                    dst = dst.rearrange("p (c n) -> p c n", c=shape[0])
                sp.wait_ge(raw_free[slot], half_use + n // 2 + 1)
                sp.dma_start(dst, src).then_inc(raw_ready[slot], 16)

            with sp.Fori(0, HALVES) as hf:
                base = hf * (RAW_H // 2)
                for i in range(2):
                    load(base, i, wv0[2 * i * P:(2 * i + 2) * P, :].rearrange(
                        "(c p) n -> p c n", p=P), (2, P))
                for b in range(HB):
                    for c in range(DC):
                        load(base, 2 + b * DC + c,
                             ctx_t[c * P:(c + 1) * P, bass.ds(hf * HB + b, 1), :].rearrange(
                                 "p b n -> p (b n)"), (1, S))
                for c in range(DC):
                    load(base, RAW_X + c, x_t[c * P:(c + 1) * P, bass.ds(hf * T, T)], (1, T))
                with sp.Fori(0, C0) as c:
                    cb = base + RAW_C // 2 + c
                    load(cb, 0, wq0[:, bass.ds(c * P, P)].rearrange("(c p) n -> p c n", p=P), (DC, P))
                    load(cb, 1, wk0[:, bass.ds(c * P, P)].rearrange("(c p) n -> p c n", p=P), (DC, P))
                for c in range(DC):
                    load(base, RAW_W0 + c, wo0[c * P:(c + 1) * P, :], (1, GW))
                with sp.Fori(0, ATT) as a:
                    with sp.Fori(0, G1) as g:
                        gb = base + RAW_A // 2 + (a * G1 + g) * (RAW_GU // 2)
                        for i, w in enumerate((wq, wk, wv)):
                            for c in range(DC):
                                load(gb, DC * i + c,
                                     w[bass.ds(a * D + c * P, P), bass.ds(g * GW, GW)], (1, GW))
                        for c in range(DC):
                            load(gb, 3 * DC + c,
                                 wo[bass.ds((a * G1 + g) * GW + c * P, P), :], (1, GW))
                with sp.Fori(0, MLPG) as m:
                    mb = base + RAW_M // 2 + m * DC
                    for c in range(DC):
                        load(mb, c, w1[c * P:(c + 1) * P, bass.ds(m * GW, GW)], (1, GW))
                    for c in range(DC):
                        load(mb, DC + c, w2[bass.ds(m * GW + c * P, P), :], (1, GW))
            sp.wait_ge(out_done, 16 * (HALVES + 1))

        @block.gpsimd
        def _(pool):
            nc.gpsimd.memset(ident[:], 0.0).then_inc(setup_pool, 1)
            nc.gpsimd.memset(eps[:, 0:1], EPS0)
            nc.gpsimd.memset(eps[:, 1:2], EPS1)
            nc.gpsimd.memset(ctx_hi[:, :, :, S:SK].bitcast(F32), 0.0)
            nc.gpsimd.memset(ctx_lo[:, :, :, S:SK].bitcast(F32), 0.0)
            pool.wait_ge(setup_pool, 1)
            nc.gpsimd.affine_select(out=ident[:], in_=ident[:], compare_op=ALU.not_equal, fill=1.0,
                                    base=0, pattern=[[-1, P]], channel_multiplier=1).then_inc(setup_pool, 1)
            for s in raw_free:
                pool.sem_inc(s, 1)

            def split(half_base, n, shape, hi, lo, signal, k):
                slot = n % 2
                src = raw[:, slot, 0:shape[0] * shape[1]]
                if shape[0] > 1:
                    src = src.rearrange("p (c n) -> p c n", c=shape[0])
                pool.wait_ge(raw_ready[slot], (half_base + (n // 2 + 1)) * 16)
                pool.sem_inc(pool_passed, 1)
                nc.gpsimd.tensor_scalar(hi, src, 1.0, 0.0, ALU.mult, ALU.add).then_inc(split_hi, 1)
                pool.wait_ge(split_hi, half_base * 2 + n + 1)
                nc.gpsimd.tensor_tensor(lo, src, hi.bitcast(F32), ALU.subtract).then_inc(signal, k)
                return slot

            def split_free(half_base, n, shape, hi, lo, signal, k, done):
                slot = split(half_base, n, shape, hi, lo, signal, k)
                pool.wait_ge(signal, done)
                pool.sem_inc(raw_free[slot], 1)

            def weights(half_base, n0, name, use, pieces=DC):
                pool.wait_ge(w_free[name], use + 1)
                for c in range(pieces):
                    if pieces == DC:
                        hi, lo, shape = w_hi[name][:, c, :], w_lo[name][:, c, :], (1, GW)
                    else:
                        wd = DC // pieces * P
                        hi, lo = (f[:, wd * c:wd * c + wd].rearrange("p (c n) -> p c n", n=P)
                                  for f in flat[name])
                        shape = (DC // pieces, P)
                    k = DC // pieces
                    split_free(half_base, n0 + c, shape, hi, lo, w_ready[name], k,
                               use * DC + k * (c + 1))

            with pool.Fori(0, HALVES) as hf:
                base = hf * (RAW_H // 2)
                pool.wait_ge(pj_free, hf * PJ_H + PJ)
                weights(base, 0, "v", hf * WV_H, pieces=2)
                for b in range(HB):
                    for c in range(DC):
                        split_free(base, 2 + b * DC + c, (1, S), ctx_hi[:, c, b, 0:S],
                                   ctx_lo[:, c, b, 0:S], ctx_ready, 1,
                                   hf * (HB * DC) + b * DC + c + 1)
                for c in range(DC):
                    split_free(base, RAW_X + c, (1, T), h_hi[:, c, :], h_lo[:, c, :], tok_ready, 1,
                               hf * DC + c + 1)
                with pool.Fori(0, C0) as c:
                    weights(base + RAW_C // 2 + c, 0, "q", hf * WQ_H + c, pieces=1)
                    weights(base + RAW_C // 2 + c, 1, "k", hf * WK_H + c, pieces=1)
                weights(base, RAW_W0, "o", hf * WO_H)
                with pool.Fori(0, ATT) as a:
                    with pool.Fori(0, G1) as g:
                        gb = base + RAW_A // 2 + (a * G1 + g) * (RAW_GU // 2)
                        weights(gb, 0, "q", hf * WQ_H + C0 + a * G1 + g)
                        weights(gb, DC, "k", hf * WK_H + C0 + a * G1 + g)
                        weights(gb, 2 * DC, "v", hf * WV_H + 1 + a * G1 + g)
                        weights(gb, 3 * DC, "o", hf * WO_H + 1 + a * G1 + g)
                with pool.Fori(0, MLPG) as m:
                    mb = base + RAW_M // 2 + m * DC
                    weights(mb, 0, "q", hf * WQ_H + C0 + ATT * G1 + m)
                    weights(mb, DC, "o", hf * WO_H + 1 + ATT * G1 + m)

        @block.tensor
        def _(pe):
            def three(dst, lhs, rhs, first, last):
                (l_hi, l_lo), (r_hi, r_lo) = lhs, rhs
                nc.tensor.matmul(dst, l_hi, r_hi, start=first, stop=False)
                nc.tensor.matmul(dst, l_hi, r_lo, start=False, stop=False)
                return nc.tensor.matmul(dst, l_lo, r_hi, start=False, stop=last)

            def transpose(dst, src, parts):
                return nc.tensor.transpose(dst, src, ident[0:parts, 0:parts])

            def q_stage(base, use, unit, width=GW):
                for h in range(width // P):
                    pe.wait_ge(pj_free, base + unit + h + 1)
                    for c in range(DC):
                        if h == 0:
                            pe.wait_ge(w_ready["q"], use * DC + (c + 1 if width == GW else DC))
                        lhs = ([w["q"][:, c, h * P:(h + 1) * P] for w in (w_hi, w_lo)] if width == GW
                               else [f[:, c * P:(c + 1) * P] for f in flat["q"]])
                        last = three(pj[(unit + h) % PJ][:, 0:T], lhs,
                                     (h_hi[:, c, :], h_lo[:, c, :]), c == 0, c == DC - 1)
                    last.then_inc(pj_ready, 1)

            def out_stage(base, use, unit, src, ready, pad=1):
                for b in range(HB):
                    ready(b)
                    pe.wait_ge(pj_free, base + unit + b + 1)
                    for h in range(HPG):
                        if b == 0:
                            pe.wait_ge(w_ready["o"], use * DC + h + 1)
                        last = three(pj[(unit + b) % PJ][0:L, :],
                                     [s[:, h, b * L:(b + 1) * L] for s in src],
                                     (w_hi["o"][:, h, :], w_lo["o"][:, h, :]), h == 0, h == HPG - 1)
                    last.then_inc(pj_ready, pad if b == HB - 1 else 1)

            def ln_stage(base, unit, nl):
                for b in range(HB):
                    pe.wait_ge(xn_ready, nl * HB + b + 1)
                    pe.wait_ge(pj_free, base + unit + b + 1)
                    for c in range(DC):
                        last = transpose(pj[(unit + b) % PJ][:, c * L:(c + 1) * L],
                                         tmp[0][0:L, c * P:(c + 1) * P], L)
                    last.then_inc(pj_ready, 3 if b == HB - 1 else 1)

            pe.wait_ge(setup_dve, 1)
            with pe.Fori(0, HALVES) as hf:
                pjb = hf * PJ_H
                for b in range(HB):
                    pe.wait_ge(ctx_ready, hf * (HB * DC) + (b + 1) * DC)
                    for s in range(SC):
                        unit = b * SC + s
                        pe.wait_ge(pj_free, pjb + unit + 1)
                        if unit == 0:
                            pe.wait_ge(w_ready["v"], hf * WV_H * DC + DC)
                        for c in range(DC):
                            last = three(pj[unit % PJ][0:KC, 0:P],
                                         [t[:, c, b, s * KC:(s + 1) * KC] for t in (ctx_hi, ctx_lo)],
                                         [f[:, c * P:(c + 1) * P] for f in flat["v"]],
                                         c == 0, c == DC - 1)
                        last.then_inc(pj_ready, 1)
                pe.wait_ge(tok_ready, hf * DC + DC)
                pe.sem_inc(pe_passed, 1)
                with pe.Fori(0, C0) as c8:
                    cpj = pjb + c8 * PJ_CU + PJ_C
                    csc = hf * SC_H + c8 * SC_CU
                    ctp = hf * TP_H + c8 * TP_CU
                    co = hf * O_H + c8 * O_CU
                    q_stage(cpj, hf * WQ_H + c8, 0, width=P)

                    def keys0(b, chunks):
                        if chunks[0] == 0:
                            pe.wait_ge(pj_free, cpj + K_UNIT[b] + 1)
                        if b == 0:
                            pe.wait_ge(w_ready["k"], (hf * WK_H + c8) * DC + DC)
                        for c in chunks:
                            last = three(pj[K_UNIT[b] % PJ][:, 0:SK],
                                         [f[:, c * P:(c + 1) * P] for f in flat["k"]],
                                         (ctx_hi[:, c, b, :], ctx_lo[:, c, b, :]), c == 0, c == DC - 1)
                        if chunks[-1] == DC - 1:
                            last.then_inc(pj_ready, 3 if b == HB - 1 else 1)

                    def place(js):
                        for j in js:
                            unit = PLACED + j
                            if j == 0:
                                pe.wait_ge(pj_free, cpj + 1 + PJ)
                            pe.wait_ge(pj_free, cpj + unit + 1)
                            for e in range(2):
                                last = nc.tensor.matmul(pj[unit % PJ][:, 0:T], place_sel[:, e, j, :],
                                                        q0_split[e], start=(e == 0), stop=(e == 1))
                            last.then_inc(pj_ready, 1)

                    def scores0(n):
                        b, j = n // HPC, n % HPC
                        if j == 0:
                            pe.wait_ge(pj_free, cpj + K_UNIT[b] + 1 + PJ)
                        if b == 0:
                            pe.wait_ge(pj_free, cpj + PLACED + j + 1 + PJ)
                        pe.wait_ge(max_ready, csc + n + 1)
                        nc.tensor.matmul(scores[n % SCR][0:L, 0:SK], qo_hi[:, j, b * L:(b + 1) * L],
                                         k0[b % 2], start=True, stop=True).then_inc(sc_ready, 1)

                    def transpose0(n):
                        unit = tp_unit("probs", n)
                        pe.wait_ge(exp_ready, csc + n + 1 + SCR)
                        pe.wait_ge(tp_free, ctp + unit + 1)
                        for s in range(SC):
                            last = transpose(tp[unit % TP][0:KC, s * L:(s + 1) * L],
                                             probs[0:L, n % 4, s * KC:(s + 1) * KC], L)
                        last.then_inc(tp_ready, 1)

                    def weigh0(u, s):
                        if u == 0:
                            pe.wait_ge(v0c_ready, (hf * C0 + c8) * 2 + 2)
                        if s == 0:
                            pe.wait_ge(tp_free, ctp + tp_unit("probs", 4 * u + 3) + 1 + TP)
                        v = v0c[0:KC, u // 2 * SC + s, u % 2, :]
                        p_hi, p_lo = (t[0:KC, :, s * L:(s + 1) * L] for t in pt0[u % 2])
                        nc.tensor.matmul(o_ps[0:32, 0:T], v, p_hi, start=(s == 0), stop=False)
                        last = nc.tensor.matmul(o_ps[0:HD0, 0:T], v[:, 0:HD0], p_lo, start=False,
                                                stop=(s == SC - 1))
                        if s == SC - 1:
                            last.then_inc(o_ready, 1)

                    def four_transpose0(u):
                        unit = tp_unit("four", u)
                        pe.wait_ge(o_mid, co + u + 1)
                        pe.wait_ge(tp_free, ctp + unit + 1)
                        pe.sem_inc(pe_passed, 1)
                        for h in range(4):
                            last = transpose(tp[unit % TP][0:L, 32 * h:32 * h + 32],
                                             o_t[:, h * L:(h + 1) * L], 32)
                        last.then_inc(tp_ready, 1)

                    def out_transpose0(b):
                        unit = tp_unit("batch", b)
                        pe.wait_ge(o_nat_ready, (hf * C0 + c8) * HB + b + 1)
                        pe.wait_ge(tp_free, ctp + unit + 1)
                        transpose(tp[unit % TP][:, 0:L],
                                  o_nat[0:L, :, :].rearrange("p h d -> p (h d)"), L).then_inc(tp_ready, 1)

                    keys0(0, range(DC))
                    place(range(4))
                    for n in range(4):
                        scores0(n)
                        place([4 + n])
                    for n in range(SC_CU):
                        b, j = n // HPC, n % HPC
                        transpose0(n)
                        if n + 4 < SC_CU:
                            scores0(n + 4)
                        if j < 2 and b + 1 < HB:
                            keys0(b + 1, (2 * j, 2 * j + 1))
                        if n >= 9 and n % 4 == 1:
                            four_transpose0((n - 9) // 4)
                        if n >= 5 and n % 4 >= 1:
                            weigh0(n // 4 - 1, n % 4 - 1)
                        if n >= 15 and j == 7:
                            out_transpose0((n - 15) // HPC)
                    four_transpose0(2 * HB - 2)
                    for s in range(SC):
                        weigh0(2 * HB - 1, s)
                    four_transpose0(2 * HB - 1)
                    out_transpose0(HB - 1)

                def ready0(b):
                    if b == 0:
                        pe.wait_ge(tp_free, hf * TP_H + TP_A + TP)
                out_stage(pjb + PJ_W0, hf * WO_H, 0, ot0, ready0, pad=3)

                with pe.Fori(0, ATT) as a:
                    apj = pjb + a * PJ_AU + PJ_A
                    ln_stage(apj, 0, hf * NL + a)
                    pe.wait_ge(pj_free, apj + 6 + PJ)
                    pe.sem_inc(pe_passed, 1)
                    with pe.Fori(0, G1) as g:
                        ag = a * G1 + g
                        gpj = apj + g * PJ_GU + 6
                        gsc = hf * SC_H + ag * SC_GU + SC_A
                        gtp = hf * TP_H + ag * SC_GU + TP_A
                        gof = (hf * ATT * G1 + ag) * HB
                        use_k, use_v = hf * WK_H + ag + C0, hf * WV_H + ag + 1

                        def keys1(b, h):
                            unit = HPG + b * (HPG + SC) + h
                            pe.wait_ge(pj_free, gpj + unit + 1)
                            for c in range(DC):
                                if b == 0 and h == 0:
                                    pe.wait_ge(w_ready["k"], use_k * DC + c + 1)
                                last = three(pj[unit % PJ][:, 0:SK],
                                             [w["k"][:, c, h * P:(h + 1) * P] for w in (w_hi, w_lo)],
                                             (ctx_hi[:, c, b, :], ctx_lo[:, c, b, :]),
                                             c == 0, c == DC - 1)
                            last.then_inc(pj_ready, 1)

                        def values1(b, s):
                            unit = HPG + b * (HPG + SC) + HPG + s
                            pe.wait_ge(pj_free, gpj + unit + 1)
                            for c in range(DC):
                                if b == 0 and s == 0:
                                    pe.wait_ge(w_ready["v"], use_v * DC + c + 1)
                                last = three(pj[unit % PJ][0:KC, :],
                                             [t[:, c, b, s * KC:(s + 1) * KC] for t in (ctx_hi, ctx_lo)],
                                             (w_hi["v"][:, c, :], w_lo["v"][:, c, :]),
                                             c == 0, c == DC - 1)
                            last.then_inc(pj_ready, 1)

                        def scores1(b, h):
                            n = b * HPG + h
                            if h == 0:
                                pe.wait_ge(pj_free, gpj + HPG + b * (HPG + SC) + HPG + PJ)
                            pe.wait_ge(exp_ready, gsc + n + 1)
                            three(scores[n % SCR][0:L, 0:SK],
                                  [q[:, h, b * L:(b + 1) * L] for q in (qo_hi, qo_lo)],
                                  (k_hi[:, h, :], k_lo[:, h, :]), True, True).then_inc(sc_ready, 1)

                        def transpose1(b, h):
                            n = b * HPG + h
                            pe.wait_ge(norm_ready, (hf * ATT * G1 + ag) * SC_GU + n + 1)
                            pe.wait_ge(tp_free, gtp + n + 1)
                            for s in range(SC):
                                last = transpose(tp[n % TP][0:KC + 1, s * L:(s + 1) * L],
                                                 probs[0:L, h, s * KC:(s + 1) * KC + 1], L)
                            last.then_inc(tp_ready, 1)

                        def weigh1(b):
                            if b == 0:
                                pe.wait_ge(bvrow_in, (hf * ATT * G1 + ag) * 32 + 32)
                            pe.wait_ge(pj_free, gpj + HPG + (b + 1) * (HPG + SC) + PJ)
                            pe.wait_ge(o_free, gof + b + 1)
                            for h in range(HPG):
                                pe.wait_ge(tp_free, gtp + b * HPG + h + 1 + TP)
                                for s in range(SC):
                                    n = KC + 1 if s == SC - 1 else KC
                                    last = three(o_ps[:, h * L:(h + 1) * L],
                                                 [v[0:n, s, h * P:(h + 1) * P] for v in v1],
                                                 [q[0:n, h, s * L:(s + 1) * L] for q in (pt_hi, pt_lo)],
                                                 s == 0, s == SC - 1)
                            last.then_inc(o_ready, 1)

                        q_stage(gpj, hf * WQ_H + ag + C0, 0)
                        for b in range(HB):
                            if b > 0:
                                transpose1(b - 1, 0)
                                transpose1(b - 1, 1)
                            keys1(b, 0)
                            if b > 0:
                                transpose1(b - 1, 2)
                                transpose1(b - 1, 3)
                            for h in range(1, HPG):
                                keys1(b, h)
                            if b > 0:
                                weigh1(b - 1)
                            values1(b, 0)
                            scores1(b, 0)
                            scores1(b, 1)
                            values1(b, 1)
                            scores1(b, 2)
                            scores1(b, 3)
                            values1(b, 2)
                        for h in range(HPG):
                            transpose1(HB - 1, h)
                        weigh1(HB - 1)

                        def ready1(b):
                            pe.wait_ge(o_free, gof + b + 2)
                        out_stage(gpj, hf * WO_H + ag + 1, PJ_GU - HB,
                                  [q[:, HPG:2 * HPG, :] for q in (qo_hi, qo_lo)], ready1)

                ln_stage(pjb + PJ_M, 0, hf * NL + ATT)
                pe.wait_ge(pj_free, pjb + PJ_M + 6 + PJ)
                pe.sem_inc(pe_passed, 1)
                with pe.Fori(0, MLPG) as m:
                    mpj = pjb + m * PJ_MU + (PJ_M + 6)
                    q_stage(mpj, hf * WQ_H + m + (C0 + ATT * G1), 0)

                    def ready2(b):
                        if b == 0:
                            pe.wait_ge(pj_free, mpj + HPG + PJ)
                    out_stage(mpj, hf * WO_H + m + (1 + ATT * G1), HPG,
                              [q[:, 0:HPG, :] for q in (qo_hi, qo_lo)], ready2, pad=2)

        @block.scalar
        def _(act):
            def move(dst, src, ready, n, bias=None, mid=None):
                act.wait_ge(ready, n)
                if bias is None:
                    i = nc.scalar.activation(dst, src, ACT.Copy)
                else:
                    i = nc.scalar.activation(dst, src, ACT.Identity, bias=bias)
                if mid is not None:
                    i.then_inc(mid, 1)

            def ln_std(nn, which):
                act.wait_ge(ln_chain, nn * 9 + 8)
                nc.scalar.activation(std[0:L, :], mean_var[0:L, :, 1], ACT.Sqrt,
                                     bias=eps[0:L, which:which + 1]).then_inc(std_ready, 1)

            def ln_stage(nl):
                for b in range(HB):
                    act.wait_ge(ln_t, (nl * HB + b + 1) * 4)
                    nc.scalar.activation(h_hi[:, :, b * L:(b + 1) * L],
                                         tmp[1][:, 0:T].rearrange("p (c l) -> p c l", c=DC),
                                         ACT.Copy).then_inc(pj_mid, 1)

            act.wait_ge(setup_bv, 3)
            act.dma_start(bv_hi_dram, pt_hi[:].rearrange("p h n -> p (h n)")[0:8, 0:GW].bitcast(F32)).then_inc(setup_dma, 16)
            act.dma_start(bv_lo_dram, pt_lo[:].rearrange("p h n -> p (h n)")[0:8, 0:GW].bitcast(F32)).then_inc(setup_dma, 16)
            act.wait_ge(setup_dma, 80)
            act.sem_inc(out_done, 16)
            act.wait_ge(setup_pool, 2)
            for s in w_free.values():
                act.sem_inc(s, 1)

            with act.Fori(0, HALVES) as hf:
                pjb = hf * PJ_H
                act.wait_ge(out_done, hf * 16 + 16)
                act.dma_start(mask_v, mask[bass.ds(hf * HB, HB), :, :].rearrange("b p n -> p b n")).then_inc(mask_in, 16)
                for b in range(HB):
                    for s in range(SC):
                        unit = b * SC + s
                        move(v0[0][0:KC, unit, :], pj[unit % PJ][0:KC, 0:P], pj_ready, pjb + unit + 1,
                             mid=pj_mid)
                with act.Fori(0, C0) as c8:
                    cpj = pjb + c8 * PJ_CU + PJ_C
                    csc = hf * SC_H + c8 * SC_CU
                    ctp = hf * TP_H + c8 * TP_CU
                    co = hf * O_H + c8 * O_CU
                    cc = hf * C0 + c8

                    def keys0(b):
                        move(k0[b % 2], pj[K_UNIT[b] % PJ][:, 0:SK], pj_ready, cpj + K_UNIT[b] + 1,
                             bias=cur[:, 1:2], mid=pj_mid)

                    def placed(j):
                        unit = PLACED + j
                        move(qo_hi[:, j, :], pj[unit % PJ][:, 0:T], pj_ready, cpj + unit + 1, mid=pj_mid)

                    def exps0(n):
                        b, j, h = n // HPC, n % HPC, n % 4
                        act.wait_ge(max_ready, csc + n + 1 + SCR)
                        nc.scalar.activation(probs[0:L, h, 0:S], probs[0:L, h, 0:S], ACT.Exp,
                                             bias=neg_max[0:L, j:j + 1], scale=-1.0,
                                             accum_out=row_sum[0:L, b % 2, j:j + 1]).then_inc(exp_ready, 1)

                    def out0(b):
                        unit = tp_unit("batch", b)
                        act.wait_ge(tp_ready, ctp + unit + 1)
                        nc.scalar.activation(
                            ot0[0][:, bass.ds(c8, 1), b * L:(b + 1) * L].rearrange("p c l -> p (c l)"),
                            tp[unit % TP][:, 0:L], ACT.Identity, bias=cur[:, 2:3]).then_inc(tp_mid, 1)

                    def outputs(u):
                        move(o_t, o_ps[0:32, 0:T], o_ready, co + u + 1, mid=o_mid)

                    act.wait_ge(cur_ready, hf * WQ_H + c8 + 1)
                    act.wait_ge(pj_ready, cpj + 1)
                    act.sem_inc(w_free["q"], 1)
                    nc.scalar.activation(q0_f32, pj[0][:, 0:T], ACT.Identity, bias=cur[:, 0:1],
                                         scale=SCALE0).then_inc(q0_ready, 1)
                    keys0(0)
                    placed(1)
                    placed(3)
                    exps0(0)
                    placed(5)
                    exps0(1)
                    placed(7)
                    exps0(2)
                    for n in range(SC_CU):
                        b, j, unit = n // HPC, n % HPC, tp_unit("probs", n)
                        if n >= 8 and n % 4 == 0:
                            outputs((n - 8) // 4)
                        move(pt0[n // 4 % 2][0][0:KC, n % 4, :], tp[unit % TP][0:KC, 0:SC * L], tp_ready,
                             ctp + unit + 1, mid=tp_mid)
                        if n + 3 < SC_CU:
                            exps0(n + 3)
                        if j == 1 and b + 1 < HB:
                            keys0(b + 1)
                        if n >= 15 and j == 7:
                            out0((n - 15) // HPC)
                    outputs(2 * HB - 2)
                    outputs(2 * HB - 1)
                    act.sem_inc(w_free["k"], 1)
                    out0(HB - 1)
                act.wait_ge(max_ready, hf * SC_H + SC_A + SCR)
                act.dma_start(xa[0:L, :, :], x[bass.ds(hf * T, T), :].rearrange("(b p) n -> p b n", p=L)).then_inc(x_in, 16)
                act.dma_start(probs_flat[0:L, :], rows_in[0:1, 0:3 * D].partition_broadcast(L)).then_inc(rows_ready, 16)
                ln_std(hf * 4, 0)

                with act.Fori(0, ATT) as a:
                    apj = pjb + a * PJ_AU + PJ_A
                    act.wait_ge(post_ln, hf * 12 + 12)
                    act.dma_start(tmp[2][0:L, :], rows_in[0:1, bass.ds((a + 3) * D, D)].partition_broadcast(L)).then_inc(rows_ready, 16)
                    ln_std(hf * 4 + a + 1, 1)
                    ln_stage(hf * NL + a)
                    with act.Fori(0, G1) as g:
                        ag = a * G1 + g
                        gpj = apj + g * PJ_GU + 6
                        gsc = hf * SC_H + ag * SC_GU + SC_A
                        gtp = hf * TP_H + ag * SC_GU + TP_A
                        go = hf * O_H + ag * HB + O_A
                        gg = hf * ATT * G1 + ag

                        def values1(b, s):
                            unit = HPG + b * (HPG + SC) + HPG + s
                            move(v1[0][0:KC, s, :], pj[unit % PJ][0:KC, :], pj_ready, gpj + unit + 1,
                                 mid=pj_mid)
                            if b == HB - 1 and s == SC - 1:
                                act.sem_inc(w_free["v"], 1)

                        def keys1(b, h):
                            unit = HPG + b * (HPG + SC) + h
                            move(k_hi[:, h, 0:S], pj[unit % PJ][:, 0:S], pj_ready, gpj + unit + 1,
                                 bias=cur[:, 4 + h:5 + h], mid=pj_mid)
                            if b == HB - 1 and h == HPG - 1:
                                act.sem_inc(w_free["k"], 1)

                        def exps1(b, h):
                            n = b * HPG + h
                            act.wait_ge(max_ready, gsc + n + 1 + SCR)
                            nc.scalar.activation(probs[0:L, h, 0:SK], scores[n % SCR][0:L, 0:SK], ACT.Exp,
                                                 bias=neg_max[0:L, h:h + 1],
                                                 accum_out=row_sum[0:L, 0, h:h + 1]).then_inc(exp_ready, 1)

                        def split_p(b, h):
                            n = b * HPG + h
                            move(pt_hi[0:KC + 1, h, :], tp[n % TP][0:KC + 1, 0:SC * L], tp_ready,
                                 gtp + n + 1, mid=tp_mid)

                        def out1(b):
                            act.wait_ge(o_ready, go + b + 1)
                            for h in range(HPG):
                                i = nc.scalar.activation(qo_hi[:, HPG + h, b * L:(b + 1) * L],
                                                         o_ps[:, h * L:(h + 1) * L], ACT.Identity,
                                                         bias=cur[:, 12 + h:13 + h])
                            i.then_inc(o_mid, 1)

                        act.wait_ge(cur_ready, hf * WQ_H + ag + C0 + 1)
                        act.wait_ge(o_ready, go)
                        act.dma_start(v1[0][KC:KC + 1, SC - 1, :].bitcast(F32), bv_hi_dram[bass.ds(ag, 1), :]).then_inc(bvrow_in, 16)
                        act.dma_start(v1[1][KC:KC + 1, SC - 1, :].bitcast(F32), bv_lo_dram[bass.ds(ag, 1), :]).then_inc(bvrow_in, 16)
                        for h in range(HPG):
                            if h == 3:
                                act.wait_ge(pj_free, gpj + 1 + PJ)
                            act.wait_ge(pj_ready, gpj + h + 1)
                            nc.scalar.activation(tmp[h % 3][:, 0:T], pj[h % PJ][:, 0:T], ACT.Identity,
                                                 bias=cur[:, h:h + 1], scale=SCALE1).then_inc(pj_mid, 1)
                        act.sem_inc(w_free["q"], 1)
                        for b in range(HB):
                            if b > 0:
                                split_p(b - 1, 0)
                                split_p(b - 1, 1)
                            keys1(b, 0)
                            if b > 0:
                                split_p(b - 1, 2)
                                split_p(b - 1, 3)
                            for h in range(1, HPG):
                                keys1(b, h)
                            if b > 0:
                                out1(b - 1)
                            values1(b, 0)
                            exps1(b, 0)
                            exps1(b, 1)
                            values1(b, 1)
                            exps1(b, 2)
                            exps1(b, 3)
                            values1(b, 2)
                        for h in range(HPG):
                            split_p(HB - 1, h)
                        out1(HB - 1)

                act.dma_start(tmp[2][0:L, :], rows_in[0:1, 5 * D:6 * D].partition_broadcast(L)).then_inc(rows_ready, 16)
                ln_std(hf * 4 + 3, 1)
                ln_stage(hf * NL + ATT)
                with act.Fori(0, MLPG) as m:
                    mpj = pjb + m * PJ_MU + (PJ_M + 6)
                    act.wait_ge(cur_ready, hf * WQ_H + m + (C0 + ATT * G1) + 1)
                    for h in range(HPG):
                        act.wait_ge(pj_free, mpj + h + 1)
                        act.wait_ge(pj_ready, mpj + h + 1)
                        nc.scalar.activation(tmp[h % 3][:, 0:T], pj[h % PJ][:, 0:T], ACT.Gelu,
                                             bias=cur[:, h:h + 1]).then_inc(pj_mid, 1)
                    act.sem_inc(w_free["q"], 1)
                act.wait_ge(pj_free, pjb + PJ_H + PJ)
                act.dma_start(out[bass.ds(hf * T, T), :].rearrange("(b p) n -> p b n", p=L), xa[0:L, :, :]).then_inc(out_done, 16)

        @block.vector
        def _(dve):
            def lo_of(dst, src, hi, mid, n, signal, k=1, bias=None):
                dve.wait_ge(mid, n)
                if bias is None:
                    i = nc.vector.tensor_tensor(dst, src, hi.bitcast(F32), ALU.subtract)
                else:
                    i = nc.vector.scalar_tensor_tensor(dst, src, bias, hi.bitcast(F32), ALU.add, ALU.subtract)
                i.then_inc(signal, k)

            def ln_stats(nn):
                for b in range(HB):
                    nc.vector.bn_stats(stats[0:L, b, :], xa[0:L, b, :]).then_inc(ln_chain, 1)
                for b in range(HB):
                    dve.wait_ge(ln_chain, nn * 9 + b + 1)
                    dve.sem_inc(dve_passed, 1)
                    nc.vector.bn_aggr(mean_var[0:L, b, :], stats[0:L, b, :]).then_inc(ln_chain, 1)
                dve.wait_ge(std_ready, nn + 1)
                nc.vector.reciprocal(rstd[0:L, :], std[0:L, :]).then_inc(ln_chain, 1)
                dve.wait_ge(ln_chain, nn * 9 + 9)

            def ln_stage(base, unit, nn, nl, mid0, par):
                nc.vector.tensor_copy(ln_cur[:], par).then_inc(ln_par, 1)
                ln_stats(nn)
                dve.wait_ge(ln_par, nl + 1)
                dve.wait_ge(rows_ready, nn * 16 + 16)

                def normed(b):
                    nc.vector.tensor_scalar(tmp[0][0:L, :], xa[0:L, b, :], mean_var[0:L, b, 0:1],
                                            rstd[0:L, b:b + 1], ALU.subtract, ALU.mult).then_inc(xn_ready, 1)
                    dve.wait_ge(xn_ready, nl * HB + b + 1)
                    nc.vector.tensor_tensor(xa[0:L, b, :], xa[0:L, b, :], tmp[2][0:L, :], ALU.add).then_inc(bias_added, 1)

                normed(0)
                for b in range(HB):
                    bank = pj[(unit + b) % PJ]
                    dve.wait_ge(pj_ready, base + unit + b + 1)
                    dve.wait_ge(pj_free, base + unit + b + PJ)
                    for c in range(DC):
                        nc.vector.tensor_scalar(tmp[1][:, c * L:(c + 1) * L], bank[:, c * L:(c + 1) * L],
                                                ln_cur[:, c:c + 1], ln_cur[:, 4 + c:5 + c],
                                                ALU.mult, ALU.add).then_inc(ln_t, 1)
                    if b + 1 < HB:
                        normed(b + 1)
                    lo_of(h_lo[:, :, b * L:(b + 1) * L], tmp[1][:, 0:T].rearrange("p (c l) -> p c l", c=DC),
                          h_hi[:, :, b * L:(b + 1) * L], pj_mid, mid0 + b + 1, pj_free,
                          3 if b == HB - 1 else 1)

            def out_stage(base, unit, pad=1):
                for b in range(HB):
                    dve.wait_ge(pj_ready, base + unit + b + 1)
                    if b == HB - 1:
                        dve.sem_inc(w_free["o"], 1)
                    nc.vector.tensor_tensor(xa[0:L, b, :], pj[(unit + b) % PJ][0:L, :], xa[0:L, b, :],
                                            ALU.add).then_inc(pj_free, pad if b == HB - 1 else 1)

            def q_stage(base, mid0, done0):
                for h in range(HPG):
                    dve.wait_ge(pj_mid, mid0 + h + 1)
                    nc.vector.tensor_copy(qo_hi[:, h, :], tmp[h % 3][:, 0:T]).then_inc(qh_done, 1)
                    lo_of(qo_lo[:, h, :], tmp[h % 3][:, 0:T], qo_hi[:, h, :], qh_done, done0 + h + 1, pj_free)

            dve.wait_ge(setup_pool, 2)
            dve.sem_inc(pj_free, PJ)
            dve.sem_inc(max_ready, SCR)
            dve.sem_inc(exp_ready, SCR)
            dve.sem_inc(tp_free, TP)
            dve.sem_inc(o_free, 1)
            dve.wait_ge(setup_dma, 48)
            q1 = prm[:, 0:PRM_LN].rearrange("p (j e) -> p j e", e=16)[:, :, 0:HPG]
            nc.vector.tensor_scalar(q1, q1, SCALE1, None, ALU.mult).then_inc(setup_dve, 1)
            q0 = prm[:, PRM_C:PRM_N].rearrange("p (c e) -> p c e", e=3)[:, :, 0]
            nc.vector.tensor_scalar(q0, q0, SCALE0, None, ALU.mult).then_inc(setup_dve, 1)
            rows8 = xa[0:ATT * G1, :, :]
            nc.vector.tensor_tensor(rows8[:, 2, :], rows8[:, 0, :], rows8[:, 1, :], ALU.subtract).then_inc(setup_bv, 1)
            dve.wait_ge(setup_bv, 1)
            row_hi = pt_hi[:].rearrange("p h n -> p (h n)")[0:8, 0:GW]
            row_lo = pt_lo[:].rearrange("p h n -> p (h n)")[0:8, 0:GW]
            nc.vector.tensor_copy(row_hi, rows8[:, 2, :]).then_inc(setup_bv, 1)
            dve.wait_ge(setup_bv, 2)
            nc.vector.tensor_tensor(row_lo, rows8[:, 2, :], row_hi.bitcast(F32), ALU.subtract).then_inc(setup_bv, 1)
            dve.wait_ge(setup_dve, 2)

            with dve.Fori(0, HALVES) as hf:
                pjb = hf * PJ_H
                midb = hf * MID_H
                dve.wait_ge(pj_free, pjb + PJ)
                nc.vector.memset(place_sel.bitcast(F32), 0.0).then_inc(sel_zero, 1)
                dve.wait_ge(sel_zero, hf + 1)
                for kv in range(KV2):
                    heads = ident[:, kv * 64:kv * 64 + 64].rearrange("p (j d) -> p j d", d=HD0)
                    for e in range(2):
                        for r in range(2):
                            at = 64 * kv + 32 * r + 16 * e
                            nc.vector.tensor_copy(place_sel[:, e, 4 * kv:4 * kv + 4, at:at + HD0], heads)
                for b in range(HB):
                    for s in range(SC):
                        unit = b * SC + s
                        lo_of(v0[1][0:KC, unit, :], pj[unit % PJ][0:KC, 0:P], v0[0][0:KC, unit, :],
                              pj_mid, midb + unit + 1, pj_free)
                with dve.Fori(0, C0) as c8:
                    cpj = pjb + c8 * PJ_CU + PJ_C
                    cmid = midb + c8 * MID_CU + MID_C
                    csc = hf * SC_H + c8 * SC_CU
                    ctp = hf * TP_H + c8 * TP_CU
                    ctm = hf * TM_H + c8 * TM_CU
                    cc = hf * C0 + c8
                    ob = hf * (C0 * HB) + c8 * HB

                    def keys0(b):
                        dve.wait_ge(pj_mid, cmid + mid_keys(b) + 1)
                        for r in (32, 96):
                            rows = slice(r, r + 32)
                            i = nc.vector.scalar_tensor_tensor(
                                k0[b % 2][rows, :], pj[K_UNIT[b] % PJ][rows, 0:SK], cur[rows, 1:2],
                                k0[b % 2][rows, :].bitcast(F32), ALU.add, ALU.subtract)
                        i.then_inc(pj_free, 3 if b == HB - 1 else 1)

                    def placed(j):
                        unit = PLACED + j
                        if j % 2 == 1:
                            dve.wait_ge(pj_mid, cmid + 1 + j // 2 + 1)
                            dve.wait_ge(pj_free, cpj + unit + PJ)
                            dve.sem_inc(pj_free, 1)
                        else:
                            dve.wait_ge(pj_ready, cpj + unit + 1)
                            nc.vector.tensor_copy(qo_hi[:, j, :], pj[unit % PJ][:, 0:T]).then_inc(pj_free, 1)

                    def max0(n):
                        b, j = n // HPC, n % HPC
                        dve.wait_ge(sc_ready, csc + n + 1)
                        dve.sem_inc(dve_passed, 1)
                        nc.vector.tensor_tensor_reduce(
                            probs[0:L, n % 4, 0:S], scores[n % SCR][0:L, 0:S], mask_v[:, b, :], -1.0, 3.0e38,
                            ALU.add, ALU.min, neg_max[0:L, j:j + 1]).then_inc(max_ready, 1)

                    def sum_outputs(u):
                        unit = tp_unit("four", u)
                        dve.wait_ge(tp_ready, ctp + unit + 1)
                        nc.vector.tensor_reduce(
                            o_nat[0:L, 4 * (u % 2):4 * (u % 2) + 4, :],
                            tp[unit % TP][0:L, 0:P].rearrange("p (h e d) -> p h d e", e=2, d=HD0),
                            AX_X, ALU.add).then_inc(tp_free, 1)

                    def inverse_sums(b):
                        dve.wait_ge(exp_ready, csc + HPC * (b + 1) + SCR)
                        nc.vector.reciprocal(inv_sum[0:L, :], row_sum[0:L, b % 2, :]).then_inc(o_inv, 1)

                    def scale_outputs(b):
                        dve.wait_ge(o_inv, ob + b + 1)
                        dve.wait_ge(tp_free, ctp + tp_unit("four", 2 * b + 1) + 1 + TP)
                        nc.vector.tensor_tensor(o_nat[0:L], o_nat[0:L],
                                                inv_sum[0:L, :].unsqueeze(2).broadcast_to([L, HPC, HD0]),
                                                ALU.mult).then_inc(o_nat_ready, 1)

                    def out0(b):
                        n = tp_unit("batch", b)
                        dst = [o[:, bass.ds(c8, 1), b * L:(b + 1) * L].rearrange("p c l -> p (c l)") for o in ot0]
                        lo_of(dst[1], tp[n % TP][:, 0:L], dst[0], tp_mid,
                              ctm + tp_mid_unit("batch", b) + 1, tp_free,
                              bias=cur[:, 2:3])

                    dve.wait_ge(pj_ready, cpj + 1)
                    dve.wait_ge(pj_free, cpj + PJ)
                    dve.wait_ge(tp_free, ctp + TP)
                    nc.vector.tensor_copy(cur[:, 0:3], prm[:, bass.ds(c8 * 3 + PRM_C, 3)]).then_inc(cur_ready, 1)
                    dve.wait_ge(q0_ready, cc + 1)
                    nc.vector.tensor_copy(q0_split[0], q0_f32).then_inc(q0_hi, 1)
                    lo_of(q0_split[1], q0_f32, q0_split[0], q0_hi, cc + 1, pj_free)
                    dve.wait_ge(cur_ready, hf * WQ_H + c8 + 1)
                    keys0(0)
                    for j in range(4):
                        placed(j)
                    dve.wait_ge(mask_in, hf * 16 + 16)
                    for n in range(4):
                        max0(n)
                        placed(4 + n)
                    for e, v in enumerate(v0):
                        nc.vector.tensor_copy(
                            v0c[0:KC, :, :, e * HD0:(e + 1) * HD0],
                            v[0:KC, :, bass.ds(c8 * (KV2 * HD0), KV2 * HD0)].bitcast(F32).rearrange(
                                "p n (k d) -> p n k d", d=HD0)).then_inc(v0c_ready, 1)
                    for n in range(SC_CU):
                        b, j, unit = n // HPC, n % HPC, tp_unit("probs", n)
                        if b > 0 and j == 0:
                            inverse_sums(b - 1)
                        if n + 4 < SC_CU:
                            max0(n + 4)
                        lo_of(pt0[n // 4 % 2][1][0:KC, n % 4, :], tp[unit % TP][0:KC, 0:SC * L],
                              pt0[n // 4 % 2][0][0:KC, n % 4, :], tp_mid,
                              ctm + tp_mid_unit("probs", n) + 1, tp_free)
                        if j == 1 and b + 1 < HB:
                            keys0(b + 1)
                        if n >= 9 and n % 4 == 1:
                            sum_outputs((n - 9) // 4)
                            if n % HPC == 5:
                                scale_outputs((n - 13) // HPC)
                        if n >= 15 and j == 7:
                            out0((n - 15) // HPC)
                    inverse_sums(HB - 1)
                    sum_outputs(2 * HB - 2)
                    sum_outputs(2 * HB - 1)
                    scale_outputs(HB - 1)
                    out0(HB - 1)

                dve.wait_ge(x_in, hf * 16 + 16)
                dve.wait_ge(rows_ready, hf * 64 + 16)
                for b in range(HB):
                    nc.vector.tensor_tensor(xa[0:L, b, :], xa[0:L, b, :], tmp[0][0:L, :], ALU.add).then_inc(bias_added, 1)
                dve.wait_ge(bias_added, hf * 16 + 4)
                out_stage(pjb + PJ_W0, 0, pad=3)
                dve.sem_inc(w_free["v"], 1)
                dve.wait_ge(pj_free, pjb + PJ_A + PJ)
                ln_stats(hf * 4)
                for b in range(HB):
                    nc.vector.tensor_scalar(xa[0:L, b, :], xa[0:L, b, :], mean_var[0:L, b, 0:1],
                                            rstd[0:L, b:b + 1], ALU.subtract, ALU.mult).then_inc(post_ln, 1)
                for k, op in ((1, ALU.mult), (2, ALU.add)):
                    for b in range(HB):
                        dve.wait_ge(post_ln, hf * 12 + 4 * (k - 1) + b + 1)
                        nc.vector.tensor_tensor(xa[0:L, b, :], xa[0:L, b, :], tmp[k][0:L, :], op).then_inc(post_ln, 1)
                dve.wait_ge(post_ln, hf * 12 + 12)
                dve.sem_inc(dve_passed, 1)

                with dve.Fori(0, ATT) as a:
                    apj = pjb + a * PJ_AU + PJ_A
                    amid = midb + a * MID_AU + MID_A
                    dve.wait_ge(pj_free, apj + PJ)
                    ln_stage(apj, 0, hf * 4 + a + 1, hf * NL + a, amid,
                             prm[:, bass.ds(a * 8 + PRM_LN, 8)])
                    with dve.Fori(0, G1) as g:
                        ag = a * G1 + g
                        gpj = apj + g * PJ_GU + 6
                        gmid = amid + g * MID_GU + HB
                        gsc = hf * SC_H + ag * SC_GU + SC_A
                        gtm = hf * TM_H + ag * SC_GU + TM_A
                        gof = (hf * ATT * G1 + ag) * HB
                        gg = (hf * ATT * G1 + ag) * SC_GU

                        def keys1(b, h):
                            unit = HPG + b * (HPG + SC) + h
                            lo_of(k_lo[:, h, 0:S], pj[unit % PJ][:, 0:S], k_hi[:, h, 0:S], pj_mid,
                                  gmid + unit + 1, pj_free, bias=cur[:, 4 + h:5 + h])

                        def values1(b, s):
                            unit = HPG + b * (HPG + SC) + HPG + s
                            lo_of(v1[1][0:KC, s, :], pj[unit % PJ][0:KC, :], v1[0][0:KC, s, :], pj_mid,
                                  gmid + unit + 1, pj_free)

                        def max1(b, h):
                            n = b * HPG + h
                            dve.wait_ge(sc_ready, gsc + n + 1)
                            nc.vector.tensor_reduce(neg_max[0:L, h:h + 1], scores[n % SCR][0:L, 0:SK], AX_X,
                                                    ALU.max, negate=True).then_inc(max_ready, 1)

                        def norm1(b, h):
                            n = b * HPG + h
                            dve.wait_ge(exp_ready, gsc + n + 1 + SCR)
                            nc.vector.reciprocal(inv_sum[0:L, h:h + 1], row_sum[0:L, 0, h:h + 1]).then_inc(inv_ready, 1)
                            dve.wait_ge(inv_ready, gg + n + 1)
                            nc.vector.tensor_scalar(probs[0:L, h, 0:SK], probs[0:L, h, 0:SK],
                                                    inv_sum[0:L, h:h + 1], None, ALU.mult).then_inc(norm_ready, 1)

                        def split_p(b, h):
                            n = b * HPG + h
                            lo_of(pt_lo[0:KC + 1, h, :], tp[n % TP][0:KC + 1, 0:SC * L],
                                  pt_hi[0:KC + 1, h, :], tp_mid, gtm + n + 1, tp_free)

                        def out1(b):
                            dve.wait_ge(o_mid, hf * O_H + ag * HB + (O_A + b + 1))
                            for h in range(HPG):
                                cols = slice(b * L, (b + 1) * L)
                                i = nc.vector.scalar_tensor_tensor(
                                    qo_lo[:, HPG + h, cols], o_ps[:, h * L:(h + 1) * L], cur[:, 12 + h:13 + h],
                                    qo_hi[:, HPG + h, cols].bitcast(F32), ALU.add, ALU.subtract)
                            i.then_inc(o_free, 1)

                        dve.wait_ge(pj_ready, gpj + 1)
                        dve.wait_ge(o_free, gof + 1)
                        nc.vector.tensor_copy(cur[:], prm[:, bass.ds(ag * 16, 16)]).then_inc(cur_ready, 1)
                        dve.wait_ge(cur_ready, hf * WQ_H + ag + C0 + 1)
                        kb = cur[:, 8:12].unsqueeze(2)
                        nc.vector.tensor_copy(k_hi[:, :, S:SK], kb).then_inc(kbias_hi, 1)
                        dve.wait_ge(kbias_hi, hf * ATT * G1 + ag + 1)
                        nc.vector.tensor_tensor(k_lo[:, :, S:SK], kb, k_hi[:, :, S:SK].bitcast(F32), ALU.subtract)
                        q_stage(gpj, gmid, (hf * (ATT * G1 + MLPG) + ag) * HPG)
                        for b in range(HB):
                            if b > 0:
                                split_p(b - 1, 0)
                                split_p(b - 1, 1)
                            keys1(b, 0)
                            if b > 0:
                                split_p(b - 1, 2)
                                split_p(b - 1, 3)
                            for h in range(1, HPG):
                                keys1(b, h)
                            if b > 0:
                                out1(b - 1)
                            values1(b, 0)
                            max1(b, 0)
                            max1(b, 1)
                            norm1(b, 0)
                            norm1(b, 1)
                            values1(b, 1)
                            max1(b, 2)
                            max1(b, 3)
                            norm1(b, 2)
                            norm1(b, 3)
                            values1(b, 2)
                        for h in range(HPG):
                            split_p(HB - 1, h)
                        out1(HB - 1)
                        out_stage(gpj, PJ_GU - HB)

                mlp = pjb + PJ_M
                dve.wait_ge(pj_free, mlp + PJ)
                ln_stage(mlp, 0, hf * 4 + 3, hf * NL + ATT, midb + MID_M, prm[:, PRM_LN + 16:PRM_LN + 24])
                with dve.Fori(0, MLPG) as m:
                    mpj = pjb + m * PJ_MU + (PJ_M + 6)
                    dve.wait_ge(pj_ready, mpj + 1)
                    dve.wait_ge(o_free, (hf + 1) * (ATT * G1 * HB) + 1)
                    nc.vector.tensor_copy(cur[:, 0:HPG], prm[:, bass.ds(m * HPG + PRM_B1, HPG)]).then_inc(cur_ready, 1)
                    q_stage(mpj, midb + m * HPG + (MID_M + HB), (hf * (ATT * G1 + MLPG) + m + ATT * G1) * HPG)
                    out_stage(mpj, HPG, pad=2)


def kernel(**inputs):
    import numpy as np
    import concourse.bacc as bacc
    from concourse.bass_utils import run_bass_kernel_spmd

    i = {k: np.asarray(v) for k, v in inputs.items()}
    L0, L1 = "L0_xattn_", "L1_xattn_"
    tokens = i["x"].reshape(B * L, D)

    def columns(v, n):
        return v.reshape(n, P).T

    def both(name):
        return np.stack([i[f"{L1}{name}1"], i[f"{L1}{name}2"]])

    def rep_kv(a):
        s = a.shape[:-1]
        return np.repeat(a.reshape(*s, 8, 1, HD0), 4, axis=-2).reshape(*s, D)

    heads = [both(n).reshape(ATT * G1, HPG, P) for n in ("bq", "bk", "bias_k", "bv")]
    per_group = np.stack(heads, axis=1).reshape(ATT * G1 * 16, P).T
    norms = [columns(i[L1 + n], DC) for n in
             ("ln1_scale", "ln1_offset", "ln2_scale", "ln2_offset", "ln_mlp_scale", "ln_mlp_offset")]
    per_chunk = np.stack([i[L0 + "bq"].reshape(C0, P), rep_kv(i[L0 + "bk"]).reshape(C0, P),
                          rep_kv(i[L0 + "bv"]).reshape(C0, P)], axis=1).reshape(C0 * 3, P).T
    prm = np.concatenate([per_group, *norms, columns(i[L1 + "b_fc1"], 16), per_chunk], axis=1)
    rows = np.concatenate([i[L0 + "bo"], i[L0 + "gamma"], i[L0 + "beta"], i[L1 + "bo1"], i[L1 + "bo2"],
                           i[L1 + "b_fc2"]]).reshape(1, 6 * D)
    arrays = {
        "x": tokens, "x_t": tokens.T, "ctx_t": i["ctx_2048"].transpose(2, 0, 1),
        "mask": i["mask_Bx1xSxS2_ff0"].reshape(B, L, S),
        "wq0": i[L0 + "Wq"], "wk0": rep_kv(i[L0 + "Wk"]), "wv0": i[L0 + "Wv"], "wo0": i[L0 + "Wo"],
        "wq": both("wq").reshape(ATT * D, NH1 * HD1), "wk": both("wk").reshape(ATT * D, NH1 * HD1),
        "wv": both("wv").reshape(ATT * D, NH1 * HD1), "wo": both("wo").reshape(ATT * NH1 * HD1, D),
        "w1": i[L1 + "w_fc1"], "w2": i[L1 + "w_fc2"],
        "bias_v": both("bias_v").reshape(ATT * G1, GW), "bv": both("bv").reshape(ATT * G1, GW),
        "prm": prm, "rows": rows,
    }
    nc = bacc.Bacc("TRN2", target_bir_lowering=False, num_devices=1)
    sent, args = {}, []
    for name, a in arrays.items():
        sent[f"in_{name}"] = np.ascontiguousarray(a)
        args.append(nc.dram_tensor(f"in_{name}", a.shape, mybir.dt.float32, kind="ExternalInput").ap())
    args.append(nc.dram_tensor("out", (B * L, D), mybir.dt.float32, kind="ExternalOutput").ap())
    xattn_program(nc, *args)
    r = run_bass_kernel_spmd(nc, [sent], core_ids=[0])
    return r.results[0]["out"].reshape(B, L, D)
```

```python
from contextlib import ExitStack

import concourse.bass as bass
from concourse import mybir

F32 = mybir.dt.float32
F32R = mybir.dt.float32r
ALU = mybir.AluOpType
ACT = mybir.ActivationFunctionType
AX_X = mybir.AxisListType.X

P = 128
B, L, S, D = 8, 112, 375, 512
HALVES = 2
HB = B // HALVES
T = HB * L
DC = D // P
SC = 3
KC = S // SC
SK = S + 1
NH0, HD0 = 32, 16
C0 = 4
HPC = NH0 // C0
KV2 = 2
ATT = 2
NH1, HD1 = 16, 128
G1 = 4
HPG = NH1 // G1
GW = HPG * HD1
MLPG = 4
SCALE0 = 0.25
SCALE1 = float(HD1) ** -0.5
EPS0, EPS1 = 1e-6, 1e-5

PJ, SCR, TP = 3, 2, 2

VT_UNIT = (0, 1, 3, 5)
V_UNIT = (2, 4, 6, 7)
PJ_P = 9
PJ_C = PJ_P + 12
PJ_CU = 15
PJ_W0 = PJ_C + C0 * PJ_CU
PJ_A = PJ_W0 + 6
PJ_GU = HPG + HB * (HPG + SC) + HB
PJ_AU = 6 + G1 * PJ_GU
PJ_M = PJ_A + ATT * PJ_AU
PJ_MU = 9
PJ_H = PJ_M + 6 + MLPG * PJ_MU

MID_P = 2 * HB
MID_C = MID_P + 2 + HPC // 2
MID_CU = 9
MID_A = MID_C + C0 * MID_CU
MID_GU = HPG + HB * (HPG + SC)
MID_AU = HB + G1 * MID_GU
MID_M = MID_A + ATT * MID_AU
MID_H = MID_M + HB + MLPG * HPG

CH_KEYS = {1: 0, 2: 1, 3: 3, 4: 4}
CH_Q, CH_PLACED = 2, 5
PR_Q, PR_KEYS, PR_PLACED = 0, 1, 2
SC_CU, SC_GU = HB * HPC, HB * HPG
SC_A = C0 * SC_CU + 4
SC_H = SC_A + ATT * G1 * SC_GU
TP_CU = HB * HPC + 2 * HB + HB
TP_A = C0 * TP_CU
TP_H = TP_A + ATT * G1 * SC_GU
TM_CU = TP_CU - 2 * HB
TM_A = C0 * TM_CU
TM_H = TM_A + ATT * G1 * SC_GU
O_CU = 2 * HB
O_A = C0 * O_CU
O_H = O_A + ATT * G1 * HB

C1 = C0 + 1
WQ_H = C1 + ATT * G1 + MLPG
WK_H = C1 + ATT * G1
WV_H = 1 + ATT * G1
WO_H = 1 + ATT * G1 + MLPG
RAW_X = 2
RAW_C = RAW_X + DC
RAW_W0 = RAW_C + 2 * C1
RAW_A = RAW_W0 + DC
RAW_GU = 4 * DC
RAW_M = RAW_A + ATT * G1 * RAW_GU
RAW_H = RAW_M + MLPG * 2 * DC
assert PJ_H % PJ == 0 and PJ_A % PJ == 0 and PJ_GU % PJ == 0 and PJ_MU % PJ == 0
assert RAW_C % 2 == 0 and RAW_W0 % 2 == 0

PRM_LN = ATT * G1 * 16
PRM_B1 = PRM_LN + 3 * 8
PRM_C = PRM_B1 + 16
PRM_N = PRM_C + 2 + C0 * 3
CUR_A = 1 + 2 * C0
CUR_H = CUR_A + ATT * G1 + MLPG
ST_H = (2 + ATT * G1) * HB
NL = ATT + 1


TP_ORDER = []
for n in range(HB * HPC):
    TP_ORDER.append(("probs", n))
    if n >= 9 and n % 4 == 1:
        TP_ORDER.append(("four", (n - 9) // 4))
    if n >= 14 and n % HPC == 6:
        TP_ORDER.append(("batch", (n - 14) // HPC))
TP_ORDER += [("four", 2 * HB - 2), ("four", 2 * HB - 1), ("batch", HB - 1)]
assert len(TP_ORDER) == TP_CU


def tp_unit(what, i):
    return TP_ORDER.index((what, i))


def tp_mid_unit(what, i):
    unit = tp_unit(what, i)
    return unit - sum(w == "four" for w, _ in TP_ORDER[:unit])


def xattn_program(nc, x, x_t, ctx_t, mask, wq0, wk0, wv0, wo0, wq, wk, wv, wo, w1, w2,
                  bias_v, bv, prm_in, rows_in, out):
    bv_hi_dram = nc.dram_tensor("bv_hi_scratch", (ATT * G1, GW), F32, kind="Internal").ap()
    bv_lo_dram = nc.dram_tensor("bv_lo_scratch", (ATT * G1, GW), F32, kind="Internal").ap()

    ctx_dram = nc.dram_tensor("ctx_copy", (D, B, S), F32, kind="Internal").ap()

    with ExitStack() as ctx:
        def sb(name, shape, dt=F32):
            return ctx.enter_context(nc.sbuf_tensor(name, shape, dt))

        def sem(name):
            return ctx.enter_context(nc.semaphore(name))

        ctx_hi = sb("ctx_hi", [P, DC, HB, SK], F32R)
        ctx_lo = sb("ctx_lo", [P, DC, HB, SK], F32R)
        h_hi = sb("h_hi", [P, DC, T], F32R)
        h_lo = sb("h_lo", [P, DC, T], F32R)
        qo_hi = sb("qo_hi", [P, 2 * HPG, T], F32R)
        qo_lo = sb("qo_lo", [P, 2 * HPG, T], F32R)
        k_hi = sb("k_hi", [P, HPG, SK], F32R)
        k_lo = sb("k_lo", [P, HPG, SK], F32R)
        v_hi = sb("v_hi", [P, SC * GW], F32R)
        v_lo = sb("v_lo", [P, SC * GW], F32R)
        probs = sb("probs", [P, HPG, 384])
        pt_hi = sb("pt_hi", [P, HPG, SC * L], F32R)
        pt_lo = sb("pt_lo", [P, HPG, SC * L], F32R)
        w_hi = {n: sb(f"w{n}_hi", [P, DC, GW], F32R) for n in "qkvo"}
        w_lo = {n: sb(f"w{n}_lo", [P, DC, GW], F32R) for n in "qkvo"}
        raw = sb("raw", [P, 2, GW])
        xacc = sb("xacc", [P, HB * D])
        ident = sb("ident", [P, P])
        o_nat = sb("o_nat", [P, HPC, HD0])
        prm = sb("prm", [P, PRM_N])
        cur = sb("cur", [P, 16])
        ln_cur = sb("ln_cur", [P, 8])
        neg_max = sb("neg_max", [P, HPC])
        row_sum = sb("row_sum", [P, 2, HPC])
        inv_sum = sb("inv_sum", [P, HPC])
        stats = sb("stats", [P, HB, 6])
        mean_var = sb("mean_var", [P, HB, 2])
        std = sb("std", [P, HB])
        rstd = sb("rstd", [P, HB])
        eps = sb("eps", [P, 2])

        probs_flat = probs[:].rearrange("p h n -> p (h n)")
        tmp = [probs_flat[:, 512 * i:512 * i + 512] for i in range(3)]
        xa = xacc[:].rearrange("p (b n) -> p b n", b=HB)
        mask_v = xacc[0:L, 0:HB * S].rearrange("p (b n) -> p b n", b=HB)
        vt = xacc[:, 1536:1536 + SK]
        q0_split = [qo_lo[:, e, :] for e in range(2)]
        place_sel = qo_lo[:].rearrange("p h n -> p (h n)")[:, 2 * T:2 * T + 2 * HPC * P].rearrange(
            "p (e j m) -> p e j m", e=2, j=HPC)
        o_t = xacc[0:32, 1536:1536 + T]
        pt0 = [[pt_hi[:], pt_lo[:]],
               [w["k"][:].rearrange("p c n -> p (c n)")[:, 512:512 + 4 * SC * L].rearrange(
                   "p (h n) -> p h n", h=4) for w in (w_hi, w_lo)]]
        k0 = [k_hi[:, 0, :], k_lo[:, 0, :]]
        v0 = [v[:].rearrange("p (n d) -> p n d", d=P) for v in (v_hi, v_lo)]
        v1 = [v[:].rearrange("p (c n) -> p c n", c=SC) for v in (v_hi, v_lo)]
        v0c = k_hi[:].rearrange("p h n -> p (h n)")[:, SK:SK + 768].rearrange(
            "p (n k e) -> p n k e", k=KV2, e=2 * HD0)
        wv_flat = [w["v"][:].rearrange("p c n -> p (c n)") for w in (w_hi, w_lo)]
        ot0 = [w[:, 0:C0 * T].rearrange("p (c t) -> p c t", c=C0) for w in wv_flat]
        flat = {n: [w[n][:].rearrange("p c n -> p (c n)") for w in (w_hi, w_lo)] for n in "qkvo"}

        pj = [ctx.enter_context(nc.psum_tensor(f"pj{i}", [P, 512], F32)) for i in range(PJ)]
        scores = [ctx.enter_context(nc.psum_tensor(f"scores{i}", [P, 512], F32)) for i in range(SCR)]
        tp = [ctx.enter_context(nc.psum_tensor(f"tp{i}", [P, 512], F32)) for i in range(TP)]
        o_ps = ctx.enter_context(nc.psum_tensor("o_ps", [P, 512], F32))

        pj_ready, pj_mid, pj_free = sem("pj_ready"), sem("pj_mid"), sem("pj_free")
        sc_ready = sem("sc_ready")
        tp_ready, tp_mid, tp_free = sem("tp_ready"), sem("tp_mid"), sem("tp_free")
        o_ready, o_mid, o_free = sem("o_ready"), sem("o_mid"), sem("o_free")
        max_ready, exp_ready = sem("max_ready"), sem("exp_ready")
        inv_ready, norm_ready = sem("inv_ready"), sem("norm_ready")
        raw_ready = [sem("raw_ready0"), sem("raw_ready1")]
        raw_free = [sem("raw_free0"), sem("raw_free1")]
        split_hi = sem("split_hi")
        w_ready = {n: sem(f"w{n}_ready") for n in "qkvo"}
        w_free = {n: sem(f"w{n}_free") for n in "qkvo"}
        tok_ready, ctx_ready = sem("tok_ready"), sem("ctx_ready")
        ctx_hi_ready = sem("ctx_hi_ready")
        ctx_in = [sem(f"ctx_in{b}") for b in range(HB)]
        ctx_copied = [sem(f"ctx_copied{b}") for b in range(HB + 1)]
        cur_ready, sel_zero, sel_ready = sem("cur_ready"), sem("sel_zero"), sem("sel_ready")
        v0c_ready, kbias_hi = sem("v0c_ready"), sem("kbias_hi")
        o_inv, o_nat_ready = sem("o_inv"), sem("o_nat_ready")
        qh_done = sem("qh_done")
        ln_chain, std_ready, xn_ready, ln_t, ln_par = (
            sem("ln_chain"), sem("std_ready"), sem("xn_ready"), sem("ln_t"), sem("ln_par"))
        post_ln, bias_added, stats_ready = sem("post_ln"), sem("bias_added"), sem("stats_ready")
        mask_in, x_in, rows_ready, bvrow_in, out_done = (
            sem("mask_in"), sem("x_in"), sem("rows_ready"), sem("bvrow_in"), sem("out_done"))
        setup_dma, setup_dve, setup_pool, setup_bv = (
            sem("setup_dma"), sem("setup_dve"), sem("setup_pool"), sem("setup_bv"))

        pool_passed, dve_passed, pe_passed, sp_passed, act_passed = (
            sem("pool_passed"), sem("dve_passed"), sem("pe_passed"), sem("sp_passed"), sem("act_passed"))

        def load_ctx(engine, half, b):
            engine.dma_start(ctx_lo[:, :, b, 0:S].bitcast(F32),
                             ctx_dram[:, bass.ds(half * HB + b, 1), :].rearrange(
                                 "(c p) b n -> p c (b n)", p=P)).then_inc(ctx_in[b], 16)

        block = ctx.enter_context(nc.Block())

        @block.sync
        def _(sp):
            sp.dma_start(prm[:], prm_in).then_inc(setup_dma, 16)
            sp.dma_start(xa[0:ATT * G1, 0, :], bias_v).then_inc(setup_dma, 16)
            sp.dma_start(xa[0:ATT * G1, 1, :], bv).then_inc(setup_dma, 16)

            def load(half_use, n, src, shape):
                slot = n % 2
                dst = raw[:, slot, 0:shape[0] * shape[1]]
                if shape[0] > 1:
                    dst = dst.rearrange("p (c n) -> p c n", c=shape[0])
                sp.wait_ge(raw_free[slot], half_use + n // 2 + 1)
                sp.dma_start(dst, src).then_inc(raw_ready[slot], 16)

            with sp.Fori(0, HALVES) as hf:
                base = hf * (RAW_H // 2)
                for i in range(2):
                    load(base, i, wv0[2 * i * P:(2 * i + 2) * P, :].rearrange(
                        "(c p) n -> p c n", p=P), (2, P))
                for c in range(DC):
                    load(base, RAW_X + c, x_t[c * P:(c + 1) * P, bass.ds(hf * T, T)], (1, T))
                sp.wait_ge(out_done, hf * 16 + 16)
                sp.dma_start(mask_v, mask[bass.ds(hf * HB, HB), :, :].rearrange("b p n -> p b n")).then_inc(mask_in, 16)
                sp.dma_start(ctx_dram[:, bass.ds((1 - hf) * HB, HB), :],
                             ctx_t[:, bass.ds((1 - hf) * HB, HB), :]).then_inc(ctx_copied[HB], 16)
                with sp.Fori(0, C1) as c:
                    cb = base + RAW_C // 2 + c
                    load(cb, 0, wq0[:, bass.ds(c * P, P)].rearrange("(c p) n -> p c n", p=P), (DC, P))
                    load(cb, 1, wk0[:, bass.ds(c * P, P)].rearrange("(c p) n -> p c n", p=P), (DC, P))
                for c in range(DC):
                    load(base, RAW_W0 + c, wo0[c * P:(c + 1) * P, :], (1, GW))
                with sp.Fori(0, ATT) as a:
                    with sp.Fori(0, G1) as g:
                        gb = base + RAW_A // 2 + (a * G1 + g) * (RAW_GU // 2)
                        for i, w in enumerate((wq, wk, wv)):
                            for c in range(DC):
                                load(gb, DC * i + c,
                                     w[bass.ds(a * D + c * P, P), bass.ds(g * GW, GW)], (1, GW))
                        for c in range(DC):
                            load(gb, 3 * DC + c,
                                 wo[bass.ds((a * G1 + g) * GW + c * P, P), :], (1, GW))
                sp.wait_ge(ctx_copied[HB], hf * 16 + 16)
                sp.wait_ge(o_ready, hf * O_H + O_H)
                sp.sem_inc(sp_passed, 1)
                for b in range(HB):
                    load_ctx(sp, 1 - hf, b)
                with sp.Fori(0, MLPG) as m:
                    mb = base + RAW_M // 2 + m * DC
                    for c in range(DC):
                        load(mb, c, w1[c * P:(c + 1) * P, bass.ds(m * GW, GW)], (1, GW))
                    for c in range(DC):
                        load(mb, DC + c, w2[bass.ds(m * GW + c * P, P), :], (1, GW))
            sp.wait_ge(ctx_copied[HB], 16 * HALVES)
            for s in ctx_in:
                sp.wait_ge(s, 16 * (HALVES + 1))
            sp.wait_ge(out_done, 16 * (HALVES + 1))

        @block.gpsimd
        def _(pool):
            nc.gpsimd.memset(ident[:], 0.0).then_inc(setup_pool, 1)
            nc.gpsimd.memset(eps[:, 0:1], EPS0)
            nc.gpsimd.memset(eps[:, 1:2], EPS1)
            nc.gpsimd.memset(ctx_hi[:, :, :, S:SK].bitcast(F32), 0.0)
            nc.gpsimd.memset(ctx_lo[:, :, :, S:SK].bitcast(F32), 0.0)
            pool.wait_ge(setup_pool, 1)
            nc.gpsimd.affine_select(out=ident[:], in_=ident[:], compare_op=ALU.not_equal, fill=1.0,
                                    base=0, pattern=[[-1, P]], channel_multiplier=1).then_inc(setup_pool, 1)
            for s in raw_free:
                pool.sem_inc(s, 1)

            def split(half_base, n, shape, hi, lo, signal, k):
                slot = n % 2
                src = raw[:, slot, 0:shape[0] * shape[1]]
                if shape[0] > 1:
                    src = src.rearrange("p (c n) -> p c n", c=shape[0])
                pool.wait_ge(raw_ready[slot], (half_base + (n // 2 + 1)) * 16)
                pool.sem_inc(pool_passed, 1)
                nc.gpsimd.tensor_scalar(hi, src, 1.0, 0.0, ALU.mult, ALU.add).then_inc(split_hi, 1)
                pool.wait_ge(split_hi, half_base * 2 + n + 1)
                nc.gpsimd.tensor_tensor(lo, src, hi.bitcast(F32), ALU.subtract).then_inc(signal, k)
                return slot

            def split_free(half_base, n, shape, hi, lo, signal, k, done):
                slot = split(half_base, n, shape, hi, lo, signal, k)
                pool.wait_ge(signal, done)
                pool.sem_inc(raw_free[slot], 1)

            def weights(half_base, n0, name, use, pieces=DC):
                pool.wait_ge(w_free[name], use + 1)
                for c in range(pieces):
                    if pieces == DC:
                        hi, lo, shape = w_hi[name][:, c, :], w_lo[name][:, c, :], (1, GW)
                    else:
                        wd = DC // pieces * P
                        hi, lo = (f[:, wd * c:wd * c + wd].rearrange("p (c n) -> p c n", n=P)
                                  for f in flat[name])
                        shape = (DC // pieces, P)
                    k = DC // pieces
                    split_free(half_base, n0 + c, shape, hi, lo, w_ready[name], k,
                               use * DC + k * (c + 1))

            with pool.Fori(0, HALVES) as hf:
                base = hf * (RAW_H // 2)
                weights(base, 0, "v", hf * WV_H, pieces=2)
                pool.wait_ge(pj_free, hf * PJ_H + PJ)
                for c in range(DC):
                    split_free(base, RAW_X + c, (1, T), h_hi[:, c, :], h_lo[:, c, :], tok_ready, 1,
                               hf * DC + c + 1)
                with pool.Fori(0, C1) as c:
                    weights(base + RAW_C // 2 + c, 0, "q", hf * WQ_H + c, pieces=1)
                    weights(base + RAW_C // 2 + c, 1, "k", hf * WK_H + c, pieces=1)
                weights(base, RAW_W0, "o", hf * WO_H)
                with pool.Fori(0, ATT) as a:
                    with pool.Fori(0, G1) as g:
                        gb = base + RAW_A // 2 + (a * G1 + g) * (RAW_GU // 2)
                        weights(gb, 0, "q", hf * WQ_H + C1 + a * G1 + g)
                        weights(gb, DC, "k", hf * WK_H + C1 + a * G1 + g)
                        weights(gb, 2 * DC, "v", hf * WV_H + 1 + a * G1 + g)
                        weights(gb, 3 * DC, "o", hf * WO_H + 1 + a * G1 + g)
                with pool.Fori(0, MLPG) as m:
                    mb = base + RAW_M // 2 + m * DC
                    weights(mb, 0, "q", hf * WQ_H + C1 + ATT * G1 + m)
                    weights(mb, DC, "o", hf * WO_H + 1 + ATT * G1 + m)

        @block.tensor
        def _(pe):
            def three(dst, lhs, rhs, first, last):
                (l_hi, l_lo), (r_hi, r_lo) = lhs, rhs
                nc.tensor.matmul(dst, l_hi, r_hi, start=first, stop=False)
                nc.tensor.matmul(dst, l_hi, r_lo, start=False, stop=False)
                return nc.tensor.matmul(dst, l_lo, r_hi, start=False, stop=last)

            def transpose(dst, src, parts):
                return nc.tensor.transpose(dst, src, ident[0:parts, 0:parts])

            def q_stage(base, use, unit):
                for h in range(HPG):
                    pe.wait_ge(pj_free, base + unit + h + 1)
                    for c in range(DC):
                        if h == 0:
                            pe.wait_ge(w_ready["q"], use * DC + c + 1)
                        last = three(pj[(unit + h) % PJ][:, 0:T],
                                     [w["q"][:, c, h * P:(h + 1) * P] for w in (w_hi, w_lo)],
                                     (h_hi[:, c, :], h_lo[:, c, :]), c == 0, c == DC - 1)
                    last.then_inc(pj_ready, 1)

            def out_part(base, use, unit, b, src, ready=None, pad=1):
                pe.wait_ge(pj_free, base + unit + b + 1)
                for h in range(HPG):
                    if b == 0:
                        pe.wait_ge(w_ready["o"], use * DC + h + 1)
                        if ready is not None:
                            ready(h)
                    last = three(pj[(unit + b) % PJ][0:L, :],
                                 [s[:, h, b * L:(b + 1) * L] for s in src],
                                 (w_hi["o"][:, h, :], w_lo["o"][:, h, :]), h == 0, h == HPG - 1)
                last.then_inc(pj_ready, pad if b == HB - 1 else 1)

            def ln_stage(base, unit, nl):
                for b in range(HB):
                    pe.wait_ge(xn_ready, nl * HB + b + 1)
                    pe.wait_ge(pj_free, base + unit + b + 1)
                    for c in range(DC):
                        last = transpose(pj[(unit + b) % PJ][:, c * L:(c + 1) * L],
                                         tmp[0][0:L, c * P:(c + 1) * P], L)
                    last.then_inc(pj_ready, 3 if b == HB - 1 else 1)

            pe.wait_ge(setup_dve, 1)
            with pe.Fori(0, HALVES) as hf:
                pjb = hf * PJ_H
                def values_t(b):
                    unit = VT_UNIT[b]
                    pe.wait_ge(ctx_ready, hf * HB + b + 1)
                    pe.wait_ge(pj_free, pjb + unit + 1)
                    if b == 0:
                        pe.wait_ge(w_ready["v"], hf * WV_H * DC + DC)
                    for c in range(DC):
                        last = three(pj[unit % PJ][:, 0:SK], [f[:, c * P:(c + 1) * P] for f in flat["v"]],
                                     (ctx_hi[:, c, b, :], ctx_lo[:, c, b, :]), c == 0, c == DC - 1)
                    last.then_inc(pj_ready, 1)

                def values(b):
                    unit = V_UNIT[b]
                    pe.wait_ge(pj_mid, hf * MID_H + 2 * b + 1)
                    pe.wait_ge(pj_free, pjb + unit + 1)
                    pe.sem_inc(pe_passed, 1)
                    for s in range(SC):
                        last = transpose(pj[unit % PJ][0:KC, s * P:(s + 1) * P],
                                         vt[:, s * KC:(s + 1) * KC], P)
                    last.then_inc(pj_ready, 2 if b == HB - 1 else 1)

                values_t(0)
                for b in range(HB):
                    if b + 1 < HB:
                        values_t(b + 1)
                    values(b)
                pe.wait_ge(tok_ready, hf * DC + DC)
                pe.sem_inc(pe_passed, 1)

                def queries0(base, unit, use, chunks):
                    if chunks[0] == 0:
                        pe.wait_ge(pj_free, base + unit + 1)
                        pe.wait_ge(w_ready["q"], use * DC + DC)
                    for c in chunks:
                        last = three(pj[unit % PJ][:, 0:T], [f[:, c * P:(c + 1) * P] for f in flat["q"]],
                                     (h_hi[:, c, :], h_lo[:, c, :]), c == 0, c == DC - 1)
                    if chunks[-1] == DC - 1:
                        last.then_inc(pj_ready, 1)

                def keys0(base, unit, use, b, chunks):
                    if chunks[0] == 0:
                        pe.wait_ge(pj_free, base + unit + 1)
                        pe.wait_ge(w_ready["k"], use * DC + DC)
                    for c in chunks:
                        last = three(pj[unit % PJ][:, 0:SK], [f[:, c * P:(c + 1) * P] for f in flat["k"]],
                                     (ctx_hi[:, c, b, :], ctx_lo[:, c, b, :]), c == 0, c == DC - 1)
                    if chunks[-1] == DC - 1:
                        last.then_inc(pj_ready, 1)

                def place(base, q, unit, j):
                    if j == 0:
                        pe.wait_ge(pj_free, base + q + 1 + PJ)
                    pe.wait_ge(pj_free, base + unit + 1)
                    for e in range(2):
                        last = nc.tensor.matmul(pj[unit % PJ][:, 0:T], place_sel[:, e, j, :],
                                                q0_split[e], start=(e == 0), stop=(e == 1))
                    last.then_inc(pj_ready, 3 if j == HPC - 1 else 1)

                def scores0(csc, n):
                    b, j = n // HPC % HB, n % HPC
                    pe.wait_ge(max_ready, csc + n + 1)
                    nc.tensor.matmul(scores[n % SCR][0:L, 0:SK], qo_hi[:, j, b * L:(b + 1) * L],
                                     k0[b % 2], start=True, stop=True).then_inc(sc_ready, 1)

                ppj = pjb + PJ_P
                queries0(ppj, PR_Q, hf * WQ_H, range(DC))
                keys0(ppj, PR_KEYS, hf * WK_H, 0, range(DC))
                pe.wait_ge(sel_ready, hf * 8 + 8)
                for j in range(4):
                    place(ppj, PR_Q, PR_PLACED + j, j)
                for n in range(4):
                    pe.wait_ge(pj_free, ppj + PR_PLACED + n + 1 + PJ)
                    scores0(hf * SC_H, n)
                    place(ppj, PR_Q, PR_PLACED + 4 + n, 4 + n)

                with pe.Fori(0, C0) as c8:
                    cpj = pjb + c8 * PJ_CU + PJ_C
                    csc = hf * SC_H + c8 * SC_CU
                    ctp = hf * TP_H + c8 * TP_CU
                    co = hf * O_H + c8 * O_CU

                    def transpose0(n):
                        unit = tp_unit("probs", n)
                        pe.wait_ge(exp_ready, csc + n + 1 + SCR)
                        pe.wait_ge(tp_free, ctp + unit + 1)
                        for s in range(SC):
                            last = transpose(tp[unit % TP][0:KC, s * L:(s + 1) * L],
                                             probs[0:L, n % 4, s * KC:(s + 1) * KC], L)
                        last.then_inc(tp_ready, 1)

                    def weigh0(u, s):
                        if u == 0:
                            pe.wait_ge(v0c_ready, (hf * C0 + c8) * 2 + 2)
                        if s == 0:
                            pe.wait_ge(tp_free, ctp + tp_unit("probs", 4 * u + 3) + 1 + TP)
                        v = v0c[0:KC, u // 2 * SC + s, u % 2, :]
                        p_hi, p_lo = (t[0:KC, :, s * L:(s + 1) * L] for t in pt0[u % 2])
                        nc.tensor.matmul(o_ps[0:32, 0:T], v, p_hi, start=(s == 0), stop=False)
                        last = nc.tensor.matmul(o_ps[0:HD0, 0:T], v[:, 0:HD0], p_lo, start=False,
                                                stop=(s == SC - 1))
                        if s == SC - 1:
                            last.then_inc(o_ready, 1)

                    def four_transpose0(u):
                        unit = tp_unit("four", u)
                        pe.wait_ge(o_mid, co + u + 1)
                        pe.wait_ge(tp_free, ctp + unit + 1)
                        pe.sem_inc(pe_passed, 1)
                        for h in range(4):
                            last = transpose(tp[unit % TP][0:L, 32 * h:32 * h + 32],
                                             o_t[:, h * L:(h + 1) * L], 32)
                        last.then_inc(tp_ready, 1)

                    def out_transpose0(b):
                        unit = tp_unit("batch", b)
                        pe.wait_ge(o_nat_ready, (hf * C0 + c8) * HB + b + 1)
                        pe.wait_ge(tp_free, ctp + unit + 1)
                        transpose(tp[unit % TP][:, 0:L],
                                  o_nat[0:L, :, :].rearrange("p h d -> p (h d)"), L).then_inc(tp_ready, 1)

                    for n in range(SC_CU):
                        b, j = n // HPC, n % HPC
                        transpose0(n)
                        if n == 0:
                            pe.wait_ge(pj_free, cpj + PJ)
                        elif j == 4:
                            pe.wait_ge(pj_free, cpj + CH_KEYS[b + 1] + 1 + PJ)
                        if n >= SC_CU - 4:
                            pe.wait_ge(pj_free, cpj + CH_PLACED + n - (SC_CU - 4) + 1 + PJ)
                        scores0(csc, n + 4)
                        if j < 2:
                            keys0(cpj, CH_KEYS[b + 1], hf * WK_H + c8 + (b + 1) // HB, (b + 1) % HB,
                                  (2 * j, 2 * j + 1))
                        if n // 4 == 3:
                            queries0(cpj, CH_Q, hf * WQ_H + c8 + 1, (n % 4,))
                        if n >= 9 and n % 4 == 1:
                            four_transpose0((n - 9) // 4)
                        if n >= 5 and n % 4 >= 1:
                            weigh0(n // 4 - 1, n % 4 - 1)
                        if n >= 26:
                            place(cpj, CH_Q, CH_PLACED + n - 26, n - 26)
                        if n >= 14 and j == 6:
                            out_transpose0((n - 14) // HPC)
                    place(cpj, CH_Q, CH_PLACED + 6, 6)
                    four_transpose0(2 * HB - 2)
                    for s in range(SC):
                        weigh0(2 * HB - 1, s)
                    place(cpj, CH_Q, CH_PLACED + 7, 7)
                    four_transpose0(2 * HB - 1)
                    out_transpose0(HB - 1)

                pe.wait_ge(tp_free, hf * TP_H + TP_A + TP)
                for b in range(HB):
                    out_part(pjb + PJ_W0, hf * WO_H, 0, b, ot0, pad=3)

                with pe.Fori(0, ATT) as a:
                    apj = pjb + a * PJ_AU + PJ_A
                    ln_stage(apj, 0, hf * NL + a)
                    pe.wait_ge(pj_free, apj + 6 + PJ)
                    pe.sem_inc(pe_passed, 1)
                    with pe.Fori(0, G1) as g:
                        ag = a * G1 + g
                        gpj = apj + g * PJ_GU + 6
                        gsc = hf * SC_H + ag * SC_GU + SC_A
                        gtp = hf * TP_H + ag * SC_GU + TP_A
                        gof = (hf * ATT * G1 + ag) * HB
                        use_k, use_v = hf * WK_H + ag + C1, hf * WV_H + ag + 1

                        def keys1(b, h):
                            unit = HPG + b * (HPG + SC) + h
                            pe.wait_ge(pj_free, gpj + unit + 1)
                            for c in range(DC):
                                if b == 0 and h == 0:
                                    pe.wait_ge(w_ready["k"], use_k * DC + c + 1)
                                last = three(pj[unit % PJ][:, 0:SK],
                                             [w["k"][:, c, h * P:(h + 1) * P] for w in (w_hi, w_lo)],
                                             (ctx_hi[:, c, b, :], ctx_lo[:, c, b, :]),
                                             c == 0, c == DC - 1)
                            last.then_inc(pj_ready, 1)

                        def values1(b, s):
                            unit = HPG + b * (HPG + SC) + HPG + s
                            pe.wait_ge(pj_free, gpj + unit + 1)
                            for c in range(DC):
                                if b == 0 and s == 0:
                                    pe.wait_ge(w_ready["v"], use_v * DC + c + 1)
                                last = three(pj[unit % PJ][0:KC, :],
                                             [t[:, c, b, s * KC:(s + 1) * KC] for t in (ctx_hi, ctx_lo)],
                                             (w_hi["v"][:, c, :], w_lo["v"][:, c, :]),
                                             c == 0, c == DC - 1)
                            last.then_inc(pj_ready, 1)

                        def scores1(b, h):
                            n = b * HPG + h
                            if h == 0:
                                pe.wait_ge(pj_free, gpj + HPG + b * (HPG + SC) + HPG + PJ)
                            pe.wait_ge(exp_ready, gsc + n + 1)
                            three(scores[n % SCR][0:L, 0:SK],
                                  [q[:, h, b * L:(b + 1) * L] for q in (qo_hi, qo_lo)],
                                  (k_hi[:, h, :], k_lo[:, h, :]), True, True).then_inc(sc_ready, 1)

                        def transpose1(b, h):
                            n = b * HPG + h
                            pe.wait_ge(norm_ready, (hf * ATT * G1 + ag) * SC_GU + n + 1)
                            pe.wait_ge(tp_free, gtp + n + 1)
                            for s in range(SC):
                                last = transpose(tp[n % TP][0:KC + 1, s * L:(s + 1) * L],
                                                 probs[0:L, h, s * KC:(s + 1) * KC + 1], L)
                            last.then_inc(tp_ready, 1)

                        def weigh1(b):
                            if b == 0:
                                pe.wait_ge(bvrow_in, (hf * ATT * G1 + ag) * 32 + 32)
                            pe.wait_ge(pj_free, gpj + HPG + (b + 1) * (HPG + SC) + PJ)
                            pe.wait_ge(o_free, gof + b + 1)
                            for h in range(HPG):
                                pe.wait_ge(tp_free, gtp + b * HPG + h + 1 + TP)
                                for s in range(SC):
                                    n = KC + 1 if s == SC - 1 else KC
                                    last = three(o_ps[:, h * L:(h + 1) * L],
                                                 [v[0:n, s, h * P:(h + 1) * P] for v in v1],
                                                 [q[0:n, h, s * L:(s + 1) * L] for q in (pt_hi, pt_lo)],
                                                 s == 0, s == SC - 1)
                            last.then_inc(o_ready, 1)

                        q_stage(gpj, hf * WQ_H + ag + C1, 0)
                        for b in range(HB):
                            if b > 0:
                                transpose1(b - 1, 0)
                                transpose1(b - 1, 1)
                            keys1(b, 0)
                            if b > 0:
                                transpose1(b - 1, 2)
                                transpose1(b - 1, 3)
                            for h in range(1, HPG):
                                keys1(b, h)
                            if b > 0:
                                weigh1(b - 1)
                            values1(b, 0)
                            scores1(b, 0)
                            scores1(b, 1)
                            values1(b, 1)
                            scores1(b, 2)
                            scores1(b, 3)
                            values1(b, 2)

                        def out1(b):
                            pe.wait_ge(o_free, gof + b + 2)
                            out_part(gpj, hf * WO_H + ag + 1, PJ_GU - HB, b,
                                     [q[:, HPG:2 * HPG, :] for q in (qo_hi, qo_lo)])

                        transpose1(HB - 1, 0)
                        transpose1(HB - 1, 1)
                        out1(0)
                        transpose1(HB - 1, 2)
                        transpose1(HB - 1, 3)
                        out1(1)
                        weigh1(HB - 1)
                        out1(2)
                        out1(3)

                ln_stage(pjb + PJ_M, 0, hf * NL + ATT)
                pe.wait_ge(pj_free, pjb + PJ_M + 6 + PJ)
                pe.sem_inc(pe_passed, 1)
                with pe.Fori(0, MLPG) as m:
                    mpj = pjb + m * PJ_MU + (PJ_M + 6)
                    q_stage(mpj, hf * WQ_H + m + (C1 + ATT * G1), 0)

                    def ready2(h):
                        pe.wait_ge(pj_free, mpj + h + 1 + PJ)
                    for b in range(HB):
                        out_part(mpj, hf * WO_H + m + (1 + ATT * G1), HPG, b,
                                 [q[:, 0:HPG, :] for q in (qo_hi, qo_lo)], ready2, pad=2)

        @block.scalar
        def _(act):
            def move(dst, src, ready, n, bias=None, mid=None):
                act.wait_ge(ready, n)
                if bias is None:
                    i = nc.scalar.activation(dst, src, ACT.Copy)
                else:
                    i = nc.scalar.activation(dst, src, ACT.Identity, bias=bias)
                if mid is not None:
                    i.then_inc(mid, 1)

            def ln_std(nn, which):
                act.wait_ge(ln_chain, nn * 5 + 4)
                nc.scalar.activation(std[0:L, :], mean_var[0:L, :, 1], ACT.Sqrt,
                                     bias=eps[0:L, which:which + 1]).then_inc(std_ready, 1)

            def ln_stage(nl):
                for b in range(HB):
                    act.wait_ge(ln_t, (nl * HB + b + 1) * 4)
                    nc.scalar.activation(h_hi[:, :, b * L:(b + 1) * L],
                                         tmp[1][:, 0:T].rearrange("p (c l) -> p c l", c=DC),
                                         ACT.Copy).then_inc(pj_mid, 1)

            for s in w_free.values():
                act.sem_inc(s, 1)
            for b in range(HB + 1):
                if b < HB:
                    act.dma_start(ctx_dram[:, b, :], ctx_t[:, b, :]).then_inc(ctx_copied[b], 16)
                if b > 0:
                    act.wait_ge(ctx_copied[b - 1], 16)
                    load_ctx(act, 0, b - 1)
            act.wait_ge(setup_bv, 3)
            act.dma_start(bv_hi_dram, pt_hi[:].rearrange("p h n -> p (h n)")[0:8, 0:GW].bitcast(F32)).then_inc(setup_dma, 16)
            act.dma_start(bv_lo_dram, pt_lo[:].rearrange("p h n -> p (h n)")[0:8, 0:GW].bitcast(F32)).then_inc(setup_dma, 16)
            act.sem_inc(out_done, 16)

            def split_ctx(half):
                for b in range(HB):
                    act.wait_ge(ctx_in[b], half * 16 + 16)
                    nc.scalar.activation(ctx_hi[:, :, b, 0:S], ctx_lo[:, :, b, 0:S].bitcast(F32),
                                         ACT.Copy).then_inc(ctx_hi_ready, 1)

            split_ctx(0)
            with act.Fori(0, HALVES) as hf:
                pjb = hf * PJ_H

                act.wait_ge(out_done, hf * 16 + 16)
                act.sem_inc(act_passed, 1)
                for b in range(HB):
                    move(vt, pj[VT_UNIT[b] % PJ][:, 0:SK], pj_ready, pjb + VT_UNIT[b] + 1, mid=pj_mid)
                    move(v0[0][0:KC, b * SC:(b + 1) * SC, :],
                         pj[V_UNIT[b] % PJ][0:KC, 0:SC * P].rearrange("p (s n) -> p s n", s=SC),
                         pj_ready, pjb + V_UNIT[b] + 1, mid=pj_mid)

                def queries0(base, unit):
                    act.wait_ge(pj_ready, base + unit + 1)
                    act.sem_inc(w_free["q"], 1)
                    nc.scalar.activation(q0_split[0], pj[unit % PJ][:, 0:T], ACT.Identity,
                                         bias=cur[:, 1:2]).then_inc(pj_mid, 1)

                def keys0(base, unit, b):
                    move(k0[b % 2], pj[unit % PJ][:, 0:SK], pj_ready, base + unit + 1,
                         bias=cur[:, 2:3], mid=pj_mid)

                def placed(base, unit, j):
                    move(qo_hi[:, j, :], pj[unit % PJ][:, 0:T], pj_ready, base + unit + 1, mid=pj_mid)

                def exps0(csc, n):
                    b, j, h = n // HPC, n % HPC, n % 4
                    act.wait_ge(max_ready, csc + n + 1 + SCR)
                    nc.scalar.activation(probs[0:L, h, 0:S], probs[0:L, h, 0:S], ACT.Exp,
                                         bias=neg_max[0:L, j:j + 1], scale=-1.0,
                                         accum_out=row_sum[0:L, b % 2, j:j + 1]).then_inc(exp_ready, 1)

                ppj = pjb + PJ_P
                act.wait_ge(setup_dma, 80)
                act.sem_inc(act_passed, 1)
                act.wait_ge(cur_ready, hf * CUR_H + 1)
                queries0(ppj, PR_Q)
                keys0(ppj, PR_KEYS, 0)
                placed(ppj, PR_PLACED + 1, 1)
                placed(ppj, PR_PLACED + 3, 3)
                exps0(hf * SC_H, 0)
                placed(ppj, PR_PLACED + 5, 5)
                exps0(hf * SC_H, 1)
                placed(ppj, PR_PLACED + 7, 7)
                exps0(hf * SC_H, 2)
                with act.Fori(0, C0) as c8:
                    cpj = pjb + c8 * PJ_CU + PJ_C
                    csc = hf * SC_H + c8 * SC_CU
                    ctp = hf * TP_H + c8 * TP_CU
                    co = hf * O_H + c8 * O_CU

                    def out0(b):
                        unit = tp_unit("batch", b)
                        act.wait_ge(tp_ready, ctp + unit + 1)
                        nc.scalar.activation(
                            ot0[0][:, bass.ds(c8, 1), b * L:(b + 1) * L].rearrange("p c l -> p (c l)"),
                            tp[unit % TP][:, 0:L], ACT.Identity, bias=cur[:, 0:1]).then_inc(tp_mid, 1)

                    def outputs(u):
                        move(o_t, o_ps[0:32, 0:T], o_ready, co + u + 1, mid=o_mid)

                    for n in range(SC_CU):
                        b, j, unit = n // HPC, n % HPC, tp_unit("probs", n)
                        if n >= 8 and n % 4 == 0:
                            outputs((n - 8) // 4)
                        move(pt0[n // 4 % 2][0][0:KC, n % 4, :], tp[unit % TP][0:KC, 0:SC * L], tp_ready,
                             ctp + unit + 1, mid=tp_mid)
                        exps0(csc, n + 3)
                        if j == 1:
                            if b == HB - 1:
                                act.wait_ge(cur_ready, hf * CUR_H + 2 * c8 + 3)
                            keys0(cpj, CH_KEYS[b + 1], b + 1)
                            if b == HB - 2:
                                act.sem_inc(w_free["k"], 1)
                        if n == 15:
                            act.wait_ge(cur_ready, hf * CUR_H + 2 * c8 + 2)
                            queries0(cpj, CH_Q)
                        if n == SC_CU - 1:
                            outputs(2 * HB - 2)
                        if n in (27, 29, 31):
                            placed(cpj, CH_PLACED + n - 26, n - 26)
                        if n >= 14 and j == 6:
                            out0((n - 14) // HPC)
                    outputs(2 * HB - 1)
                    placed(cpj, CH_PLACED + 7, 7)
                    out0(HB - 1)
                exps0(hf * SC_H, SC_A - 1)
                act.sem_inc(w_free["k"], 1)
                act.wait_ge(exp_ready, hf * SC_H + SC_A + SCR)
                act.dma_start(xa[0:L, :, :], x[bass.ds(hf * T, T), :].rearrange("(b p) n -> p b n", p=L)).then_inc(x_in, 16)
                act.dma_start(probs_flat[0:L, :], rows_in[0:1, 0:3 * D].partition_broadcast(L)).then_inc(rows_ready, 16)
                ln_std(hf * 4, 0)

                with act.Fori(0, ATT) as a:
                    apj = pjb + a * PJ_AU + PJ_A
                    act.wait_ge(post_ln, hf * 2 * HB + 2 * HB)
                    act.dma_start(tmp[2][0:L, :], rows_in[0:1, bass.ds((a + 3) * D, D)].partition_broadcast(L)).then_inc(rows_ready, 16)
                    ln_std(hf * 4 + a + 1, 1)
                    ln_stage(hf * NL + a)
                    with act.Fori(0, G1) as g:
                        ag = a * G1 + g
                        gpj = apj + g * PJ_GU + 6
                        gsc = hf * SC_H + ag * SC_GU + SC_A
                        gtp = hf * TP_H + ag * SC_GU + TP_A
                        go = hf * O_H + ag * HB + O_A
                        gg = hf * ATT * G1 + ag

                        def values1(b, s):
                            unit = HPG + b * (HPG + SC) + HPG + s
                            move(v1[0][0:KC, s, :], pj[unit % PJ][0:KC, :], pj_ready, gpj + unit + 1,
                                 mid=pj_mid)
                            if b == HB - 1 and s == SC - 1:
                                act.sem_inc(w_free["v"], 1)

                        def keys1(b, h):
                            unit = HPG + b * (HPG + SC) + h
                            move(k_hi[:, h, 0:S], pj[unit % PJ][:, 0:S], pj_ready, gpj + unit + 1,
                                 bias=cur[:, 4 + h:5 + h], mid=pj_mid)
                            if b == HB - 1 and h == HPG - 1:
                                act.sem_inc(w_free["k"], 1)

                        def exps1(b, h):
                            n = b * HPG + h
                            act.wait_ge(max_ready, gsc + n + 1 + SCR)
                            nc.scalar.activation(probs[0:L, h, 0:SK], scores[n % SCR][0:L, 0:SK], ACT.Exp,
                                                 bias=neg_max[0:L, h:h + 1],
                                                 accum_out=row_sum[0:L, 0, h:h + 1]).then_inc(exp_ready, 1)

                        def split_p(b, h):
                            n = b * HPG + h
                            move(pt_hi[0:KC + 1, h, :], tp[n % TP][0:KC + 1, 0:SC * L], tp_ready,
                                 gtp + n + 1, mid=tp_mid)

                        def out1(b):
                            act.wait_ge(o_ready, go + b + 1)
                            for h in range(HPG):
                                i = nc.scalar.activation(qo_hi[:, HPG + h, b * L:(b + 1) * L],
                                                         o_ps[:, h * L:(h + 1) * L], ACT.Identity,
                                                         bias=cur[:, 12 + h:13 + h])
                            i.then_inc(o_mid, 1)

                        act.wait_ge(cur_ready, hf * CUR_H + ag + CUR_A + 1)
                        act.wait_ge(o_ready, go)
                        act.dma_start(v1[0][KC:KC + 1, SC - 1, :].bitcast(F32), bv_hi_dram[bass.ds(ag, 1), :]).then_inc(bvrow_in, 16)
                        act.dma_start(v1[1][KC:KC + 1, SC - 1, :].bitcast(F32), bv_lo_dram[bass.ds(ag, 1), :]).then_inc(bvrow_in, 16)
                        for h in range(HPG):
                            if h == 2:
                                act.wait_ge(bias_added, hf * 16 + a * HB + 2 * HB)
                            if h == 3:
                                act.wait_ge(pj_free, gpj + 1 + PJ)
                            act.wait_ge(pj_ready, gpj + h + 1)
                            nc.scalar.activation(tmp[h % 3][:, 0:T], pj[h % PJ][:, 0:T], ACT.Identity,
                                                 bias=cur[:, h:h + 1], scale=SCALE1).then_inc(pj_mid, 1)
                        act.sem_inc(w_free["q"], 1)
                        for b in range(HB):
                            if b > 0:
                                split_p(b - 1, 0)
                                split_p(b - 1, 1)
                            keys1(b, 0)
                            if b > 0:
                                split_p(b - 1, 2)
                                split_p(b - 1, 3)
                            for h in range(1, HPG):
                                keys1(b, h)
                            if b > 0:
                                out1(b - 1)
                            values1(b, 0)
                            exps1(b, 0)
                            exps1(b, 1)
                            values1(b, 1)
                            exps1(b, 2)
                            exps1(b, 3)
                            values1(b, 2)
                        for h in range(HPG):
                            split_p(HB - 1, h)
                        out1(HB - 1)

                act.dma_start(tmp[2][0:L, :], rows_in[0:1, 5 * D:6 * D].partition_broadcast(L)).then_inc(rows_ready, 16)
                ln_std(hf * 4 + 3, 1)
                ln_stage(hf * NL + ATT)
                with act.Fori(0, MLPG) as m:
                    mpj = pjb + m * PJ_MU + (PJ_M + 6)
                    act.wait_ge(cur_ready, hf * CUR_H + m + (CUR_A + ATT * G1) + 1)
                    for h in range(HPG):
                        act.wait_ge(pj_free, mpj + h + 1)
                        if h == 2:
                            act.wait_ge(bias_added, hf * 16 + 16)
                        act.wait_ge(pj_ready, mpj + h + 1)
                        nc.scalar.activation(tmp[h % 3][:, 0:T], pj[h % PJ][:, 0:T], ACT.Gelu,
                                             bias=cur[:, h:h + 1]).then_inc(pj_mid, 1)
                    act.sem_inc(w_free["q"], 1)
                split_ctx(hf + 1)
                act.wait_ge(pj_free, pjb + PJ_H + PJ)
                act.dma_start(out[bass.ds(hf * T, T), :].rearrange("(b p) n -> p b n", p=L), xa[0:L, :, :]).then_inc(out_done, 16)

        @block.vector
        def _(dve):
            def lo_of(dst, src, hi, mid, n, signal, k=1, bias=None):
                dve.wait_ge(mid, n)
                if bias is None:
                    i = nc.vector.tensor_tensor(dst, src, hi.bitcast(F32), ALU.subtract)
                else:
                    i = nc.vector.scalar_tensor_tensor(dst, src, bias, hi.bitcast(F32), ALU.add, ALU.subtract)
                i.then_inc(signal, k)

            def ln_stat(b):
                nc.vector.bn_stats(stats[0:L, b, :], xa[0:L, b, :]).then_inc(stats_ready, 1)

            def ln_scales(nn, st):
                for b in range(HB):
                    dve.wait_ge(stats_ready, st + b + 1)
                    dve.sem_inc(dve_passed, 1)
                    nc.vector.bn_aggr(mean_var[0:L, b, :], stats[0:L, b, :]).then_inc(ln_chain, 1)
                dve.wait_ge(std_ready, nn + 1)
                nc.vector.reciprocal(rstd[0:L, :], std[0:L, :]).then_inc(ln_chain, 1)
                dve.wait_ge(ln_chain, nn * 5 + 5)

            def ln_stage(base, unit, nn, nl, st, mid0, par):
                nc.vector.tensor_copy(ln_cur[:], par).then_inc(ln_par, 1)
                ln_scales(nn, st)
                dve.wait_ge(ln_par, nl + 1)

                def normed(b):
                    nc.vector.tensor_scalar(tmp[0][0:L, :], xa[0:L, b, :], mean_var[0:L, b, 0:1],
                                            rstd[0:L, b:b + 1], ALU.subtract, ALU.mult).then_inc(xn_ready, 1)

                normed(0)
                for b in range(HB):
                    bank = pj[(unit + b) % PJ]
                    dve.wait_ge(pj_ready, base + unit + b + 1)
                    dve.wait_ge(pj_free, base + unit + b + PJ)
                    for c in range(DC):
                        nc.vector.tensor_scalar(tmp[1][:, c * L:(c + 1) * L], bank[:, c * L:(c + 1) * L],
                                                ln_cur[:, c:c + 1], ln_cur[:, 4 + c:5 + c],
                                                ALU.mult, ALU.add).then_inc(ln_t, 1)
                    if b + 1 < HB:
                        normed(b + 1)
                    lo_of(h_lo[:, :, b * L:(b + 1) * L], tmp[1][:, 0:T].rearrange("p (c l) -> p c l", c=DC),
                          h_hi[:, :, b * L:(b + 1) * L], pj_mid, mid0 + b + 1, pj_free,
                          3 if b == HB - 1 else 1)
                dve.wait_ge(xn_ready, nl * HB + HB)
                dve.wait_ge(rows_ready, nn * 16 + 16)
                for b in range(HB):
                    nc.vector.tensor_tensor(xa[0:L, b, :], xa[0:L, b, :], tmp[2][0:L, :], ALU.add).then_inc(bias_added, 1)

            def out_part(base, unit, b, pad=1, stat=True):
                dve.wait_ge(pj_ready, base + unit + b + 1)
                if b == HB - 1:
                    dve.sem_inc(w_free["o"], 1)
                k = pad if b == HB - 1 else 1
                nc.vector.tensor_tensor(xa[0:L, b, :], pj[(unit + b) % PJ][0:L, :], xa[0:L, b, :],
                                        ALU.add).then_inc(pj_free, k)
                if stat:
                    dve.wait_ge(pj_free, base + unit + b + k + PJ)
                    dve.sem_inc(dve_passed, 1)
                    ln_stat(b)

            def q_stage(base, mid0, done0):
                for h in range(HPG):
                    dve.wait_ge(pj_mid, mid0 + h + 1)
                    nc.vector.tensor_copy(qo_hi[:, h, :], tmp[h % 3][:, 0:T]).then_inc(qh_done, 1)
                    lo_of(qo_lo[:, h, :], tmp[h % 3][:, 0:T], qo_hi[:, h, :], qh_done, done0 + h + 1, pj_free)

            dve.wait_ge(setup_pool, 2)
            dve.sem_inc(pj_free, PJ)
            dve.sem_inc(max_ready, SCR)
            dve.sem_inc(exp_ready, SCR)
            dve.sem_inc(tp_free, TP)
            dve.sem_inc(o_free, 1)
            dve.wait_ge(setup_dma, 48)
            q1 = prm[:, 0:PRM_LN].rearrange("p (j e) -> p j e", e=16)[:, :, 0:HPG]
            nc.vector.tensor_scalar(q1, q1, SCALE1, None, ALU.mult).then_inc(setup_dve, 1)
            rows8 = xa[0:ATT * G1, :, :]
            nc.vector.tensor_tensor(rows8[:, 2, :], rows8[:, 0, :], rows8[:, 1, :], ALU.subtract).then_inc(setup_bv, 1)
            dve.wait_ge(setup_bv, 1)
            row_hi = pt_hi[:].rearrange("p h n -> p (h n)")[0:8, 0:GW]
            row_lo = pt_lo[:].rearrange("p h n -> p (h n)")[0:8, 0:GW]
            nc.vector.tensor_copy(row_hi, rows8[:, 2, :]).then_inc(setup_bv, 1)
            dve.wait_ge(setup_bv, 2)
            nc.vector.tensor_tensor(row_lo, rows8[:, 2, :], row_hi.bitcast(F32), ALU.subtract).then_inc(setup_bv, 1)
            dve.wait_ge(setup_dve, 1)

            def split_ctx(half):
                for b in range(HB):
                    lo_of(ctx_lo[:, :, b, 0:S], ctx_lo[:, :, b, 0:S].bitcast(F32), ctx_hi[:, :, b, 0:S],
                          ctx_hi_ready, half * HB + b + 1, ctx_ready)

            split_ctx(0)
            with dve.Fori(0, HALVES) as hf:
                pjb = hf * PJ_H
                midb = hf * MID_H
                dve.wait_ge(pj_free, pjb + PJ)
                nc.vector.memset(place_sel.bitcast(F32), 0.0).then_inc(sel_zero, 1)
                dve.wait_ge(sel_zero, hf + 1)
                for kv in range(KV2):
                    heads = ident[:, kv * 64:kv * 64 + 64].rearrange("p (j d) -> p j d", d=HD0)
                    for e in range(2):
                        for r in range(2):
                            at = 32 * kv + 64 * r + 16 * e
                            nc.vector.tensor_scalar(place_sel[:, e, 4 * kv:4 * kv + 4, at:at + HD0], heads,
                                                    SCALE0, None, ALU.mult).then_inc(sel_ready, 1)
                nc.vector.tensor_copy(cur[:, 1:3], prm[:, PRM_C:PRM_C + 2]).then_inc(cur_ready, 1)

                def values_t_out(b):
                    dve.wait_ge(pj_mid, midb + 2 * b + 1)
                    dve.wait_ge(pj_free, pjb + VT_UNIT[b] + PJ)
                    dve.sem_inc(pj_free, 1)

                values_t_out(0)
                for b in range(HB):
                    if b + 1 < HB:
                        values_t_out(b + 1)
                    lo_of(v0[1][0:KC, b * SC:(b + 1) * SC, :],
                          pj[V_UNIT[b] % PJ][0:KC, 0:SC * P].rearrange("p (s n) -> p s n", s=SC),
                          v0[0][0:KC, b * SC:(b + 1) * SC, :], pj_mid, midb + 2 * b + 2, pj_free,
                          2 if b == HB - 1 else 1)

                def queries0(base, unit, mid):
                    lo_of(q0_split[1], pj[unit % PJ][:, 0:T], q0_split[0], pj_mid, mid + 1, pj_free,
                          bias=cur[:, 1:2])

                def keys0(base, unit, mid, b):
                    dve.wait_ge(pj_mid, mid + 1)
                    nc.vector.scalar_tensor_tensor(
                        k0[b % 2][64:P, :], pj[unit % PJ][64:P, 0:SK], cur[64:P, 2:3],
                        k0[b % 2][64:P, :].bitcast(F32), ALU.add, ALU.subtract).then_inc(pj_free, 1)

                def placed(base, unit, mid, j):
                    if j % 2 == 1:
                        dve.wait_ge(pj_mid, mid + j // 2 + 1)
                        dve.wait_ge(pj_free, base + unit + PJ)
                        dve.sem_inc(pj_free, 3 if j == HPC - 1 else 1)
                    else:
                        dve.wait_ge(pj_ready, base + unit + 1)
                        nc.vector.tensor_copy(qo_hi[:, j, :], pj[unit % PJ][:, 0:T]).then_inc(pj_free, 1)

                def max0(csc, n):
                    b, j = n // HPC % HB, n % HPC
                    dve.wait_ge(sc_ready, csc + n + 1)
                    dve.sem_inc(dve_passed, 1)
                    nc.vector.tensor_tensor_reduce(
                        probs[0:L, n % 4, 0:S], scores[n % SCR][0:L, 0:S], mask_v[:, b, :], -1.0, 3.0e38,
                        ALU.add, ALU.min, neg_max[0:L, j:j + 1]).then_inc(max_ready, 1)

                ppj, pmid = pjb + PJ_P, midb + MID_P
                dve.wait_ge(cur_ready, hf * CUR_H + 1)
                queries0(ppj, PR_Q, pmid)
                keys0(ppj, PR_KEYS, pmid + 1, 0)
                for j in range(4):
                    placed(ppj, PR_PLACED + j, pmid + 2, j)
                dve.wait_ge(mask_in, hf * 16 + 16)
                for n in range(4):
                    max0(hf * SC_H, n)
                    placed(ppj, PR_PLACED + 4 + n, pmid + 2, 4 + n)
                with dve.Fori(0, C0) as c8:
                    cpj = pjb + c8 * PJ_CU + PJ_C
                    cmid = midb + c8 * MID_CU + MID_C
                    csc = hf * SC_H + c8 * SC_CU
                    ctp = hf * TP_H + c8 * TP_CU
                    ctm = hf * TM_H + c8 * TM_CU
                    ob = hf * (C0 * HB) + c8 * HB

                    def sum_outputs(u):
                        unit = tp_unit("four", u)
                        dve.wait_ge(tp_ready, ctp + unit + 1)
                        nc.vector.tensor_reduce(
                            o_nat[0:L, 4 * (u % 2):4 * (u % 2) + 4, :],
                            tp[unit % TP][0:L, 0:P].rearrange("p (h e d) -> p h d e", e=2, d=HD0),
                            AX_X, ALU.add).then_inc(tp_free, 1)

                    def inverse_sums(b):
                        dve.wait_ge(exp_ready, csc + HPC * (b + 1) + SCR)
                        nc.vector.reciprocal(inv_sum[0:L, :], row_sum[0:L, b % 2, :]).then_inc(o_inv, 1)

                    def scale_outputs(b):
                        dve.wait_ge(o_inv, ob + b + 1)
                        dve.wait_ge(tp_free, ctp + tp_unit("four", 2 * b + 1) + 1 + TP)
                        nc.vector.tensor_tensor(o_nat[0:L], o_nat[0:L],
                                                inv_sum[0:L, :].unsqueeze(2).broadcast_to([L, HPC, HD0]),
                                                ALU.mult).then_inc(o_nat_ready, 1)

                    def out0(b):
                        n = tp_unit("batch", b)
                        dst = [o[:, bass.ds(c8, 1), b * L:(b + 1) * L].rearrange("p c l -> p (c l)") for o in ot0]
                        lo_of(dst[1], tp[n % TP][:, 0:L], dst[0], tp_mid,
                              ctm + tp_mid_unit("batch", b) + 1, tp_free,
                              bias=cur[:, 0:1])

                    def chunk_operands():
                        dve.wait_ge(tp_free, ctp + TP)
                        dve.wait_ge(pj_free, cpj + PJ)
                        nc.vector.tensor_copy(cur[:, 0:2], prm[:, bass.ds(c8 * 3 + (PRM_C + 2), 2)]).then_inc(cur_ready, 1)
                        for e, v in enumerate(v0):
                            nc.vector.tensor_copy(
                                v0c[0:KC, :, :, e * HD0:(e + 1) * HD0],
                                v[0:KC, :, bass.ds(c8 * (KV2 * HD0), KV2 * HD0)].bitcast(F32).rearrange(
                                    "p n (k d) -> p n k d", d=HD0)).then_inc(v0c_ready, 1)

                    for n in range(SC_CU):
                        b, j, unit = n // HPC, n % HPC, tp_unit("probs", n)
                        if b > 0 and j == 0:
                            inverse_sums(b - 1)
                        max0(csc, n + 4)
                        lo_of(pt0[n // 4 % 2][1][0:KC, n % 4, :], tp[unit % TP][0:KC, 0:SC * L],
                              pt0[n // 4 % 2][0][0:KC, n % 4, :], tp_mid,
                              ctm + tp_mid_unit("probs", n) + 1, tp_free)
                        if n == 0:
                            chunk_operands()
                        if j == 1:
                            if b == HB - 1:
                                dve.wait_ge(cur_ready, hf * CUR_H + 2 * c8 + 3)
                            keys0(cpj, CH_KEYS[b + 1], cmid + CH_KEYS[b + 1], b + 1)
                        if n == 15:
                            dve.wait_ge(cur_ready, hf * CUR_H + 2 * c8 + 2)
                            queries0(cpj, CH_Q, cmid + CH_Q)
                        if n == 18:
                            dve.wait_ge(pj_free, cpj + CH_KEYS[HB - 1] + 1 + PJ)
                            nc.vector.tensor_copy(cur[:, 2:3], prm[:, bass.ds(c8 * 3 + (PRM_C + 4), 1)]).then_inc(cur_ready, 1)
                        if n >= 9 and n % 4 == 1:
                            sum_outputs((n - 9) // 4)
                            if n % HPC == 5:
                                scale_outputs((n - 13) // HPC)
                        if n >= 26:
                            placed(cpj, CH_PLACED + n - 26, cmid + CH_PLACED, n - 26)
                        if n >= 14 and j == 6:
                            out0((n - 14) // HPC)
                    inverse_sums(HB - 1)
                    placed(cpj, CH_PLACED + 6, cmid + CH_PLACED, 6)
                    sum_outputs(2 * HB - 2)
                    placed(cpj, CH_PLACED + 7, cmid + CH_PLACED, 7)
                    sum_outputs(2 * HB - 1)
                    scale_outputs(HB - 1)
                    out0(HB - 1)

                dve.wait_ge(x_in, hf * 16 + 16)
                dve.wait_ge(rows_ready, hf * 64 + 16)
                for b in range(HB):
                    nc.vector.tensor_tensor(xa[0:L, b, :], xa[0:L, b, :], tmp[0][0:L, :], ALU.add).then_inc(bias_added, 1)
                dve.wait_ge(bias_added, hf * 16 + 4)
                for b in range(HB):
                    out_part(pjb + PJ_W0, 0, b, pad=3)
                dve.sem_inc(w_free["v"], 1)
                ln_scales(hf * 4, hf * ST_H)
                for b in range(HB):
                    nc.vector.scalar_tensor_tensor(xa[0:L, b, :], xa[0:L, b, :], mean_var[0:L, b, 0:1],
                                                   tmp[1][0:L, :], ALU.subtract, ALU.mult).then_inc(post_ln, 1)
                for b in range(HB):
                    dve.wait_ge(post_ln, hf * 2 * HB + b + 1)
                    nc.vector.scalar_tensor_tensor(xa[0:L, b, :], xa[0:L, b, :], rstd[0:L, b:b + 1],
                                                   tmp[2][0:L, :], ALU.mult, ALU.add).then_inc(post_ln, 1)
                for b in range(HB):
                    dve.wait_ge(post_ln, hf * 2 * HB + HB + b + 1)
                    dve.sem_inc(dve_passed, 1)
                    ln_stat(b)

                with dve.Fori(0, ATT) as a:
                    apj = pjb + a * PJ_AU + PJ_A
                    amid = midb + a * MID_AU + MID_A
                    ln_stage(apj, 0, hf * 4 + a + 1, hf * NL + a, hf * ST_H + a * (G1 * HB) + HB, amid,
                             prm[:, bass.ds(a * 8 + PRM_LN, 8)])
                    with dve.Fori(0, G1) as g:
                        ag = a * G1 + g
                        gpj = apj + g * PJ_GU + 6
                        gmid = amid + g * MID_GU + HB
                        gsc = hf * SC_H + ag * SC_GU + SC_A
                        gtm = hf * TM_H + ag * SC_GU + TM_A
                        gof = (hf * ATT * G1 + ag) * HB
                        gg = (hf * ATT * G1 + ag) * SC_GU

                        def keys1(b, h):
                            unit = HPG + b * (HPG + SC) + h
                            lo_of(k_lo[:, h, 0:S], pj[unit % PJ][:, 0:S], k_hi[:, h, 0:S], pj_mid,
                                  gmid + unit + 1, pj_free, bias=cur[:, 4 + h:5 + h])

                        def values1(b, s):
                            unit = HPG + b * (HPG + SC) + HPG + s
                            lo_of(v1[1][0:KC, s, :], pj[unit % PJ][0:KC, :], v1[0][0:KC, s, :], pj_mid,
                                  gmid + unit + 1, pj_free)

                        def max1(b, h):
                            n = b * HPG + h
                            dve.wait_ge(sc_ready, gsc + n + 1)
                            nc.vector.tensor_reduce(neg_max[0:L, h:h + 1], scores[n % SCR][0:L, 0:SK], AX_X,
                                                    ALU.max, negate=True).then_inc(max_ready, 1)

                        def norm1(b, h):
                            n = b * HPG + h
                            dve.wait_ge(exp_ready, gsc + n + 1 + SCR)
                            nc.vector.reciprocal(inv_sum[0:L, h:h + 1], row_sum[0:L, 0, h:h + 1]).then_inc(inv_ready, 1)
                            dve.wait_ge(inv_ready, gg + n + 1)
                            nc.vector.tensor_scalar(probs[0:L, h, 0:SK], probs[0:L, h, 0:SK],
                                                    inv_sum[0:L, h:h + 1], None, ALU.mult).then_inc(norm_ready, 1)

                        def split_p(b, h):
                            n = b * HPG + h
                            lo_of(pt_lo[0:KC + 1, h, :], tp[n % TP][0:KC + 1, 0:SC * L],
                                  pt_hi[0:KC + 1, h, :], tp_mid, gtm + n + 1, tp_free)

                        def out1(b):
                            dve.wait_ge(o_mid, hf * O_H + ag * HB + (O_A + b + 1))
                            for h in range(HPG):
                                cols = slice(b * L, (b + 1) * L)
                                i = nc.vector.scalar_tensor_tensor(
                                    qo_lo[:, HPG + h, cols], o_ps[:, h * L:(h + 1) * L], cur[:, 12 + h:13 + h],
                                    qo_hi[:, HPG + h, cols].bitcast(F32), ALU.add, ALU.subtract)
                            i.then_inc(o_free, 1)

                        dve.wait_ge(pj_ready, gpj + 1)
                        dve.wait_ge(o_free, gof + 1)
                        nc.vector.tensor_copy(cur[:], prm[:, bass.ds(ag * 16, 16)]).then_inc(cur_ready, 1)
                        dve.wait_ge(cur_ready, hf * CUR_H + ag + CUR_A + 1)
                        kb = cur[:, 8:12].unsqueeze(2)
                        nc.vector.tensor_copy(k_hi[:, :, S:SK], kb).then_inc(kbias_hi, 1)
                        dve.wait_ge(kbias_hi, hf * ATT * G1 + ag + 1)
                        nc.vector.tensor_tensor(k_lo[:, :, S:SK], kb, k_hi[:, :, S:SK].bitcast(F32), ALU.subtract)
                        q_stage(gpj, gmid, (hf * (ATT * G1 + MLPG) + ag) * HPG)
                        for b in range(HB):
                            if b > 0:
                                split_p(b - 1, 0)
                                split_p(b - 1, 1)
                            keys1(b, 0)
                            if b > 0:
                                split_p(b - 1, 2)
                                split_p(b - 1, 3)
                            for h in range(1, HPG):
                                keys1(b, h)
                            if b > 0:
                                out1(b - 1)
                            values1(b, 0)
                            max1(b, 0)
                            max1(b, 1)
                            norm1(b, 0)
                            norm1(b, 1)
                            values1(b, 1)
                            max1(b, 2)
                            max1(b, 3)
                            norm1(b, 2)
                            norm1(b, 3)
                            values1(b, 2)
                        split_p(HB - 1, 0)
                        split_p(HB - 1, 1)
                        out_part(gpj, PJ_GU - HB, 0)
                        split_p(HB - 1, 2)
                        split_p(HB - 1, 3)
                        out_part(gpj, PJ_GU - HB, 1)
                        out1(HB - 1)
                        out_part(gpj, PJ_GU - HB, 2)
                        out_part(gpj, PJ_GU - HB, 3)

                mlp = pjb + PJ_M
                ln_stage(mlp, 0, hf * 4 + 3, hf * NL + ATT, hf * ST_H + ST_H - HB, midb + MID_M, prm[:, PRM_LN + 16:PRM_LN + 24])
                with dve.Fori(0, MLPG) as m:
                    mpj = pjb + m * PJ_MU + (PJ_M + 6)
                    dve.wait_ge(pj_ready, mpj + 1)
                    dve.wait_ge(o_free, (hf + 1) * (ATT * G1 * HB) + 1)
                    nc.vector.tensor_copy(cur[:, 0:HPG], prm[:, bass.ds(m * HPG + PRM_B1, HPG)]).then_inc(cur_ready, 1)
                    q_stage(mpj, midb + m * HPG + (MID_M + HB), (hf * (ATT * G1 + MLPG) + m + ATT * G1) * HPG)
                    for b in range(HB):
                        out_part(mpj, HPG, b, pad=2, stat=False)
                split_ctx(hf + 1)


def kernel(**inputs):
    import numpy as np
    import concourse.bacc as bacc
    from concourse.bass_utils import run_bass_kernel_spmd

    i = {k: np.asarray(v) for k, v in inputs.items()}
    L0, L1 = "L0_xattn_", "L1_xattn_"
    tokens = i["x"].reshape(B * L, D)

    def columns(v, n):
        return v.reshape(n, P).T

    def both(name):
        return np.stack([i[f"{L1}{name}1"], i[f"{L1}{name}2"]])

    def rep_kv(a):
        s = a.shape[:-1]
        return np.repeat(a.reshape(*s, 8, 1, HD0), 4, axis=-2).reshape(*s, D)

    def and_first(w):
        return np.concatenate([w, w[:, 0:P]], axis=1)

    def rep_keys(a):
        s = a.shape[:-1]
        twice = np.repeat(a.reshape(*s, C0, 1, KV2, 1, HD0), 2, axis=-2)
        return np.repeat(twice, 2, axis=-4).reshape(*s, D)

    heads = [both(n).reshape(ATT * G1, HPG, P) for n in ("bq", "bk", "bias_k", "bv")]
    per_group = np.stack(heads, axis=1).reshape(ATT * G1 * 16, P).T
    norms = [columns(i[L1 + n], DC) for n in
             ("ln1_scale", "ln1_offset", "ln2_scale", "ln2_offset", "ln_mlp_scale", "ln_mlp_offset")]
    bq0, bk0, bv0 = (a.reshape(C0, P) for a in (i[L0 + "bq"], rep_keys(i[L0 + "bk"]), rep_kv(i[L0 + "bv"])))
    next_chunk = [(c + 1) % C0 for c in range(C0)]
    first_two = np.stack([bq0[0], bk0[0]], axis=1)
    per_chunk = np.stack([bv0, bq0[next_chunk], bk0[next_chunk]], axis=1).reshape(C0 * 3, P).T
    prm = np.concatenate([per_group, *norms, columns(i[L1 + "b_fc1"], 16), first_two, per_chunk], axis=1)
    rows = np.concatenate([i[L0 + "bo"], i[L0 + "gamma"], i[L0 + "beta"], i[L1 + "bo1"], i[L1 + "bo2"],
                           i[L1 + "b_fc2"]]).reshape(1, 6 * D)
    arrays = {
        "x": tokens, "x_t": tokens.T, "ctx_t": i["ctx_2048"].transpose(2, 0, 1),
        "mask": i["mask_Bx1xSxS2_ff0"].reshape(B, L, S),
        "wq0": and_first(i[L0 + "Wq"]), "wk0": and_first(rep_keys(i[L0 + "Wk"])), "wv0": i[L0 + "Wv"], "wo0": i[L0 + "Wo"],
        "wq": both("wq").reshape(ATT * D, NH1 * HD1), "wk": both("wk").reshape(ATT * D, NH1 * HD1),
        "wv": both("wv").reshape(ATT * D, NH1 * HD1), "wo": both("wo").reshape(ATT * NH1 * HD1, D),
        "w1": i[L1 + "w_fc1"], "w2": i[L1 + "w_fc2"],
        "bias_v": both("bias_v").reshape(ATT * G1, GW), "bv": both("bv").reshape(ATT * G1, GW),
        "prm": prm, "rows": rows,
    }
    nc = bacc.Bacc("TRN2", target_bir_lowering=False, num_devices=1)
    sent, args = {}, []
    for name, a in arrays.items():
        sent[f"in_{name}"] = np.ascontiguousarray(a)
        args.append(nc.dram_tensor(f"in_{name}", a.shape, mybir.dt.float32, kind="ExternalInput").ap())
    args.append(nc.dram_tensor("out", (B * L, D), mybir.dt.float32, kind="ExternalOutput").ap())
    xattn_program(nc, *args)
    r = run_bass_kernel_spmd(nc, [sent], core_ids=[0])
    return r.results[0]["out"].reshape(B, L, D)
```
